# Optimizing a Trainium2 kernel written in Bass

```python
import numpy as np
import jax
import jax.numpy as jnp

def _softmax(x, axis=-1):
    return jax.nn.softmax(x, axis=axis)

def _gelu(x):
    return jax.nn.gelu(x, approximate=True)

def _silu(x):
    return jax.nn.silu(x)

def _sigmoid(x):
    return jax.nn.sigmoid(x)

def _layernorm(x, axis=-1, eps=1e-05):
    m = jnp.mean(x, axis=axis, keepdims=True)
    v = jnp.var(x, axis=axis, keepdims=True)
    return (x - m) / jnp.sqrt(v + eps)

def _scatter_add(tgt, idx, src, axis=0):
    return tgt.at[idx].add(src)

def _segment_sum(src, seg, n):
    return jax.ops.segment_sum(src, seg, n)
kernel_name = 'mk_sandwich_d1_jaxref_r8_811da1'

def setup_inputs(seed: int=0):
    np.random.seed(seed)
    _w = jnp.asarray

    def _L0_attn_setup():
        import math
        import jax, jax.numpy as jnp
        import numpy as np
        N_HEAD = 16
        N_CLUSTER = 64
        GROUP_SIZE = 32

        def _sinusoidal(n, d):
            pos = jnp.arange(n, dtype=jnp.float32)[:, None]
            div = jnp.exp(jnp.arange(0, d, 2, dtype=jnp.float32) * (-math.log(10000.0) / d))
            ang = pos * div
            return jnp.stack([jnp.sin(ang), jnp.cos(ang)], axis=-1).reshape(n, d)

        def _rotary(pe, x):
            d = x.shape[-1]
            sin, cos = (pe[..., :d // 2], pe[..., d // 2:])
            x_even, x_odd = (x[..., ::2], x[..., 1::2])
            out = jnp.stack([-x_odd * cos, x_even * sin], axis=-1)
            return out.reshape(jnp.broadcast_shapes(x.shape[:-1] + (d // 2,), out.shape[:-1]) + (2,)).reshape(x.shape) if False else jnp.broadcast_to(out, x.shape[:-1] + (d // 2, 2)).reshape(x.shape)

        def _forward(x, w_attn, b_attn, w_proj, b_proj, w_assign):
            B, T, C = x.shape
            H, nc, gs = (N_HEAD, N_CLUSTER, GROUP_SIZE)
            hd = C // H
            ntpc = T // nc
            G = T // gs
            ncpg = gs // ntpc
            c_max = (G - 1) * ncpg
            qkv = x @ w_attn.T + b_attn
            q, k, v = jnp.split(qkv, 3, axis=-1)
            x_r = x.reshape(B, nc, ntpc, C)
            logits = jnp.einsum('bctd,cd->bct', x_r, w_assign)
            w = jax.nn.softmax(logits, axis=-1)
            ck = jnp.einsum('bct,bctd->bcd', w, k.reshape(B, nc, ntpc, C))
            cv = jnp.einsum('bct,bctd->bcd', w, v.reshape(B, nc, ntpc, C))
            qg = q.reshape(B, G, gs, H, hd).transpose(0, 1, 3, 2, 4)
            kl = k.reshape(B, G, gs, H, hd).transpose(0, 1, 3, 2, 4)
            vl = v.reshape(B, G, gs, H, hd).transpose(0, 1, 3, 2, 4)
            kc = ck[:, :c_max].reshape(B, c_max, H, hd)
            vc = cv[:, :c_max].reshape(B, c_max, H, hd)
            S = _sinusoidal(c_max + gs, hd)
            qr = _rotary(S[:gs], qg)
            kcr = _rotary(S[:c_max, None, :], kc)
            pos_local = jnp.arange(G)[:, None] * ncpg + jnp.arange(gs)[None, :]
            klr = _rotary(S[pos_local][None, :, None], kl)
            scale = 1.0 / math.sqrt(hd)
            sc = jnp.einsum('bghqd,bchd->bghqc', qr, kcr) * scale
            sl = jnp.einsum('bghqd,bghkd->bghqk', qr, klr) * scale
            cmask = jnp.arange(c_max)[None, :] < (jnp.arange(G) * ncpg)[:, None]
            sc = jnp.where(cmask[None, :, None, None, :], sc, -jnp.inf)
            lmask = jnp.tril(jnp.ones((gs, gs), dtype=bool))
            sl = jnp.where(lmask, sl, -jnp.inf)
            p = jax.nn.softmax(jnp.concatenate([sc, sl], axis=-1), axis=-1)
            pc, pl = (p[..., :c_max], p[..., c_max:])
            y = jnp.einsum('bghqc,bchd->bghqd', pc, vc) + jnp.einsum('bghqk,bghkd->bghqd', pl, vl)
            y = y.transpose(0, 1, 3, 2, 4).reshape(B, T, C)
            return y @ w_proj.T + b_proj
        key = jax.random.key(seed)
        ks = jax.random.split(key, 4)
        B, T, C, NC = (4, 512, 128, N_CLUSTER)
        x = jax.random.normal(ks[0], (B, T, C), jnp.float32)
        w_attn = jax.random.normal(ks[1], (3 * C, C), jnp.float32) * 0.02
        b_attn = jnp.zeros((3 * C,), jnp.float32)
        w_proj = jax.random.normal(ks[2], (C, C), jnp.float32) * 0.02
        b_proj = jnp.zeros((C,), jnp.float32)
        w_assign = jax.random.normal(ks[3], (NC, C), jnp.float32) * 0.02
        return {'x': x, 'w_attn': w_attn, 'b_attn': b_attn, 'w_proj': w_proj, 'b_proj': b_proj, 'w_assign': w_assign}
    _L0_attn_in = _L0_attn_setup()

    def _L0_ffn_setup():
        import jax, jax.numpy as jnp
        import numpy as np
        D = 128
        H = 16
        DK = D // H
        E = 8
        DFF = 4 * D
        TOPK = 2
        EPS = 1e-05

        def _layernorm(x, g, b):
            m = jnp.mean(x, axis=-1, keepdims=True)
            v = jnp.mean(jnp.square(x - m), axis=-1, keepdims=True)
            return (x - m) * jax.lax.rsqrt(v + EPS) * g + b
        key = jax.random.key(seed)
        ks = jax.random.split(key, 16)
        s_in = 1.0 / np.sqrt(D)
        s_ff = 1.0 / np.sqrt(DFF)
        return {'x': jax.random.normal(ks[0], (2, 256, D), dtype=jnp.float32), 'ln1_g': jnp.ones((D,), jnp.float32), 'ln1_b': jnp.zeros((D,), jnp.float32), 'w_qkv': jax.random.normal(ks[1], (D, 3 * D), jnp.float32) * s_in, 'b_qkv': jnp.zeros((3 * D,), jnp.float32), 'w_o': jax.random.normal(ks[2], (D, D), jnp.float32) * s_in, 'b_o': jnp.zeros((D,), jnp.float32), 'ln2_g': jnp.ones((D,), jnp.float32), 'ln2_b': jnp.zeros((D,), jnp.float32), 'gate_w': jax.random.normal(ks[3], (D, E), jnp.float32) * s_in, 'gate_b': jnp.zeros((E,), jnp.float32), 'W1': jax.random.normal(ks[4], (E, D, DFF), jnp.float32) * s_in, 'b1': jnp.zeros((E, DFF), jnp.float32), 'W2': jax.random.normal(ks[5], (E, DFF, D), jnp.float32) * s_ff, 'b2': jnp.zeros((E, D), jnp.float32)}
    _L0_ffn_in = _L0_ffn_setup()
    _d = {'L0_attn_x': _L0_attn_in['x'], 'L0_attn_w_attn': _L0_attn_in['w_attn'], 'L0_attn_b_attn': _L0_attn_in['b_attn'], 'L0_attn_w_proj': _L0_attn_in['w_proj'], 'L0_attn_b_proj': _L0_attn_in['b_proj'], 'L0_attn_w_assign': _L0_attn_in['w_assign'], 'L0_ffn_ln1_g': _L0_ffn_in['ln1_g'], 'L0_ffn_ln1_b': _L0_ffn_in['ln1_b'], 'L0_ffn_w_qkv': _L0_ffn_in['w_qkv'], 'L0_ffn_b_qkv': _L0_ffn_in['b_qkv'], 'L0_ffn_w_o': _L0_ffn_in['w_o'], 'L0_ffn_b_o': _L0_ffn_in['b_o'], 'L0_ffn_ln2_g': _L0_ffn_in['ln2_g'], 'L0_ffn_ln2_b': _L0_ffn_in['ln2_b'], 'L0_ffn_gate_w': _L0_ffn_in['gate_w'], 'L0_ffn_gate_b': _L0_ffn_in['gate_b'], 'L0_ffn_W1': _L0_ffn_in['W1'], 'L0_ffn_b1': _L0_ffn_in['b1'], 'L0_ffn_W2': _L0_ffn_in['W2'], 'L0_ffn_b2': _L0_ffn_in['b2']}
    _x0 = _d['L0_attn_x']
    _d['L0_attn_x'] = jax.random.normal(jax.random.fold_in(jax.random.key(seed), 1), (4, 1024, 128), dtype=_x0.dtype)
    del _x0
    return _d

def reference(L0_attn_x, L0_attn_w_attn, L0_attn_b_attn, L0_attn_w_proj, L0_attn_b_proj, L0_attn_w_assign, L0_ffn_ln1_g, L0_ffn_ln1_b, L0_ffn_w_qkv, L0_ffn_b_qkv, L0_ffn_w_o, L0_ffn_b_o, L0_ffn_ln2_g, L0_ffn_ln2_b, L0_ffn_gate_w, L0_ffn_gate_b, L0_ffn_W1, L0_ffn_b1, L0_ffn_W2, L0_ffn_b2):

    def _L0_attn_ref(x, w_attn, b_attn, w_proj, b_proj, w_assign):
        import math
        import jax, jax.numpy as jnp
        import numpy as np
        N_HEAD = 16
        N_CLUSTER = 64
        GROUP_SIZE = 32

        def _sinusoidal(n, d):
            pos = jnp.arange(n, dtype=jnp.float32)[:, None]
            div = jnp.exp(jnp.arange(0, d, 2, dtype=jnp.float32) * (-math.log(10000.0) / d))
            ang = pos * div
            return jnp.stack([jnp.sin(ang), jnp.cos(ang)], axis=-1).reshape(n, d)

        def _rotary(pe, x):
            d = x.shape[-1]
            sin, cos = (pe[..., :d // 2], pe[..., d // 2:])
            x_even, x_odd = (x[..., ::2], x[..., 1::2])
            out = jnp.stack([-x_odd * cos, x_even * sin], axis=-1)
            return out.reshape(jnp.broadcast_shapes(x.shape[:-1] + (d // 2,), out.shape[:-1]) + (2,)).reshape(x.shape) if False else jnp.broadcast_to(out, x.shape[:-1] + (d // 2, 2)).reshape(x.shape)

        def _forward(x, w_attn, b_attn, w_proj, b_proj, w_assign):
            B, T, C = x.shape
            H, nc, gs = (N_HEAD, N_CLUSTER, GROUP_SIZE)
            hd = C // H
            ntpc = T // nc
            G = T // gs
            ncpg = gs // ntpc
            c_max = (G - 1) * ncpg
            qkv = x @ w_attn.T + b_attn
            q, k, v = jnp.split(qkv, 3, axis=-1)
            x_r = x.reshape(B, nc, ntpc, C)
            logits = jnp.einsum('bctd,cd->bct', x_r, w_assign)
            w = jax.nn.softmax(logits, axis=-1)
            ck = jnp.einsum('bct,bctd->bcd', w, k.reshape(B, nc, ntpc, C))
            cv = jnp.einsum('bct,bctd->bcd', w, v.reshape(B, nc, ntpc, C))
            qg = q.reshape(B, G, gs, H, hd).transpose(0, 1, 3, 2, 4)
            kl = k.reshape(B, G, gs, H, hd).transpose(0, 1, 3, 2, 4)
            vl = v.reshape(B, G, gs, H, hd).transpose(0, 1, 3, 2, 4)
            kc = ck[:, :c_max].reshape(B, c_max, H, hd)
            vc = cv[:, :c_max].reshape(B, c_max, H, hd)
            S = _sinusoidal(c_max + gs, hd)
            qr = _rotary(S[:gs], qg)
            kcr = _rotary(S[:c_max, None, :], kc)
            pos_local = jnp.arange(G)[:, None] * ncpg + jnp.arange(gs)[None, :]
            klr = _rotary(S[pos_local][None, :, None], kl)
            scale = 1.0 / math.sqrt(hd)
            sc = jnp.einsum('bghqd,bchd->bghqc', qr, kcr) * scale
            sl = jnp.einsum('bghqd,bghkd->bghqk', qr, klr) * scale
            cmask = jnp.arange(c_max)[None, :] < (jnp.arange(G) * ncpg)[:, None]
            sc = jnp.where(cmask[None, :, None, None, :], sc, -jnp.inf)
            lmask = jnp.tril(jnp.ones((gs, gs), dtype=bool))
            sl = jnp.where(lmask, sl, -jnp.inf)
            p = jax.nn.softmax(jnp.concatenate([sc, sl], axis=-1), axis=-1)
            pc, pl = (p[..., :c_max], p[..., c_max:])
            y = jnp.einsum('bghqc,bchd->bghqd', pc, vc) + jnp.einsum('bghqk,bghkd->bghqd', pl, vl)
            y = y.transpose(0, 1, 3, 2, 4).reshape(B, T, C)
            return y @ w_proj.T + b_proj
        return _forward(x, w_attn, b_attn, w_proj, b_proj, w_assign)

    def _L0_ffn_ref(x, ln1_g, ln1_b, w_qkv, b_qkv, w_o, b_o, ln2_g, ln2_b, gate_w, gate_b, W1, b1, W2, b2):
        import jax, jax.numpy as jnp
        import numpy as np
        D = 128
        H = 16
        DK = D // H
        E = 8
        DFF = 4 * D
        TOPK = 2
        EPS = 1e-05

        def _layernorm(x, g, b):
            m = jnp.mean(x, axis=-1, keepdims=True)
            v = jnp.mean(jnp.square(x - m), axis=-1, keepdims=True)
            return (x - m) * jax.lax.rsqrt(v + EPS) * g + b
        B, S, _ = x.shape
        h = _layernorm(x, ln1_g, ln1_b)
        qkv = h @ w_qkv + b_qkv
        q, k, v = jnp.split(qkv, 3, axis=-1)
        q = q.reshape(B, S, H, DK)
        k = k.reshape(B, S, H, DK)
        v = v.reshape(B, S, H, DK)
        scores = jnp.einsum('bqhd,bkhd->bhqk', q, k) / np.sqrt(DK)
        attn = jax.nn.softmax(scores, axis=-1)
        o = jnp.einsum('bhqk,bkhd->bqhd', attn, v).reshape(B, S, D)
        x = x + o @ w_o + b_o
        h = _layernorm(x, ln2_g, ln2_b).reshape(B * S, D)
        logits = h @ gate_w + gate_b
        topv, topi = jax.lax.top_k(logits, TOPK)
        gw = jax.nn.softmax(topv, axis=-1)
        ew = jnp.sum(jax.nn.one_hot(topi, E, dtype=h.dtype) * gw[..., None], axis=1)
        hid = jax.nn.relu(jnp.einsum('td,edf->etf', h, W1) + b1[:, None, :])
        out_e = jnp.einsum('etf,efd->etd', hid, W2) + b2[:, None, :]
        moe = jnp.einsum('etd,te->td', out_e, ew)
        return x + moe.reshape(B, S, D)
    x = L0_attn_x
    x = x + _layernorm(_L0_attn_ref(_layernorm(x, axis=-1), L0_attn_w_attn, L0_attn_b_attn, L0_attn_w_proj, L0_attn_b_proj, L0_attn_w_assign), axis=-1)
    x = x + _layernorm(_L0_ffn_ref(_layernorm(x, axis=-1), L0_ffn_ln1_g, L0_ffn_ln1_b, L0_ffn_w_qkv, L0_ffn_b_qkv, L0_ffn_w_o, L0_ffn_b_o, L0_ffn_ln2_g, L0_ffn_ln2_b, L0_ffn_gate_w, L0_ffn_gate_b, L0_ffn_W1, L0_ffn_b1, L0_ffn_W2, L0_ffn_b2), axis=-1)
    return x

_drawn_inputs = setup_inputs


def setup_inputs(seed=0):
    import zlib

    import numpy as np

    out = dict(_drawn_inputs(seed))
    spreads = {'L0_attn_b_attn': (0.0, 0.1),
     'L0_attn_b_proj': (0.0, 0.1),
     'L0_ffn_ln1_g': (1.0, 0.2),
     'L0_ffn_ln1_b': (0.0, 0.1),
     'L0_ffn_b_qkv': (0.0, 0.1),
     'L0_ffn_b_o': (0.0, 0.1),
     'L0_ffn_ln2_g': (1.0, 0.2),
     'L0_ffn_ln2_b': (0.0, 0.1),
     'L0_ffn_gate_b': (0.0, 0.1),
     'L0_ffn_b1': (0.0, 0.484),
     'L0_ffn_b2': (0.0, 0.351)}
    factors = {'L0_attn_w_assign': 6.511}
    for name, (base, spread) in spreads.items():
        noise = np.random.default_rng([zlib.crc32(name.encode()), seed]).standard_normal(out[name].shape)
        drawn = base * np.exp(spread * noise) if base else spread * noise
        out[name] = jnp.asarray(drawn.astype(out[name].dtype))
    for name, factor in factors.items():
        out[name] = (out[name] * factor).astype(out[name].dtype)
    return out
```

```python
import concourse.bass as bass
from concourse import mybir
from contextlib import ExitStack

P = 128
B, T, C = 4, 1024, 128
H, D = 16, 8
HG, J = 4, 4
UNITS = B * HG
NT = T // P
HALF = T // 2
NCL, GS, NTPC = 64, 32, 16
NCPG = GS // NTPC
E, DFF = 8, 512
FC = DFF // P
TK = T + NCL
PARTS = 3
ROWS = PARTS * PARTS * D
KROWS = ROWS + PARTS
VW = D + 1
RING = 8
SLOTS = 3
LOOPS = 4
SCALE = float(D) ** -0.5
EPS = 1e-5

fp32 = mybir.dt.float32
bf16 = mybir.dt.bfloat16
ALU = mybir.AluOpType
ACT = mybir.ActivationFunctionType
AX = mybir.AxisListType


def settled(dve, v, sem, value):
    dve.wait_ge(sem, value)
    dve.memset(v.rstd[:, :], 0.0)


class Tally:

    def __init__(self):
        self.n = 0
        self.base = None

    def enter(self, i, per):
        self.base, self.per, self.start = self.n + i * per, per, self.n
        self.n = 0

    def leave(self, trips):
        assert self.n == self.per, (self.n, self.per)
        self.n = self.start + self.per * trips
        self.base = None

    def at(self, k=0):
        return self.n + k if self.base is None else self.base + (self.n + k)

    def index(self):
        return self.n if self.base is None else self.start + self.n

    def up(self, k=1):
        self.n += k


class Buffers:
    pass


def program(nc, A, out):
    ctx = ExitStack()
    v = Buffers()
    with ctx:
        def sb(name, shape, dt=fp32):
            return ctx.enter_context(nc.sbuf_tensor(name, shape, dt))

        def sem(name):
            return ctx.enter_context(nc.semaphore(name))

        def dram(name, shape, dt):
            return nc.dram_tensor(name, shape, dt, kind="Internal").ap()

        v.sem = sem
        v.q_dram = [dram(f"q_parts{s}", [B, H, PARTS * D, T], bf16) for s in (1, 2)]
        v.k_dram = [dram(f"k_parts{s}", [B, H, (2 * PARTS - 1) * D, TK], bf16) for s in (1, 2)]

        v.ps = ctx.enter_context(nc.psum_tensor("ps", [P, 8, 512], fp32))
        v.ident = sb("ident", [P, P])
        v.identb = sb("identb", [P, P], bf16)
        v.X = sb("X", [P, B, NT, C])
        v.XX = sb("XX", [P, B, NT, C])
        v.AO = sb("AO", [P, UNITS, NT, J * D])
        v.VT = sb("VT", [P, UNITS, NT, J * D])
        v.CV = sb("CV", [P, UNITS, J * D])
        v.Vu = [sb(f"Vu{i}", [P, NT, 2, J, VW]) for i in range(SLOTS)]
        v.wqkvT = sb("wqkvT", [P, 3 * C])
        v.wprojT = sb("wprojT", [P, C])
        v.wqkv2 = sb("wqkv2", [P, 3 * C])
        v.wo2 = sb("wo2", [P, C])
        v.W1 = sb("W1", [P, E, DFF])
        v.W2 = sb("W2", [P, E, FC, C])
        v.b1T = sb("b1T", [P, E, FC])
        v.b2r = sb("b2r", [E, C])
        v.gw = sb("gw", [P, E])
        v.bcol = sb("bcol", [P, 4])
        v.brow = sb("brow", [P, 9, C])
        (v.BK1, v.BV1, v.BP1, v.BV2, v.BO2, v.G1, v.B1, v.G2, v.B2) = range(9)
        v.gbrow = sb("gbrow", [P, E])
        v.iota = sb("iota", [P, E])
        v.qtab = sb("qtab", [P, GS])
        v.ktab = sb("ktab", [P, T])
        v.ctab = sb("ctab", [P, NCL])
        v.ind = sb("ind", [P, 2 * NCL])
        v.mask_q = sb("mask_q", [P, NT, P], bf16)
        v.mask_k = sb("mask_k", [P, NT, P], bf16)
        v.eps = sb("eps", [P, 1])
        v.stat = sb("stat", [P, NT, 6])
        v.mv = sb("mv", [P, NT, 2])
        v.std = sb("std", [P, NT])
        v.rstd = sb("rstd", [P, NT])
        v.Mneg = [sb(f"Mneg{h}", [P, J, NT // 2]) for h in range(2)]
        v.Mres = [sb(f"Mres{h}", [P, J, NT // 2]) for h in range(2)]
        v.Mpart = [sb(f"Mpart{h}", [P, 2 * J, PARTS, NT // 2], bf16) for h in range(2)]
        v.MT = [sb(f"MT{h}", [2 * J * PARTS * NT // 2, P], bf16) for h in range(2)]
        v.rden = sb("rden", [P, NT // 2, J])
        v.EW = sb("EW", [P, B * NT, E])
        SCR = 35600
        scr = sb("scr", [P, SCR], bf16)
        place = [0]

        def carve(shape, dt, reset=False):
            if reset:
                place[0] = 0
            n = 1
            for s in shape:
                n *= s
            n *= 2 if dt == fp32 else 1
            v = scr[:, place[0]:place[0] + n]
            place[0] += n
            assert place[0] <= SCR, place
            if dt == fp32:
                v = v.bitcast(fp32)
            if len(shape) == 2:
                v = v.rearrange("p (a b) -> p a b", a=shape[0])
            if len(shape) == 3:
                v = v.rearrange("p (a b c) -> p a b c", a=shape[0], b=shape[1])
            return v

        v.Qst = [carve([J, T], bf16, reset=i == 0) for i in range(SLOTS)]
        v.Kst = [carve([J, TK], bf16) for _ in range(SLOTS)]
        v.ring = [carve([512], fp32) for _ in range(RING)]
        v.Osb = carve([T], fp32)
        v.Hb = carve([NT, C], fp32, reset=True)
        v.Ab = carve([NT, C], fp32)
        v.Yb = carve([NT, C], fp32)
        v.hT = carve([T], fp32)
        v.aT = carve([T], fp32)
        v.QF = carve([T], fp32)
        v.KF = carve([TK], fp32)
        v.QR = carve([T], fp32)
        v.KR = carve([TK], fp32)
        v.Qp = carve([PARTS, T], bf16)
        v.Kp = carve([PARTS, TK], bf16)
        v.KT = carve([NT, C], fp32)
        v.wx = carve([NT, C], fp32)
        v.junk = carve([NT, C], fp32)
        v.lg = carve([NT], fp32)
        v.sm = carve([P], fp32)
        v.sm2 = carve([16], fp32)
        v.wT = carve([P], fp32)
        v.wt = carve([NT], fp32)
        v.Aw = carve([NT, P], fp32)
        v.wload = carve([3, C], fp32)
        v.wpload = carve([C], fp32)
        v.b1rows = carve([P], fp32)
        v.GL = carve([8, NT, E], fp32, reset=True)
        v.ewT = carve([NT, P], fp32)
        v.hT2 = carve([T], fp32)
        v.aT2 = carve([T], fp32)
        v.Hb2 = carve([NT, C], fp32)
        v.Ab2 = carve([NT, C], fp32)
        v.Nb2 = carve([NT, C], fp32)
        v.red = carve([8, NT], fp32)
        v.H3T = carve([B * T], fp32)
        v.hid = [carve([512], fp32) for _ in range(2 * FC)]
        v.fin = [carve([4, C], fp32) for _ in range(2)]

        v.experts_loaded = sem("experts_loaded")
        load_all(nc, A, v)
        project(nc, 1, v)
        attend(nc, 1, v)
        project(nc, 2, v)
        attend(nc, 2, v)
        gate(nc, v)
        experts(nc, v, out)


def load_all(nc, A, v):
    loaded, const_set, turned, w_out = v.sem("loaded"), v.sem("const_set"), v.sem("turned"), v.sem("w_out")
    jobs = [
        (v.ident[:, :], A["c_ident"]),
        (v.wload, A["L0_attn_w_attn"].rearrange("(a p) c -> p a c", p=P)),
        (v.wpload, A["L0_attn_w_proj"]),
        (v.X[:, :, :, :].rearrange("p b t c -> p (b t) c"),
         A["L0_attn_x"].rearrange("b (t p) c -> p (b t) c", p=P)),
        (v.qtab[:, :], A["c_qtab"]), (v.ktab[:, :], A["c_ktab"]), (v.ctab[:, :], A["c_ctab"]),
        (v.ind[:, :], A["c_ind"]),
        (v.bcol[:, 0:1], A["L0_attn_b_attn"][0:C].rearrange("(p o) -> p o", o=1)),
        (v.bcol[:, 1:2], A["L0_attn_b_attn"][C:2 * C].rearrange("(p o) -> p o", o=1)),
        (v.bcol[:, 2:3], A["L0_ffn_b_qkv"][0:C].rearrange("(p o) -> p o", o=1)),
        (v.bcol[:, 3:4], A["L0_ffn_b_qkv"][C:2 * C].rearrange("(p o) -> p o", o=1)),
        (v.AO[:, 0:4, :, :].rearrange("p u t n -> p (u t n)"), A["c_mask_q"]),
        (v.AO[:, 4:8, :, :].rearrange("p u t n -> p (u t n)"), A["c_mask_k"]),
        (v.wqkv2[:, :], A["L0_ffn_w_qkv"]), (v.wo2[:, :], A["L0_ffn_w_o"]),
        (v.gw[:, :], A["L0_ffn_gate_w"]), (v.iota[:, :], A["c_iota"]),
        (v.b2r[:, :], A["L0_ffn_b2"]),
        (v.b1rows[0:E * FC, :], A["L0_ffn_b1"].rearrange("e (f p) -> (e f) p", p=P)),
        (v.gbrow[:, :], A["L0_ffn_gate_b"].partition_broadcast(P)),
    ]
    rows = {v.BK1: A["L0_attn_b_attn"][C:2 * C], v.BV1: A["L0_attn_b_attn"][2 * C:3 * C],
            v.BP1: A["L0_attn_b_proj"], v.BV2: A["L0_ffn_b_qkv"][2 * C:3 * C], v.BO2: A["L0_ffn_b_o"],
            v.G1: A["L0_ffn_ln1_g"], v.B1: A["L0_ffn_ln1_b"], v.G2: A["L0_ffn_ln2_g"], v.B2: A["L0_ffn_ln2_b"]}
    jobs += [(v.brow[:, k, :], r.partition_broadcast(P)) for k, r in rows.items()]
    jobs += [(v.wx[16 * k:16 * k + 16, :, :],
              A["L0_attn_w_assign"].rearrange("(t k) c -> k t c", k=NCL // NT)[k].partition_broadcast(NTPC))
             for k in range(NCL // NT)]
    experts_in = [(v.W1[:, :, :], A["L0_ffn_W1"].rearrange("e p f -> p e f")),
             (v.W2[:, :, :, :].rearrange("p e f c -> p (e f) c"),
              A["L0_ffn_W2"].rearrange("e (f p) c -> p (e f) c", p=P))]

    with nc.Block() as block:
        @block.sync
        def _(sp):
            for dst, src in jobs:
                sp.dma_start(dst, src).then_inc(loaded, 16)
            for dst, src in experts_in:
                sp.dma_start(dst, src).then_inc(v.experts_loaded, 16)
            sp.wait_ge(loaded, 16 * len(jobs))

        @block.vector
        def _(dve):
            dve.memset(v.eps[:, :], EPS)
            for m in v.Mpart:
                dve.memset(m[:, :, :, :], 0.0)
            dve.wait_ge(loaded, 16 * len(jobs))
            dve.tensor_copy(v.identb[:, :], v.ident[:, :])
            for m, u in ((v.mask_q, 0), (v.mask_k, 4)):
                dve.tensor_copy(m[:, :, :].rearrange("p t n -> p (t n)"),
                                v.AO[:, u:u + 4, :, :].rearrange("p u t n -> p (u t n)"))
            dve.memset(v.ps[:, :, :], 0.0).then_inc(const_set, 1)
            dve.wait_ge(turned, 1)
            dve.tensor_copy(v.wqkvT[:, :], v.ps[:, 0, 0:3 * C])
            dve.tensor_copy(v.b1T[:, :, :].rearrange("p e f -> p (e f)"), v.ps[:, 1, 0:E * FC])
            dve.tensor_copy(v.wprojT[:, :], v.ps[:, 0, 3 * C:4 * C]).then_inc(w_out, 1)

        @block.gpsimd
        def _(pool):
            for i in range(SLOTS):
                pool.memset(v.Vu[i][:, :, :, :, :], 1.0)
            pool.memset(v.rden[:, :, :], 1.0).then_inc(const_set, 1)

        @block.tensor
        def _(pe):
            pe.wait_ge(loaded, 16 * len(jobs))
            pe.wait_ge(const_set, 2)
            for a in range(3):
                pe.transpose(v.ps[:, 0, a * C:a * C + C], v.wload[:, a, :], v.ident[:, :])
            pe.transpose(v.ps[:, 1, 0:E * FC], v.b1rows[0:E * FC, :], v.ident[0:E * FC, 0:E * FC])
            pe.transpose(v.ps[:, 0, 3 * C:4 * C], v.wpload, v.ident[:, :]).then_inc(turned, 1)


def norm_sems(v, S, stage, *tags):
    S["norms"] = tags
    for n in ("stats", "aggr", "root", "inv", "norm"):
        S[n] = v.sem(f"{stage}_{n}")


def norm_count(S, b, tag):
    return b * len(S["norms"]) + (S["norms"].index(tag) + 1)


def norm_steps(dve, v, S, b, src, dst, tag):
    n = norm_count(S, b, tag)
    for t in range(NT):
        last = dve.bn_stats(v.stat[:, t, :], src(t))
    last.then_inc(S["stats"], 1)
    settled(dve, v, S["stats"], n)
    for t in range(NT):
        last = dve.bn_aggr(v.mv[:, t, :], v.stat[:, t, :])
    last.then_inc(S["aggr"], 1)
    dve.wait_ge(S["root"], n)
    dve.reciprocal(v.rstd[:, :], v.std[:, :]).then_inc(S["inv"], 1)
    dve.wait_ge(S["inv"], n)
    for t in range(NT):
        last = dve.tensor_scalar(dst(t), src(t), v.mv[:, t, 0:1], v.rstd[:, t:t + 1],
                                 ALU.subtract, ALU.mult)
    last.then_inc(S["norm"], 1)
    settled(dve, v, S["norm"], n)


def root_step(act, v, S, b, tag):
    act.wait_ge(S["aggr"], norm_count(S, b, tag))
    act.activation(v.std[:, :], v.mv[:, :, 1], ACT.Sqrt, bias=v.eps[:, 0:1]).then_inc(S["root"], 1)


def over(ap, n, axis=1):
    a = ap.unsqueeze(axis)
    s = list(a.shape)
    s[axis] = n
    return a.broadcast_to(s)


def heads_last(VT, b):
    return VT[:, bass.ts(b, HG), :, :].rearrange("p g t n -> p t g n")


def project(nc, stage, v):
    S = {}

    def new(*ns):
        for n in ns:
            S[n] = v.sem(f"p{stage}_{n}")

    new("turned", "hT", "q_ps", "k_ps", "v_ps", "qf", "kf", "kfc", "kv", "q1", "q2", "k1", "k2", "qr", "kr",
        "q3", "k3", "stored_q", "stored_k", "parts_free")
    if stage == 1:
        new("lg", "lgT", "mx", "shifted", "ex", "sums", "winv", "wT", "wback", "wt", "aw", "ck", "cv")
    else:
        new("gather", "aturned", "aT", "y_ps", "y", "x1", "gain", "bias")
    norm_sems(v, S, f"p{stage}", *(("h_",) if stage == 1 else ("a_", "x_", "h_")))
    w = v.wqkvT if stage == 1 else v.wqkv2
    NK = TK if stage == 1 else T
    qd, kd = v.q_dram[stage - 1], v.k_dram[stage - 1]
    bank = lambda i, n=2: v.ps[:, i:i + n, :].rearrange("p a n -> p (a n)")
    KF, KR = v.KF[:, 0:NK], v.KR[:, 0:NK]

    with nc.Block() as block:
        @block.vector
        def _(dve):
            if stage == 1:
                dve.memset(v.sm[:, :], 0.0)
            for n in ("qf", "kf", "kfc") + (("kv",) if stage == 1 else ()):
                dve.sem_inc(S[n], 1)
            with dve.Fori(0, B) as b:
                if stage == 1:
                    norm_steps(dve, v, S, b, lambda t: v.X[:, b, t, :], lambda t: v.Hb[:, t, :], "h_")
                else:
                    dve.wait_ge(S["y_ps"], b + 1)
                    dve.tensor_tensor(v.Yb, bank(2).rearrange("p (t c) -> p t c", t=NT),
                                      over(v.brow[:, v.BP1, :], NT), ALU.add).then_inc(S["y"], 1)
                    dve.wait_ge(S["y"], b + 1)
                    norm_steps(dve, v, S, b, lambda t: v.Yb[:, t, :], lambda t: v.Ab[:, t, :], "a_")
                    dve.tensor_tensor(v.X[:, b, :, :], v.X[:, b, :, :], v.Ab, ALU.add).then_inc(S["x1"], 1)
                    settled(dve, v, S["x1"], b + 1)
                    norm_steps(dve, v, S, b, lambda t: v.X[:, b, t, :], lambda t: v.XX[:, b, t, :], "x_")
                    norm_steps(dve, v, S, b, lambda t: v.XX[:, b, t, :], lambda t: v.Ab[:, t, :], "h_")
                    dve.tensor_tensor(v.Yb, v.Ab, over(v.brow[:, v.G1, :], NT), ALU.mult).then_inc(S["gain"], 1)
                    dve.wait_ge(S["gain"], b + 1)
                    dve.tensor_tensor(v.Hb, v.Yb, over(v.brow[:, v.B1, :], NT), ALU.add).then_inc(S["bias"], 1)
                dve.wait_ge(S["q_ps"], b + 1)
                dve.wait_ge(S["q1"], b + 1)
                dve.wait_ge(S["qr"], b + 1)
                if stage == 1:
                    dve.scalar_tensor_tensor(v.QF.rearrange("p (g s) -> p g s", s=GS),
                                             bank(6).rearrange("p (g s) -> p g s", s=GS), v.bcol[:, 0:1],
                                             over(v.qtab[:, :], T // GS), ALU.add, ALU.mult).then_inc(S["qf"], 1)
                else:
                    dve.tensor_scalar(v.QF, bank(6), v.bcol[:, 2:3], None, ALU.add).then_inc(S["qf"], 1)
                dve.wait_ge(S["k_ps"], b + 1)
                dve.wait_ge(S["k1"], b + 1)
                dve.wait_ge(S["kr"], b + 1)
                if stage == 1:
                    dve.scalar_tensor_tensor(v.KF[:, 0:T], bank(0), v.bcol[:, 1:2], v.ktab[:, :],
                                             ALU.add, ALU.mult).then_inc(S["kf"], 1)
                else:
                    dve.tensor_scalar(v.KF[:, 0:T], bank(0), v.bcol[:, 3:4], None, ALU.add).then_inc(S["kf"], 1)
                dve.wait_ge(S["v_ps"], b + 1)
                if stage == 1:
                    kv = bank(2, 4).rearrange("p (t n) -> p t n", t=NT)
                    dve.tensor_tensor(v.KT, kv[:, :, 0:C], over(v.brow[:, v.BK1, :], NT), ALU.add)
                    dve.tensor_tensor(heads_last(v.VT, b), kv[:, :, C:2 * C].rearrange("p t (g n) -> p t g n", g=HG),
                                      over(v.brow[:, v.BV1, :].rearrange("p (g n) -> p g n", g=HG), NT),
                                      ALU.add).then_inc(S["kv"], 1)
                    for t in range(NT):
                        last = dve.tensor_tensor_reduce(out=v.junk[:, t, :], in0=v.Hb[:, t, :], in1=v.wx[:, t, :],
                                                        scale=1.0, scalar=0.0, op0=ALU.mult, op1=ALU.add,
                                                        accum_out=v.lg[:, t:t + 1])
                    last.then_inc(S["lg"], 1)
                    dve.wait_ge(S["lgT"], b + 1)
                    lgT = v.ps[0:NT, 6, 0:P].rearrange("p (k s) -> p k s", s=NTPC)
                    dve.tensor_reduce(v.sm2[0:NT, 0:8], lgT, AX.X, ALU.max).then_inc(S["mx"], 1)
                    dve.wait_ge(S["mx"], b + 1)
                    smv = v.sm[0:NT, :].rearrange("p (k s) -> p k s", s=NTPC)
                    dve.tensor_tensor(smv, lgT, over(v.sm2[0:NT, 0:8], NTPC, 2), ALU.subtract)\
                       .then_inc(S["shifted"], 1)
                    dve.wait_ge(S["ex"], b + 1)
                    wTv = v.wT[0:NT, :].rearrange("p (k s) -> p k s", s=NTPC)
                    dve.tensor_reduce(v.sm2[0:NT, 8:16], wTv, AX.X, ALU.add).then_inc(S["sums"], 1)
                    dve.wait_ge(S["sums"], b + 1)
                    dve.reciprocal(v.sm2[0:NT, 0:8], v.sm2[0:NT, 8:16]).then_inc(S["winv"], 1)
                    dve.wait_ge(S["winv"], b + 1)
                    dve.tensor_tensor(smv, wTv, over(v.sm2[0:NT, 0:8], NTPC, 2), ALU.mult).then_inc(S["wT"], 1)
                    dve.wait_ge(S["wback"], b + 1)
                    dve.tensor_copy(v.wt[:, :], v.ps[:, 6, P:P + NT]).then_inc(S["wt"], 1)
                    dve.wait_ge(S["wt"], b + 1)
                    for t in range(NT):
                        at = NCL - 8 - 8 * t
                        last = dve.tensor_scalar(v.Aw[:, t, :].rearrange("p (a c) -> p a c", a=2),
                                                 over(v.ind[:, at:at + NCL], 2), v.wt[:, t:t + 1], None, ALU.mult)
                    last.then_inc(S["aw"], 1)
                    dve.wait_ge(S["ck"], b + 1)
                    dve.tensor_tensor(v.KF[:, T:TK], v.ps[:, 7, 0:NCL], v.ctab[:, :], ALU.mult)
                    dve.tensor_copy(v.CV[:, bass.ts(b, HG), :], v.ps[:, 7, P:2 * P].rearrange("p (g n) -> p g n", g=HG))\
                       .then_inc(S["kfc"], 1)
                else:
                    dve.tensor_tensor(heads_last(v.VT, b), bank(2).rearrange("p (t g n) -> p t g n", t=NT, g=HG),
                                      over(v.brow[:, v.BV2, :].rearrange("p (g n) -> p g n", g=HG), NT),
                                      ALU.add).then_inc(S["kfc"], 1)

        @block.scalar
        def _(act):
            for n in ("q1", "k1"):
                act.sem_inc(S[n], 1)
            with act.Fori(0, B) as b:
                if stage == 2:
                    act.wait_ge(S["aturned"], b + 2)
                    act.activation(v.aT, bank(0), ACT.Copy).then_inc(S["aT"], 1)
                    root_step(act, v, S, b, "a_")
                    root_step(act, v, S, b, "x_")
                root_step(act, v, S, b, "h_")
                act.wait_ge(S["turned"], b + 1)
                act.activation(v.hT, bank(4), ACT.Copy).then_inc(S["hT"], 1)
                act.wait_ge(S["qf"], b + 2)
                act.wait_ge(S["parts_free"], b + 1)
                act.activation(v.Qp[:, 0, :], v.QF, ACT.Copy).then_inc(S["q1"], 1)
                act.wait_ge(S["qr"], b + 2)
                act.activation(v.Qp[:, 1, :], v.QR, ACT.Copy).then_inc(S["q2"], 1)
                if stage == 1:
                    act.wait_ge(S["shifted"], b + 1)
                    act.activation(v.wT[0:NT, :], v.sm[0:NT, :], ACT.Exp).then_inc(S["ex"], 1)
                act.wait_ge(S["kf"], b + 2)
                act.wait_ge(S["kfc"], b + 2)
                act.activation(v.Kp[:, 0, 0:NK], KF, ACT.Copy).then_inc(S["k1"], 1)
                act.wait_ge(S["kr"], b + 2)
                act.activation(v.Kp[:, 1, 0:NK], KR, ACT.Copy).then_inc(S["k2"], 1)

        @block.gpsimd
        def _(pool):
            for n in ("qr", "q3", "kr", "k3"):
                pool.sem_inc(S[n], 1)
            with pool.Fori(0, B) as b:
                if stage == 2:
                    pool.wait_ge(S["aturned"], b + 1)
                    for g in range(HG):
                        pool.tensor_copy(v.junk[:, :, g * J * D:(g + 1) * J * D],
                                         v.AO[:, b * HG + g, :, :]).then_inc(S["gather"], 1)
                pool.wait_ge(S["q1"], b + 2)
                pool.wait_ge(S["q3"], b + 1)
                pool.tensor_tensor(v.QR, v.QF, v.Qp[:, 0, :], ALU.subtract).then_inc(S["qr"], 1)
                pool.wait_ge(S["q2"], b + 1)
                pool.tensor_tensor(v.Qp[:, 2, :], v.QR, v.Qp[:, 1, :], ALU.subtract).then_inc(S["q3"], 1)
                pool.wait_ge(S["k1"], b + 2)
                pool.wait_ge(S["k3"], b + 1)
                pool.tensor_tensor(KR, KF, v.Kp[:, 0, 0:NK], ALU.subtract).then_inc(S["kr"], 1)
                pool.wait_ge(S["k2"], b + 1)
                pool.tensor_tensor(v.Kp[:, 2, 0:NK], KR, v.Kp[:, 1, 0:NK], ALU.subtract).then_inc(S["k3"], 1)

        @block.sync
        def _(sp):
            sp.sem_inc(S["parts_free"], 1)
            with sp.Fori(0, B) as b:
                sp.wait_ge(S["q3"], b + 2)
                qrow = qd[b].rearrange("h (a d) n -> a h d n", a=PARTS)
                for a in range(PARTS):
                    sp.dma_start(qrow[a], v.Qp[:, a, :]).then_inc(S["stored_q"], 16)
                sp.wait_ge(S["k3"], b + 2)
                krow = kd[b].rearrange("h (a d) n -> a h d n", a=2 * PARTS - 1)
                for a in range(2 * PARTS - 1):
                    sp.dma_start(krow[a][:, :, 0:NK], v.Kp[:, a % PARTS, 0:NK]).then_inc(S["stored_k"], 16)
                sp.wait_ge(S["stored_q"], b * (16 * PARTS) + 16 * PARTS)
                sp.wait_ge(S["stored_k"], b * (16 * (2 * PARTS - 1)) + 16 * (2 * PARTS - 1))
                sp.sem_inc(S["parts_free"], 1)

        @block.tensor
        def _(pe):
            if stage == 2:
                pe.sem_inc(S["aturned"], 1)
            with pe.Fori(0, B) as b:
                if stage == 2:
                    pe.wait_ge(S["gather"], HG * (b + 1))
                    pe.wait_ge(S["kf"], b + 1)
                    for t in range(NT):
                        last = pe.transpose(v.ps[:, t // 4, t % 4 * C:t % 4 * C + C], v.junk[:, t, :], v.ident[:, :])
                    last.then_inc(S["aturned"], 1)
                    pe.wait_ge(S["aT"], b + 1)
                    pe.wait_ge(S["kfc"], b + 1)
                    for t in range(NT):
                        last = pe.matmul(v.ps[:, 2 + t // 4, t % 4 * C:t % 4 * C + C],
                                         v.aT[:, t * P:t * P + P], v.wprojT[:, :], start=True, stop=True)
                    last.then_inc(S["y_ps"], 1)
                    pe.wait_ge(S["bias"], b + 1)
                else:
                    pe.wait_ge(S["norm"], b + 1)
                    pe.wait_ge(S["kv"], b + 1)
                for t in range(NT):
                    last = pe.transpose(v.ps[:, 4 + t // 4, t % 4 * C:t % 4 * C + C], v.Hb[:, t, :], v.ident[:, :])
                last.then_inc(S["turned"], 1)
                pe.wait_ge(S["hT"], b + 1)
                pe.wait_ge(S["kfc"], b + 1)
                pe.wait_ge(S["qf"], b + 1)
                for n in range(2):
                    last = pe.matmul(v.ps[:, 6 + n, :], w[:, 0:C], v.hT[:, n * 512:n * 512 + 512], start=True, stop=True)
                last.then_inc(S["q_ps"], 1)
                pe.wait_ge(S["kf"], b + 1)
                for n in range(2):
                    last = pe.matmul(v.ps[:, n, :], w[:, C:2 * C], v.hT[:, n * 512:n * 512 + 512], start=True, stop=True)
                last.then_inc(S["k_ps"], 1)
                if stage == 1:
                    for t in range(NT):
                        last = pe.matmul(v.ps[:, 2 + t // 2, t % 2 * 2 * C:t % 2 * 2 * C + 2 * C],
                                         v.hT[:, t * P:t * P + P], w[:, C:3 * C], start=True, stop=True)
                    last.then_inc(S["v_ps"], 1)
                    pe.wait_ge(S["lg"], b + 1)
                    pe.wait_ge(S["qf"], b + 2)
                    pe.transpose(v.ps[0:NT, 6, 0:P], v.lg[:, :], v.ident[:, :]).then_inc(S["lgT"], 1)
                    pe.wait_ge(S["wT"], b + 1)
                    pe.transpose(v.ps[:, 6, P:2 * P], v.sm[:, :], v.ident[:, :]).then_inc(S["wback"], 1)
                    pe.wait_ge(S["aw"], b + 1)
                    pe.wait_ge(S["kv"], b + 2)
                    for t in range(NT):
                        pe.matmul(v.ps[:, 7, 0:NCL], v.KT[:, t, :], v.Aw[:, t, 0:NCL], start=t == 0, stop=t == NT - 1)
                    for t in range(NT):
                        last = pe.matmul(v.ps[:, 7, P:2 * P], v.Aw[:, t, :], v.VT[:, bass.ts(b, HG), t, :],
                                         start=t == 0, stop=t == NT - 1)
                    last.then_inc(S["ck"], 1)
                else:
                    pe.wait_ge(S["y"], b + 1)
                    for t in range(NT):
                        last = pe.matmul(v.ps[:, 2 + t // 4, t % 4 * C:t % 4 * C + C],
                                         v.hT[:, t * P:t * P + P], w[:, 2 * C:3 * C], start=True, stop=True)
                    last.then_inc(S["v_ps"], 1)


def attend(nc, stage, v):
    S = {n: v.sem(f"a{stage}_{n}") for n in (
        "s1_full", "s1_free", "split0", "split1", "split2", "split3", "s2_full", "exp_done", "av_done",
        "o_out", "inv", "vu", "stacked0", "stacked1", "stacked2", "rows0", "rows1", "ones")}
    stacked = [S[f"stacked{i}"] for i in range(SLOTS)]
    rows = [S["rows0"], S["rows1"]]
    full = stage == 2
    PIECES = 16 if full else 4
    GROUPS = 8 if full else 4
    STEPS = 4 if full else 1
    NK = T if full else TK
    TH = NT // 2
    qd = v.q_dram[stage - 1].rearrange("b (g j) r n -> (b g) r j n", j=J)
    kd = v.k_dram[stage - 1].rearrange("b (g j) r n -> (b g) r j n", j=J)
    steps_unit = 2 * GROUPS * STEPS
    LOADS = 6

    def uses(first, last):
        out = []
        for h in range(2):
            for k in range(PIECES):
                if not last:
                    out.append(("piece", h, k))
                if h == 0 and k == 1:
                    out.append(("parts", 1, 0))
                if h == 0 and k == PIECES // 2 + 1 and not first:
                    out += [("outs", 0, 0), ("outs", 1, 0)]
                if h == 1 and k == 1 and not last:
                    out.append(("parts", 0, 1))
        return out

    def schedule(first, last):
        us = uses(first, last)
        n = 2 * GROUPS
        if last:
            return [us[0:1], [], [], us[1:]] + [[] for _ in range(n - 4)]
        return [us[len(us) * g // n:len(us) * (g + 1) // n] for g in range(n)]

    def prologue_uses():
        rest = [("piece", 1, k) for k in range(PIECES)]
        return [("piece", 0, k) for k in range(PIECES)] + rest[:2] + [("parts", 0, 0)] + rest[2:]

    def bodies(eng, tallies, per, body):
        body(0, 0, True, False)
        with eng.Fori(0, LOOPS) as i:
            for t, n in zip(tallies, per):
                t.enter(i, n)
            for r in range(SLOTS):
                body(i * SLOTS + (r + 1), (r + 1) % SLOTS, False, False)
        for t in tallies:
            t.leave(LOOPS)
        for u in range(SLOTS * LOOPS + 1, UNITS):
            body(u, u % SLOTS, False, u == UNITS - 1)

    USES = len(uses(False, False))

    def segments(stack, j, r, a, b):
        one = stack[0:r, j, a:a + 64]
        return bass.AP(tensor=one.tensor, offset=one.offset, ap=[list(one.ap[0]), [b - a, 2], [1, 64]])

    with nc.Block() as block:
        @block.sync
        def _(sp):
            def load(u, slot):
                for c in range(PARTS):
                    sp.dma_start(v.Qst[slot][c * 24:c * 24 + 24, :, :], qd[u]).then_inc(stacked[slot], 16)
                    sp.dma_start(v.Kst[slot][c * 24:c * 24 + 24, :, 0:NK],
                                 kd[u][c * D:c * D + 24, :, 0:NK]).then_inc(stacked[slot], 16)

            def shift_rows(slot, h):
                n = PARTS * TH
                for j in range(J):
                    sp.dma_start(v.Qst[slot][ROWS:KROWS, j, h * HALF:(h + 1) * HALF].rearrange("p (t q) -> p t q", t=TH),
                                 v.MT[h][j * n:j * n + n, :]).then_inc(rows[h], 16)

            s1, s2 = Tally(), Tally()

            def follow(us, now, nxt):
                for kind, h, k in us:
                    s1.up()
                    if kind == "parts":
                        sp.wait_ge(S["s1_free"], s1.at())
                        shift_rows(now if h == 1 else nxt, h)

            sp.wait_ge(S["ones"], SLOTS)
            load(0, 0)
            load(1, 1)
            follow(prologue_uses(), None, 0)

            def body(u, slot, first, last):
                if not (isinstance(u, int) and u + 2 >= UNITS):
                    if not first:
                        sp.wait_ge(S["s2_full"], s2.at())
                    load(u + 2, (slot + 2) % SLOTS)
                s2.up(steps_unit)
                follow(uses(first, last), slot, (slot + 1) % SLOTS)
            bodies(sp, [s1, s2], [USES * SLOTS, SLOTS * steps_unit], body)
            sp.wait_ge(rows[0], 16 * J * UNITS)
            sp.wait_ge(rows[1], 16 * J * UNITS)

        @block.gpsimd
        def _(pool):
            for i in range(SLOTS):
                pool.memset(v.Kst[i][64:96, :, :], 1.0).then_inc(S["ones"], 1)
            pool.wait_ge(S["ones"], SLOTS)
            av = Tally()

            def body(u, slot, first, last):
                out = v.Vu[slot]
                if not (isinstance(u, int) and u < SLOTS):
                    pool.wait_ge(S["av_done"], av.at(-(SLOTS - 1) * 2 * GROUPS))
                av.up(2 * GROUPS)
                if full:
                    pool.tensor_copy(out[:, :, 0, :, 0:D], v.VT[:, u, :, :].rearrange("p t (j d) -> p t j d", j=J))\
                        .then_inc(S["vu"], 1)
                    return
                for s, lo, cl in ((0, 0, 64), (1, 64, 0)):
                    pool.tensor_copy(out[lo:lo + 64, :, s, :, 0:D],
                                     v.VT[lo:lo + 64, u, :, :].rearrange("p t (j d) -> p t j d", j=J))
                    last_one = pool.tensor_copy(out[cl:cl + 64, :, s, :, 0:D],
                                                over(v.CV[cl:cl + 64, u, :].rearrange("p (j d) -> p j d", j=J), NT))
                last_one.then_inc(S["vu"], 1)
            for u in range(SLOTS):
                body(u, u, u == 0, False)
            with pool.Fori(0, LOOPS) as i:
                av.enter(i, 2 * GROUPS * SLOTS)
                for r in range(SLOTS):
                    body(i * SLOTS + (r + SLOTS), r, False, False)
            av.leave(LOOPS)
            body(UNITS - 1, (UNITS - 1) % SLOTS, False, True)

        @block.vector
        def _(dve):
            s1, spl, inv = Tally(), Tally(), Tally()
            taken = [Tally(), Tally()]
            dve.sem_inc(S["inv"], 1)
            inv.up()

            def use(kind, h, k, u):
                at = s1.index() % 2
                s1.up()
                dve.wait_ge(S["s1_full"], s1.at())
                banks = v.ps[:, 2 * at:2 * at + 2, :].rearrange("p a n -> p (a n)")
                if kind == "piece":
                    if k == 0:
                        if spl.base is not None or spl.n:
                            dve.wait_ge(S["split3"], spl.at())
                    if full:
                        j, t = k % J, k // J
                        ins = dve.tensor_reduce(v.Mneg[h][:, j, t:t + 1], banks, AX.X, ALU.max, negate=True)
                    else:
                        ins = dve.tensor_reduce(v.Mneg[h][:, :, k], banks[:, 0:512].rearrange("p (j n) -> p j n", j=J),
                                                AX.X, ALU.max, negate=True)
                    ins.then_inc(S["s1_free"], 1)
                    if k == PIECES - 1:
                        dve.wait_ge(S["s1_free"], s1.at())
                        m, r, p = v.Mneg[h][:, :, :], v.Mres[h][:, :, :], v.Mpart[h][:, 0:J, :, :]
                        dve.tensor_copy(p[:, :, 0, :], m).then_inc(S["split0"], 1)
                        dve.wait_ge(S["split0"], spl.at(1))
                        dve.tensor_tensor(r, m, p[:, :, 0, :], ALU.subtract).then_inc(S["split1"], 1)
                        dve.wait_ge(S["split1"], spl.at(1))
                        dve.tensor_copy(p[:, :, 1, :], r).then_inc(S["split2"], 1)
                        dve.wait_ge(S["split2"], spl.at(1))
                        dve.tensor_tensor(p[:, :, 2, :], r, p[:, :, 1, :], ALU.subtract).then_inc(S["split3"], 1)
                        spl.up()
                elif kind == "parts":
                    if taken[h].base is not None or taken[h].n:
                        dve.wait_ge(rows[h], taken[h].at())
                    taken[h].up(16 * J)
                    dve.tensor_copy(v.MT[h][:, :], banks[0:2 * J * PARTS * TH, 0:P // 2].bitcast(bf16))\
                       .then_inc(S["s1_free"], 1)
                else:
                    o = banks[:, 0:512].rearrange("p (t j n) -> p t j n", t=TH, j=J)
                    dve.wait_ge(S["s1_free"], s1.at(-1))
                    dve.reciprocal(v.rden[:, :, :], o[:, :, :, D]).then_inc(S["inv"], 1)
                    inv.up()
                    dve.wait_ge(S["inv"], inv.at())
                    dst = v.AO[:, u - 1, h * TH:(h + 1) * TH, :].rearrange("p t (j d) -> p t j d", j=J)
                    dve.tensor_tensor(dst, o[:, :, :, 0:D], over(v.rden[:, :, :], D, 3), ALU.mult)\
                       .then_inc(S["s1_free"], 1)

            for kind, h, k in prologue_uses():
                use(kind, h, k, 0)

            def body(u, slot, first, last):
                for kind, h, k in uses(first, last):
                    use(kind, h, k, u)
            bodies(dve, [s1, spl, inv] + taken,
                   [USES * SLOTS, 2 * SLOTS, 2 * SLOTS, 16 * J * SLOTS, 16 * J * SLOTS], body)
            for h in range(2):
                use("outs", h, 0, UNITS)

        @block.scalar
        def _(act):
            s2, done, outs = Tally(), Tally(), Tally()
            lag = RING // STEPS

            def body(u, slot, first, last):
                for g in range(2 * GROUPS):
                    for s in range(STEPS):
                        n = s2.index()
                        s2.up()
                        act.wait_ge(S["s2_full"], s2.at())
                        if s == 0 and not (first and g < lag):
                            act.wait_ge(S["av_done"], done.at(1 - lag))
                        act.activation(v.ring[n % RING], v.ps[:, 4 + n % 2, :], ACT.Exp, scale=SCALE)\
                           .then_inc(S["exp_done"], 1)
                    done.up()
                    if g == 1 and not first:
                        act.wait_ge(S["av_done"], done.at(-2))
                        act.wait_ge(S["inv"], outs.at(1))
                        act.activation(v.Osb[:, HALF:T], v.ps[:, 7, :], ACT.Copy).then_inc(S["o_out"], 1)
                    if g == GROUPS + 1:
                        act.wait_ge(S["av_done"], done.at(-2))
                        if not first:
                            act.wait_ge(S["inv"], outs.at(2))
                            outs.up(2)
                        act.activation(v.Osb[:, 0:HALF], v.ps[:, 6, :], ACT.Copy).then_inc(S["o_out"], 1)
            bodies(act, [s2, done, outs], [SLOTS * steps_unit, SLOTS * 2 * GROUPS, 2 * SLOTS], body)
            act.wait_ge(S["av_done"], done.at())
            act.wait_ge(S["inv"], outs.at(1))
            act.activation(v.Osb[:, HALF:T], v.ps[:, 7, :], ACT.Copy).then_inc(S["o_out"], 1)

        @block.tensor
        def _(pe):
            s1, s2, spl, outs, rws, vu, oc = (Tally() for _ in range(7))
            stk = [Tally() for _ in range(SLOTS)]

            def use(kind, h, k, slot):
                at = s1.index() % 2
                if s1.base is not None or s1.n >= 2:
                    pe.wait_ge(S["s1_free"], s1.at(-1))
                s1.up()
                banks = v.ps[:, 2 * at:2 * at + 2, :]
                if kind == "piece" and full:
                    j, t = k % J, k // J
                    for n in range(2):
                        last = pe.matmul(banks[:, n, :], v.Qst[slot][0:ROWS, j, h * HALF + t * P:h * HALF + t * P + P],
                                         v.Kst[slot][0:ROWS, j, n * 512:n * 512 + 512], start=True, stop=True)
                elif kind == "piece":
                    t = h * TH + k
                    pe.matmul(banks[:, 0, :], v.identb[:, :], over(v.mask_q[:, t, :], J), start=True, stop=False,
                              skip_group_check=True)
                    for j in range(J):
                        for s in range(2):
                            q0 = t * P + 64 * s
                            last = pe.matmul(banks[64 * s:64 * s + 64, 0, j * P:j * P + P],
                                             v.Qst[slot][0:ROWS, j, q0:q0 + 64],
                                             segments(v.Kst[slot], j, ROWS, q0, T), start=False, stop=True,
                                             skip_group_check=True)
                elif kind == "parts":
                    spl.up()
                    pe.wait_ge(S["split3"], spl.at())
                    last = pe.transpose(banks[0:2 * J * PARTS * TH, 0, 0:P // 2].bitcast(bf16),
                                        v.Mpart[h][:, :, :, :].rearrange("p j a t -> p (j a t)"), v.identb[:, :])
                else:
                    outs.up()
                    pe.wait_ge(S["o_out"], outs.at())
                    for t in range(TH):
                        q0 = h * HALF + t * P
                        last = pe.transpose(banks[:, 0, t * P:t * P + P], v.Osb[:, q0:q0 + P], v.ident[:, :])
                last.then_inc(S["s1_full"], 1)

            def scores(g, s, slot):
                n = s2.index()
                if s2.base is not None or s2.n >= 2:
                    pe.wait_ge(S["exp_done"], s2.at(-1))
                s2.up()
                o = v.ps[:, 4 + n % 2, :]
                if full:
                    h, kt = g // GROUPS, g % GROUPS
                    last = pe.matmul(o, v.Kst[slot][0:KROWS, s, kt * P:kt * P + P],
                                     v.Qst[slot][0:KROWS, s, h * HALF:(h + 1) * HALF], start=True, stop=True)
                else:
                    pe.matmul(o, v.identb[:, :], over(v.mask_k[:, g, :].rearrange("p (s q) -> p s q", s=2), J, 2),
                              start=True, stop=False, skip_group_check=True)
                    for hs in range(2):
                        q0 = g * P + 64 * hs
                        for j in range(J):
                            c = (hs * J + j) * 64
                            for p0, k0 in ((64 * hs, q0), (64 - 64 * hs, T)):
                                last = pe.matmul(o[p0:p0 + 64, c:c + 64], v.Kst[slot][0:KROWS, j, k0:k0 + 64],
                                                 v.Qst[slot][0:KROWS, j, q0:q0 + 64], start=False, stop=True,
                                                 skip_group_check=True)
                last.then_inc(S["s2_full"], 1)

            def times_v(g, slot, n):
                h = g // GROUPS
                pe.wait_ge(S["exp_done"], n)
                if full:
                    kt = g % GROUPS
                    for j in range(J):
                        last = pe.matmul(v.ps[32 * j:32 * j + VW, 6 + h, :], v.Vu[slot][:, kt, 0, j, :],
                                         v.ring[(STEPS * g + j) % RING], start=kt == 0, stop=kt == GROUPS - 1)
                else:
                    for hs in range(2):
                        for j in range(J):
                            c = (hs * J + j) * 64
                            q0 = g % TH * P + 64 * hs
                            last = pe.matmul(v.ps[32 * j:32 * j + VW, 6 + h, q0:q0 + 64], v.Vu[slot][:, g, hs, j, :],
                                             v.ring[g % RING][:, c:c + 64], start=True, stop=True)
                last.then_inc(S["av_done"], 1)

            stk[0].up(16 * LOADS)
            pe.wait_ge(stacked[0], stk[0].at())
            for kind, h, k in prologue_uses():
                use(kind, h, k, 0)

            def body(u, slot, first, last):
                nxt = (slot + 1) % SLOTS
                if not last:
                    stk[nxt].up(16 * LOADS)
                    pe.wait_ge(stacked[nxt], stk[nxt].at())
                sched = schedule(first, last)
                rws.up(16 * J)
                vu.up()
                for g in range(2 * GROUPS):
                    if g % GROUPS == 0:
                        pe.wait_ge(rows[g // GROUPS], rws.at())
                    work = list(sched[g])
                    for s in range(STEPS):
                        scores(g, s, slot)
                        if s % 2 == 1 and work:
                            use(*work.pop(0), slot=nxt)
                    if g == 0 and not first:
                        times_v(2 * GROUPS - 1, (slot + 2) % SLOTS, s2.at(-STEPS))
                    if g > 0:
                        if g == 1:
                            pe.wait_ge(S["vu"], vu.at())
                        if (g - 1) % GROUPS == 0 and not first:
                            pe.wait_ge(S["o_out"], oc.at(1 if g == 1 else 2))
                        times_v(g - 1, slot, s2.at(-STEPS))
                    while work:
                        use(*work.pop(0), slot=nxt)
                if not first:
                    oc.up(2)
            bodies(pe, [s1, s2, spl, outs, rws, vu, oc] + stk,
                   [USES * SLOTS, SLOTS * steps_unit, 2 * SLOTS, 2 * SLOTS, 16 * J * SLOTS, SLOTS, 2 * SLOTS]
                   + [16 * LOADS] * SLOTS, body)
            times_v(2 * GROUPS - 1, (UNITS - 1) % SLOTS, s2.at())
            for h in range(2):
                use("outs", h, 0, 0)


def gate(nc, v):
    S = {}
    norm_sems(v, S, "g", "h_")
    for n in ("gather", "aturned", "aT", "y_ps", "yb", "x2", "gain", "bias", "turned", "hT", "lg_ps", "delta", "ex",
              "ew", "ewturned", "ewT", "b2_ps", "x3", "chain", "t1", "t2"):
        S[n] = v.sem(f"g_{n}")
    bank = lambda i, n=2: v.ps[:, i:i + n, :].rearrange("p a n -> p (a n)")
    rowsof = lambda a: a.rearrange("p (t c) -> p t c", t=NT)
    LINKS = 14

    with nc.Block() as block:
        @block.gpsimd
        def _(pool):
            with pool.Fori(0, B) as b:
                pool.wait_ge(S["aturned"], b + 1)
                for g in range(HG):
                    last = pool.tensor_copy(v.Ab2[:, :, g * J * D:(g + 1) * J * D], v.AO[:, b * HG + g, :, :])
                last.then_inc(S["gather"], 1)

        @block.tensor
        def _(pe):
            pe.sem_inc(S["aturned"], 1)
            with pe.Fori(0, B) as b:
                pe.wait_ge(S["gather"], b + 1)
                pe.wait_ge(S["x3"], b + 1)
                for t in range(NT):
                    last = pe.transpose(v.ps[:, t // 4, t % 4 * C:t % 4 * C + C], v.Ab2[:, t, :], v.ident[:, :])
                last.then_inc(S["aturned"], 1)
                pe.wait_ge(S["aT"], b + 1)
                for t in range(NT):
                    last = pe.matmul(v.ps[:, 2 + t // 4, t % 4 * C:t % 4 * C + C], v.aT2[:, t * P:t * P + P],
                                     v.wo2[:, :], start=True, stop=True)
                last.then_inc(S["y_ps"], 1)
                pe.wait_ge(S["bias"], b + 1)
                for t in range(NT):
                    last = pe.transpose(v.ps[:, 4 + t // 4, t % 4 * C:t % 4 * C + C], v.Hb2[:, t, :], v.ident[:, :])
                last.then_inc(S["turned"], 1)
                pe.wait_ge(S["hT"], b + 1)
                for t in range(NT):
                    last = pe.matmul(v.ps[:, 6, t * E:t * E + E], v.hT2[:, t * P:t * P + P], v.gw[:, :],
                                     start=True, stop=True)
                last.then_inc(S["lg_ps"], 1)
                pe.wait_ge(S["ew"], b + 1)
                for t in range(NT):
                    last = pe.transpose(v.ps[0:E, 2 + t // 4, t % 4 * P:t % 4 * P + P], v.GL[:, 7, t, :], v.ident[:, :])
                last.then_inc(S["ewturned"], 1)
                pe.wait_ge(S["ewT"], b + 1)
                for t in range(NT):
                    last = pe.matmul(v.ps[:, t // 4, t % 4 * C:t % 4 * C + C], v.ewT[0:E, t, :], v.b2r[:, :],
                                     start=True, stop=True)
                last.then_inc(S["b2_ps"], 1)

        @block.scalar
        def _(act):
            with act.Fori(0, B) as b:
                act.wait_ge(S["aturned"], b + 2)
                act.activation(v.aT2, bank(0), ACT.Copy).then_inc(S["aT"], 1)
                root_step(act, v, S, b, "h_")
                act.wait_ge(S["turned"], b + 1)
                act.activation(v.hT2, bank(4), ACT.Copy).then_inc(S["hT"], 1)
                act.wait_ge(S["hT"], b + 1)
                act.activation(v.H3T[:, bass.ts(b, T)], v.hT2, ACT.Copy)
                act.wait_ge(S["delta"], b + 1)
                act.activation(v.red[:, 4, :], v.red[:, 3, :], ACT.Exp).then_inc(S["ex"], 1)
                act.wait_ge(S["ewturned"], b + 1)
                act.activation(v.ewT[0:E, :, :], v.ps[0:E, 2:4, :].rearrange("p a (t c) -> p (a t) c", c=P), ACT.Copy)\
                   .then_inc(S["ewT"], 1)

        @block.vector
        def _(dve):
            dve.sem_inc(S["x3"], 1)
            with dve.Fori(0, B) as b:
                chain = [0]

                def link(ins):
                    chain[0] += 1
                    ins.then_inc(S["chain"], 1)
                    dve.wait_ge(S["chain"], b * LINKS + chain[0])

                dve.wait_ge(S["y_ps"], b + 1)
                dve.tensor_tensor(v.Hb2, rowsof(bank(2)), over(v.brow[:, v.BO2, :], NT), ALU.add).then_inc(S["yb"], 1)
                dve.wait_ge(S["yb"], b + 1)
                dve.tensor_tensor(v.XX[:, b, :, :], v.XX[:, b, :, :], v.Hb2, ALU.add).then_inc(S["x2"], 1)
                settled(dve, v, S["x2"], b + 1)
                norm_steps(dve, v, S, b, lambda t: v.XX[:, b, t, :], lambda t: v.Nb2[:, t, :], "h_")
                dve.tensor_tensor(v.Nb2, v.Nb2, over(v.brow[:, v.G2, :], NT), ALU.mult).then_inc(S["gain"], 1)
                dve.wait_ge(S["gain"], b + 1)
                dve.tensor_tensor(v.Hb2, v.Nb2, over(v.brow[:, v.B2, :], NT), ALU.add).then_inc(S["bias"], 1)
                L, hit1, first1, L2, hit2, first2, ew = (v.GL[:, k, :, :] for k in (0, 1, 2, 3, 4, 5, 7))
                m1, m2, i1, delta, ex, den, i2 = (v.red[:, k, :] for k in (0, 1, 2, 3, 4, 5, 6))
                dve.wait_ge(S["lg_ps"], b + 1)
                link(dve.tensor_tensor(L, v.ps[:, 6, 0:NT * E].rearrange("p (t e) -> p t e", t=NT),
                                       over(v.gbrow[:, :], NT), ALU.add))
                link(dve.tensor_reduce(m1, L, AX.X, ALU.max))
                link(dve.tensor_tensor(hit1, L, over(m1, E, 2), ALU.is_equal))
                link(dve.scalar_tensor_tensor(first1, hit1, -float(E), over(v.iota[:, :], NT), ALU.mult, ALU.add))
                link(dve.tensor_reduce(i1, first1, AX.X, ALU.min))
                link(dve.tensor_tensor(hit1, first1, over(i1, E, 2), ALU.is_equal))
                link(dve.scalar_tensor_tensor(L2, hit1, -3.0e38, L, ALU.mult, ALU.add))
                link(dve.tensor_reduce(m2, L2, AX.X, ALU.max))
                dve.tensor_tensor(delta, m2, m1, ALU.subtract).then_inc(S["delta"], 1)
                link(dve.tensor_tensor(hit2, L2, over(m2, E, 2), ALU.is_equal))
                link(dve.scalar_tensor_tensor(first2, hit2, -float(E), over(v.iota[:, :], NT), ALU.mult, ALU.add))
                link(dve.tensor_reduce(i2, first2, AX.X, ALU.min))
                link(dve.tensor_tensor(hit2, first2, over(i2, E, 2), ALU.is_equal))
                dve.wait_ge(S["ex"], b + 1)
                link(dve.tensor_scalar(den, ex, 1.0, None, ALU.add))
                link(dve.reciprocal(m1, den))
                dve.tensor_tensor(first2, hit2, over(ex, E, 2), ALU.mult).then_inc(S["t1"], 1)
                dve.wait_ge(S["t1"], b + 1)
                dve.tensor_tensor(first1, first2, hit1, ALU.add).then_inc(S["t2"], 1)
                dve.wait_ge(S["t2"], b + 1)
                dve.tensor_tensor(v.EW[:, bass.ts(b, NT), :], first1, over(m1, E, 2), ALU.mult)
                dve.tensor_tensor(ew, first1, over(m1, E, 2), ALU.mult).then_inc(S["ew"], 1)
                assert chain[0] == LINKS
                dve.wait_ge(S["b2_ps"], b + 1)
                dve.tensor_tensor(v.XX[:, b, :, :], v.XX[:, b, :, :], rowsof(bank(0)), ALU.add).then_inc(S["x3"], 1)


def experts(nc, v, out):
    CT = 4
    CHUNKS = B * NT // CT
    S = {n: v.sem(f"e_{n}") for n in ("hid_full", "relu_done", "out_full", "added", "stats", "aggr", "root", "inv",
                                      "norm", "fin", "stored", "fin_free")}
    XXt = v.XX[:, :, :, :].rearrange("p b t c -> p (b t) c")
    Xt = v.X[:, :, :, :].rearrange("p b t c -> p (b t) c")
    outt = out.rearrange("b (t p) c -> p (b t) c", p=P)

    with nc.Block() as block:
        @block.tensor
        def _(pe):
            pe.sem_inc(S["out_full"], 1)
            pe.wait_ge(v.experts_loaded, 32)
            with pe.Fori(0, CHUNKS) as c:
                def hidden(e):
                    for f in range(FC):
                        pe.wait_ge(S["relu_done"], c * (E * FC) + (e * FC + f - FC + 1 if e else 0) + 1)
                        pe.matmul(v.ps[:, f, :], v.W1[:, e, f * P:f * P + P], v.H3T[:, bass.ts(c, CT * P)],
                                  start=True, stop=True).then_inc(S["hid_full"], 1)

                hidden(0)
                for e in range(E):
                    if e + 1 < E:
                        hidden(e + 1)
                    pe.wait_ge(S["relu_done"], c * (E * FC) + (e + 1) * FC + 1)
                    pe.wait_ge(S["added"], c * E + max(e - 1, 0) + 1)
                    for t in range(CT):
                        for f in range(FC):
                            last = pe.matmul(v.ps[:, 4 + e % 2, t * C:t * C + C],
                                             v.hid[e % 2 * FC + f][:, t * P:t * P + P], v.W2[:, e, f, :],
                                             start=f == 0, stop=f == FC - 1)
                    last.then_inc(S["out_full"], 1)

        @block.scalar
        def _(act):
            act.sem_inc(S["relu_done"], 1)
            with act.Fori(0, CHUNKS) as c:
                for e in range(E):
                    act.wait_ge(S["out_full"], c * E + max(e - 1, 0) + 1)
                    for f in range(FC):
                        act.wait_ge(S["hid_full"], c * E * FC + (e * FC + f + 1))
                        act.activation(v.hid[e % 2 * FC + f], v.ps[:, f, :], ACT.Relu, bias=v.b1T[:, e, f:f + 1])\
                           .then_inc(S["relu_done"], 1)
                act.wait_ge(S["aggr"], c + 1)
                act.activation(v.std[:, 0:CT], v.mv[:, 0:CT, 1], ACT.Sqrt, bias=v.eps[:, 0:1]).then_inc(S["root"], 1)

        @block.vector
        def _(dve):
            dve.sem_inc(S["added"], 1)
            with dve.Fori(0, CHUNKS) as c:
                for e in range(E):
                    dve.wait_ge(S["out_full"], c * E + (e + 2))
                    dve.wait_ge(S["added"], c * E + (e + 1))
                    for t in range(CT):
                        x = XXt[:, c * CT + t, :]
                        last = dve.scalar_tensor_tensor(x, v.ps[:, 4 + e % 2, t * C:t * C + C],
                                                        v.EW[:, c * CT + t, e:e + 1], x, ALU.mult, ALU.add)
                    last.then_inc(S["added"], 1)
                settled(dve, v, S["added"], c * E + (E + 1))
                for t in range(CT):
                    last = dve.bn_stats(v.stat[:, t, :], XXt[:, c * CT + t, :])
                last.then_inc(S["stats"], 1)
                settled(dve, v, S["stats"], c + 1)
                for t in range(CT):
                    last = dve.bn_aggr(v.mv[:, t, :], v.stat[:, t, :])
                last.then_inc(S["aggr"], 1)
                dve.wait_ge(S["root"], c + 1)
                dve.reciprocal(v.rstd[:, 0:CT], v.std[:, 0:CT]).then_inc(S["inv"], 1)
                dve.wait_ge(S["inv"], c + 1)
                for t in range(CT):
                    last = dve.tensor_scalar(XXt[:, c * CT + t, :], XXt[:, c * CT + t, :], v.mv[:, t, 0:1],
                                             v.rstd[:, t:t + 1], ALU.subtract, ALU.mult)
                last.then_inc(S["norm"], 1)
                dve.wait_ge(S["norm"], c + 1)
                dve.wait_ge(S["fin_free"], c + 1)
                dve.tensor_tensor(v.fin[0], XXt[:, bass.ts(c, CT), :], Xt[:, bass.ts(c, CT), :], ALU.add)\
                   .then_inc(S["fin"], 1)

        @block.sync
        def _(sp):
            sp.sem_inc(S["fin_free"], 1)
            with sp.Fori(0, CHUNKS) as c:
                sp.wait_ge(S["fin"], c + 1)
                sp.dma_start(outt[:, bass.ts(c, CT), :], v.fin[0]).then_inc(S["stored"], 16)
                sp.wait_ge(S["stored"], c * 16 + 16)
                sp.sem_inc(S["fin_free"], 1)


_INS = ["L0_attn_x", "L0_attn_w_attn", "L0_attn_b_attn", "L0_attn_w_proj", "L0_attn_b_proj", "L0_attn_w_assign",
        "L0_ffn_ln1_g", "L0_ffn_ln1_b", "L0_ffn_w_qkv", "L0_ffn_b_qkv", "L0_ffn_w_o", "L0_ffn_b_o", "L0_ffn_ln2_g",
        "L0_ffn_ln2_b", "L0_ffn_gate_w", "L0_ffn_gate_b", "L0_ffn_W1", "L0_ffn_b1", "L0_ffn_W2", "L0_ffn_b2"]


def constants():
    import numpy as np

    f = np.float32
    div = np.exp(np.arange(0, D, 2, dtype=f) * f(-np.log(10000.0) / D)).astype(f)

    def table(pos):
        ang = np.asarray(pos, f)[:, None] * div
        s = np.stack([np.sin(ang), np.cos(ang)], axis=-1).reshape(len(pos), D).astype(f)
        a = np.stack([s[:, :D // 2], s[:, D // 2:]], axis=-1).reshape(len(pos), D)
        return np.tile(a, (1, H))

    t = np.arange(T)
    p = np.arange(P)
    neg = f(-1e30)
    mask_q = np.zeros((P, NT, P), f)
    mask_k = np.zeros((P, NT, P), f)
    for tile in range(NT):
        for q in range(P):
            s, r = q // 64, q % 64
            k = np.arange(64)
            local = (k // GS == r // GS) & (k <= r)
            group = (tile * P + q) // GS
            clus = k < group * NCPG
            row = np.where(np.concatenate([local, clus]), f(0), neg)
            mask_q[q, tile] = row
            mask_k[:, tile, q] = row if s == 0 else np.concatenate([row[64:], row[:64]])
    return {
        "c_ident": np.eye(P, dtype=f),
        "c_qtab": np.ascontiguousarray(table(np.arange(GS)).T),
        "c_ktab": np.ascontiguousarray(table(t // GS * NCPG + t % GS).T),
        "c_ctab": np.ascontiguousarray(table(np.arange(NCL)).T),
        "c_ind": (np.arange(2 * NCL)[None, :] == (NCL - 8) + p[:, None] // NTPC).astype(f),
        "c_iota": np.tile(np.arange(E, dtype=f), (P, 1)),
        "c_mask_q": mask_q.reshape(P, NT * P),
        "c_mask_k": mask_k.reshape(P, NT * P),
    }


def kernel(**inputs):
    import numpy as np
    import concourse.bacc as bacc
    from concourse.bass_utils import run_bass_kernel_spmd as run

    nc = bacc.Bacc("TRN2", target_bir_lowering=False, num_devices=1)
    arrays = {n: np.ascontiguousarray(inputs[n]) for n in _INS}
    arrays.update(constants())
    A = {n: nc.dram_tensor(f"in_{n}", a.shape, mybir.dt.from_np(a.dtype), kind="ExternalInput").ap()
         for n, a in arrays.items()}
    out = nc.dram_tensor("out_dram", (B, T, C), fp32, kind="ExternalOutput").ap()
    program(nc, A, out)
    r = run(nc, [{f"in_{n}": a for n, a in arrays.items()}], core_ids=[0])
    return r.results[0]["out_dram"]
```

```python
import concourse.bass as bass
from concourse import mybir
from contextlib import ExitStack

P = 128
B, T, C = 4, 1024, 128
H, D = 16, 8
HG, J = 4, 4
UNITS = B * HG
NT = T // P
HALF = T // 2
NCL, GS, NTPC = 64, 32, 16
NCPG = GS // NTPC
E, DFF = 8, 512
FC = DFF // P
TK = T + NCL
PARTS = 3
ROWS = PARTS * PARTS * D
KROWS = ROWS + PARTS
VW = D + 1
RING = 8
SLOTS = 3
LOOPS = 4
SCALE = float(D) ** -0.5
EPS = 1e-5

fp32 = mybir.dt.float32
bf16 = mybir.dt.bfloat16
ALU = mybir.AluOpType
ACT = mybir.ActivationFunctionType
AX = mybir.AxisListType


def settled(dve, v, sem, value):
    dve.wait_ge(sem, value)
    dve.memset(v.rstd[:, :], 0.0)


class Tally:

    def __init__(self):
        self.n = 0
        self.base = None

    def enter(self, i, per):
        self.base, self.per, self.start = self.n + i * per, per, self.n
        self.n = 0

    def leave(self, trips):
        assert self.n == self.per, (self.n, self.per)
        self.n = self.start + self.per * trips
        self.base = None

    def at(self, k=0):
        return self.n + k if self.base is None else self.base + (self.n + k)

    def index(self):
        return self.n if self.base is None else self.start + self.n

    def up(self, k=1):
        self.n += k


class Buffers:
    pass


def program(nc, A, out):
    ctx = ExitStack()
    v = Buffers()
    with ctx:
        def sb(name, shape, dt=fp32):
            return ctx.enter_context(nc.sbuf_tensor(name, shape, dt))

        def sem(name):
            return ctx.enter_context(nc.semaphore(name))

        def dram(name, shape, dt):
            return nc.dram_tensor(name, shape, dt, kind="Internal").ap()

        v.sem = sem
        v.q_dram = [dram(f"q_parts{s}", [B, H, PARTS * D, T], bf16) for s in (1, 2)]
        v.k_dram = [dram(f"k_parts{s}", [B, H, (2 * PARTS - 1) * D, TK], bf16) for s in (1, 2)]

        v.ps = ctx.enter_context(nc.psum_tensor("ps", [P, 8, 512], fp32))
        v.ident = sb("ident", [P, P])
        v.identb = sb("identb", [P, P], bf16)
        v.X = sb("X", [P, B, NT, C])
        v.XX = sb("XX", [P, B, NT, C])
        v.AO = sb("AO", [P, UNITS, NT, J * D])
        v.VT = sb("VT", [P, UNITS, NT, J * D])
        v.CV = sb("CV", [P, UNITS, J * D])
        v.Vu = [sb(f"Vu{i}", [P, NT, 2, J, VW]) for i in range(SLOTS)]
        v.wqkvT = sb("wqkvT", [P, 3 * C])
        v.wprojT = sb("wprojT", [P, C])
        v.wqkv2 = sb("wqkv2", [P, 3 * C])
        v.wo2 = sb("wo2", [P, C])
        v.W1 = sb("W1", [P, E, DFF])
        v.W2 = sb("W2", [P, E, FC, C])
        v.b1T = sb("b1T", [P, E, FC])
        v.b2r = sb("b2r", [E, C])
        v.gw = sb("gw", [P, E])
        v.bcol = sb("bcol", [P, 4])
        v.gbcol = sb("gbcol", [P, 4])
        v.brow = sb("brow", [P, 5, C])
        (v.BK1, v.BV1, v.BP1, v.BV2, v.BO2) = range(5)
        v.gbrow = sb("gbrow", [P, E])
        v.iota = sb("iota", [P, E])
        v.qtab = sb("qtab", [P, GS])
        v.ktab = sb("ktab", [P, T])
        v.ctab = sb("ctab", [P, NCL])
        v.ind = sb("ind", [P, 2 * NCL])
        v.mask_q = sb("mask_q", [P, NT, P], bf16)
        v.mask_k = sb("mask_k", [P, NT, P], bf16)
        v.eps = sb("eps", [P, 1])
        v.stat = sb("stat", [P, NT, 6])
        v.mv = sb("mv", [P, NT, 2])
        v.rstd = sb("rstd", [P, NT])
        v.mv_all = sb("mv_all", [P, B * NT, 2])
        v.mv_chunk = sb("mv_chunk", [P, NT // 2, 2])
        v.std_all = sb("std_all", [P, B * NT])
        v.rstd_all = sb("rstd_all", [P, B * NT])
        v.shift_all = sb("shift_all", [P, B * NT])
        v.Mneg = [sb(f"Mneg{h}", [P, J, NT // 2]) for h in range(2)]
        v.Mres = [sb(f"Mres{h}", [P, J, NT // 2]) for h in range(2)]
        v.Mpart = [sb(f"Mpart{h}", [P, 2 * J, PARTS, NT // 2], bf16) for h in range(2)]
        v.MT = [sb(f"MT{h}", [2 * J * PARTS * NT // 2, P], bf16) for h in range(2)]
        v.rden = sb("rden", [P, NT // 2, J])
        v.EW = sb("EW", [P, B * NT, E])
        SCR = 35600
        scr = sb("scr", [P, SCR], bf16)
        place = [0]

        def carve(shape, dt, reset=False):
            if reset:
                place[0] = 0
            n = 1
            for s in shape:
                n *= s
            n *= 2 if dt == fp32 else 1
            v = scr[:, place[0]:place[0] + n]
            place[0] += n
            assert place[0] <= SCR, place
            if dt == fp32:
                v = v.bitcast(fp32)
            if len(shape) == 2:
                v = v.rearrange("p (a b) -> p a b", a=shape[0])
            if len(shape) == 3:
                v = v.rearrange("p (a b c) -> p a b c", a=shape[0], b=shape[1])
            return v

        v.Qst = [carve([J, T], bf16, reset=i == 0) for i in range(SLOTS)]
        v.Kst = [carve([J, TK], bf16) for _ in range(SLOTS)]
        v.ring = [carve([512], fp32) for _ in range(RING)]
        v.Osb = carve([T], fp32)
        v.Hb = [carve([NT, C], fp32, reset=i == 0) for i in range(2)]
        v.hT = [carve([T], fp32) for _ in range(2)]
        v.QF = carve([T], fp32)
        v.KF = carve([TK], fp32)
        v.QR = carve([T], fp32)
        v.KR = carve([TK], fp32)
        v.Qp = [carve([PARTS, T], bf16) for _ in range(2)]
        v.Kp = [carve([PARTS, TK], bf16) for _ in range(2)]
        shared_at = place[0]
        v.Ab = [carve([NT, C], fp32) for _ in range(2)]
        v.aT = carve([T], fp32)
        place[0] = shared_at
        v.KT = carve([NT, C], fp32)
        v.wx = carve([NT, C], fp32)
        v.Aw = carve([NT, P], fp32)
        v.wt = carve([B * NT], fp32)
        v.products = v.QR.rearrange("p (t c) -> p t c", t=NT)
        v.sm, v.wT, v.sm2, v.lg = (v.QF[:, a:a + n] for a, n in (
            (0, P), (P, P), (2 * P, 16), (3 * P, B * NT)))
        v.wload = v.Hb[0][:, 0:3, :]
        v.wpload = v.Hb[0][:, 3, :]
        v.b1rows = v.Hb[0][:, 4, :]
        v.H3T = carve([B * T], fp32, reset=True)
        gate_at = place[0]
        v.GL = carve([6, B * NT * E], fp32).rearrange("p k (t e) -> p k t e", e=E)
        v.ewT = [carve([NT, P], fp32) for _ in range(2)]
        v.hT2 = [carve([T], fp32) for _ in range(2)]
        v.aT2 = carve([T], fp32)
        v.Hb2 = [carve([NT, C], fp32) for _ in range(2)]
        v.Ab2 = [carve([NT, C], fp32) for _ in range(2)]
        v.red = carve([7, B * NT], fp32)
        place[0] = gate_at
        v.hid = [carve([512], fp32) for _ in range(2 * FC)]

        v.experts_loaded = sem("experts_loaded")
        v.x_loaded = [sem(f"x_loaded{b}") for b in range(B)]
        v.first = {n: sem(f"x_{n}") for n in ("stats", "mv", "aggr")}
        load_all(nc, A, v)
        project(nc, 1, v)
        attend(nc, 1, v)
        project(nc, 2, v)
        attend(nc, 2, v)
        gate(nc, v)
        experts(nc, v, out)


def load_all(nc, A, v):
    loaded, const_set, turned, w_out = v.sem("loaded"), v.sem("const_set"), v.sem("turned"), v.sem("w_out")
    jobs = [
        (v.ident[:, :], A["c_ident"]),
        (v.wload, A["L0_attn_w_attn"].rearrange("(a p) c -> p a c", p=P)),
        (v.wpload, A["L0_attn_w_proj"]),
        (v.qtab[:, :], A["c_qtab"]), (v.ktab[:, :], A["c_ktab"]), (v.ctab[:, :], A["c_ctab"]),
        (v.ind[:, :], A["c_ind"]),
        (v.bcol[:, 0:1], A["L0_attn_b_attn"][0:C].rearrange("(p o) -> p o", o=1)),
        (v.bcol[:, 1:2], A["L0_attn_b_attn"][C:2 * C].rearrange("(p o) -> p o", o=1)),
        (v.bcol[:, 2:3], A["L0_ffn_b_qkv"][0:C].rearrange("(p o) -> p o", o=1)),
        (v.bcol[:, 3:4], A["L0_ffn_b_qkv"][C:2 * C].rearrange("(p o) -> p o", o=1)),
        *[(v.gbcol[:, k:k + 1], A[n].rearrange("(p o) -> p o", o=1))
          for k, n in enumerate(("L0_ffn_ln1_g", "L0_ffn_ln1_b", "L0_ffn_ln2_g", "L0_ffn_ln2_b"))],
        (v.AO[:, 0:4, :, :].rearrange("p u t n -> p (u t n)"), A["c_mask_q"]),
        (v.AO[:, 4:8, :, :].rearrange("p u t n -> p (u t n)"), A["c_mask_k"]),
        (v.wqkv2[:, :], A["L0_ffn_w_qkv"]), (v.wo2[:, :], A["L0_ffn_w_o"]),
        (v.gw[:, :], A["L0_ffn_gate_w"]), (v.iota[:, :], A["c_iota"]),
        (v.b2r[:, :], A["L0_ffn_b2"]),
        (v.b1rows[0:E * FC, :], A["L0_ffn_b1"].rearrange("e (f p) -> (e f) p", p=P)),
        (v.gbrow[:, :], A["L0_ffn_gate_b"].partition_broadcast(P)),
    ]
    rows = {v.BK1: A["L0_attn_b_attn"][C:2 * C], v.BV1: A["L0_attn_b_attn"][2 * C:3 * C],
            v.BP1: A["L0_attn_b_proj"], v.BV2: A["L0_ffn_b_qkv"][2 * C:3 * C], v.BO2: A["L0_ffn_b_o"]}
    jobs += [(v.brow[:, k, :], r.partition_broadcast(P)) for k, r in rows.items()]
    jobs += [(v.wx[16 * k:16 * k + 16, :, :],
              A["L0_attn_w_assign"].rearrange("(t k) c -> k t c", k=NCL // NT)[k].partition_broadcast(NTPC))
             for k in range(NCL // NT)]
    experts_in = [(v.W1[:, :, :], A["L0_ffn_W1"].rearrange("e p f -> p e f")),
             (v.W2[:, :, :, :].rearrange("p e f c -> p (e f) c"),
              A["L0_ffn_W2"].rearrange("e (f p) c -> p (e f) c", p=P))]

    with nc.Block() as block:
        @block.sync
        def _(sp):
            for b in range(B):
                sp.dma_start(v.X[:, b, :, :], A["L0_attn_x"][b].rearrange("(t p) c -> p t c", p=P))\
                  .then_inc(v.x_loaded[b], 16)
            for dst, src in jobs[0::2]:
                sp.dma_start(dst, src).then_inc(loaded, 16)
            for dst, src in experts_in:
                sp.dma_start(dst, src).then_inc(v.experts_loaded, 16)
            sp.wait_ge(loaded, 16 * len(jobs))

        @block.scalar
        def _(act):
            for dst, src in jobs[1::2]:
                act.dma_start(dst, src).then_inc(loaded, 16)

        @block.vector
        def _(dve):
            dve.memset(v.eps[:, :], EPS)
            for b in range(B):
                dve.wait_ge(v.x_loaded[b], 16)
                row_stats(dve, v, v.first, b, lambda t: v.X[:, b, t, :], None, None, b)
            for m in v.Mpart:
                dve.memset(m[:, :, :, :], 0.0)
            dve.wait_ge(loaded, 16 * len(jobs))
            dve.tensor_copy(v.identb[:, :], v.ident[:, :])
            for m, u in ((v.mask_q, 0), (v.mask_k, 4)):
                dve.tensor_copy(m[:, :, :].rearrange("p t n -> p (t n)"),
                                v.AO[:, u:u + 4, :, :].rearrange("p u t n -> p (u t n)"))
            dve.memset(v.ps[:, :, :], 0.0).then_inc(const_set, 1)
            dve.wait_ge(turned, 1)
            dve.tensor_copy(v.wqkvT[:, :], v.ps[:, 0, 0:3 * C])
            dve.tensor_copy(v.b1T[:, :, :].rearrange("p e f -> p (e f)"), v.ps[:, 1, 0:E * FC])
            dve.tensor_copy(v.wprojT[:, :], v.ps[:, 0, 3 * C:4 * C]).then_inc(w_out, 1)

        @block.gpsimd
        def _(pool):
            for i in range(SLOTS):
                pool.memset(v.Vu[i][:, :, :, :, :], 1.0)
            pool.memset(v.rden[:, :, :], 1.0).then_inc(const_set, 1)

        @block.tensor
        def _(pe):
            pe.wait_ge(loaded, 16 * len(jobs))
            pe.wait_ge(const_set, 2)
            for a in range(3):
                pe.transpose(v.ps[:, 0, a * C:a * C + C], v.wload[:, a, :], v.ident[:, :])
            pe.transpose(v.ps[:, 1, 0:E * FC], v.b1rows[0:E * FC, :], v.ident[0:E * FC, 0:E * FC])
            pe.transpose(v.ps[:, 0, 3 * C:4 * C], v.wpload, v.ident[:, :]).then_inc(turned, 1)


def row_stats(dve, v, S, b, src, written, value, count):
    if written is not None:
        settled(dve, v, written, value)
    for t in range(NT):
        last = dve.bn_stats(v.stat[:, t, :], src(t))
    last.then_inc(S["stats"], 1)
    settled(dve, v, S["stats"], count + 1)
    for t in range(NT):
        last = dve.bn_aggr(v.mv[:, t, :], v.stat[:, t, :])
    last.then_inc(S["mv"], 1)
    dve.wait_ge(S["mv"], count + 1)
    dve.tensor_copy(v.mv_all[:, bass.ts(b, NT), :], v.mv[:, :, :]).then_inc(S["aggr"], 1)


def over(ap, n, axis=1):
    a = ap.unsqueeze(axis)
    s = list(a.shape)
    s[axis] = n
    return a.broadcast_to(s)


def heads_last(VT, b):
    return VT[:, bass.ts(b, HG), :, :].rearrange("p g t n -> p t g n")


def apply_norm(act, v, src, dst, b):
    for t in range(NT):
        last = act.activation(dst(t), src(t), ACT.Identity, bias=v.shift_all[:, bass.ds(b * NT + t, 1)],
                              scale=v.rstd_all[:, bass.ds(b * NT + t, 1)])
    return last


def roots(act, v, S, rows):
    act.wait_ge(S["aggr"], rows)
    act.activation(v.std_all[:, :], v.mv_all[:, :, 1], ACT.Sqrt, bias=v.eps[:, 0:1]).then_inc(S["root"], 1)


def inverses(dve, v, S, n):
    dve.wait_ge(S["root"], n)
    dve.reciprocal(v.rstd_all[:, :], v.std_all[:, :]).then_inc(S["inv"], 1)
    dve.wait_ge(S["inv"], n)
    dve.scalar_tensor_tensor(v.shift_all[:, :], v.mv_all[:, :, 0], -1.0, v.rstd_all[:, :], ALU.mult, ALU.mult)\
       .then_inc(S["shift"], 1)


def project(nc, stage, v):
    S = {}

    def new(*ns):
        for n in ns:
            S[n] = v.sem(f"p{stage}_{n}")

    new("root", "inv", "shift", "copied", "turned", "hT", "q_ps", "k_ps", "v_ps", "qf", "kf",
        "vt", "q1", "q2", "k1", "k2", "qr", "kr", "q3", "k3", "stored0", "stored1")
    if stage == 1:
        S.update(v.first)
        new("norm", "xw", "lg", "lgT", "mx", "shifted", "ex", "sums", "winv", "wT", "wback", "wt", "aw", "ck", "kfc", "kc")
    else:
        new("stats", "mv", "aggr", "gather", "aturned", "aT", "y_ps", "y", "normed_y", "x1", "normed_x")
    stored = [S["stored0"], S["stored1"]]
    w = v.wqkvT if stage == 1 else v.wqkv2
    NK = TK if stage == 1 else T
    ALL = B * NT
    qd, kd = v.q_dram[stage - 1], v.k_dram[stage - 1]
    bank = lambda i, n=2: v.ps[:, i:i + n, :].rearrange("p a n -> p (a n)")
    KF, KR = v.KF[:, 0:T], v.KR[:, 0:T]
    clusters = [p[:, :, T:TK] for p in v.Kp]
    DMAS = 3 * PARTS - 1

    def pairs(eng, body):
        with eng.Fori(0, B // 2) as i:
            for par in range(2):
                body(i * 2 + par, i, par)

    with nc.Block() as block:
        @block.vector
        def _(dve):
            for n in ("qf", "kf", "vt") + (("kfc", "ck", "lg") if stage == 1 else ()):
                dve.sem_inc(S[n], 1)
            if stage == 2:
                dve.sem_inc(S["y"], 1)
            if stage == 1:
                inverses(dve, v, S, 1)
                with dve.Fori(0, B) as b:
                    dve.wait_ge(S["norm"], b + 1)
                    dve.wait_ge(S["lg"], b + 1)
                    dve.tensor_tensor(v.products, v.XX[:, b, :, :], v.wx, ALU.mult).then_inc(S["xw"], 1)
                    dve.wait_ge(S["xw"], b + 1)
                    dve.tensor_reduce(v.lg[:, bass.ts(b, NT)], v.products, AX.X, ALU.add).then_inc(S["lg"], 1)
                dve.wait_ge(S["lgT"], 1)
                lgT = v.ps[0:ALL, 6, 0:P].rearrange("p (k s) -> p k s", s=NTPC)
                dve.tensor_reduce(v.sm2[0:ALL, 0:8], lgT, AX.X, ALU.max).then_inc(S["mx"], 1)
                dve.wait_ge(S["mx"], 1)
                smv = v.sm[0:ALL, :].rearrange("p (k s) -> p k s", s=NTPC)
                dve.tensor_tensor(smv, lgT, over(v.sm2[0:ALL, 0:8], NTPC, 2), ALU.subtract).then_inc(S["shifted"], 1)
                dve.wait_ge(S["ex"], 1)
                wTv = v.wT[0:ALL, :].rearrange("p (k s) -> p k s", s=NTPC)
                dve.tensor_reduce(v.sm2[0:ALL, 8:16], wTv, AX.X, ALU.add).then_inc(S["sums"], 1)
                dve.wait_ge(S["sums"], 1)
                dve.reciprocal(v.sm2[0:ALL, 0:8], v.sm2[0:ALL, 8:16]).then_inc(S["winv"], 1)
                dve.wait_ge(S["winv"], 1)
                dve.tensor_tensor(smv, wTv, over(v.sm2[0:ALL, 0:8], NTPC, 2), ALU.mult).then_inc(S["wT"], 1)
                dve.wait_ge(S["wback"], 1)
                dve.tensor_copy(v.wt[:, :], v.ps[:, 6, P:P + ALL]).then_inc(S["wt"], 1)
                dve.wait_ge(S["wt"], 1)
            else:
                with dve.Fori(0, B) as b:
                    dve.wait_ge(S["y_ps"], b + 1)
                    dve.tensor_tensor(v.XX[:, b, :, :], bank(2).rearrange("p (t c) -> p t c", t=NT),
                                      over(v.brow[:, v.BP1, :], NT), ALU.add).then_inc(S["y"], 1)
                    row_stats(dve, v, S, b, lambda t: v.XX[:, b, t, :], S["y"], b + 2, b)
                inverses(dve, v, S, 1)
                with dve.Fori(0, B) as b:
                    dve.wait_ge(S["normed_y"], b + 1)
                    dve.tensor_tensor(v.X[:, b, :, :], v.X[:, b, :, :], v.XX[:, b, :, :], ALU.add)\
                       .then_inc(S["x1"], 1)
                    row_stats(dve, v, S, b, lambda t: v.X[:, b, t, :], S["x1"], b + 1, b + B)
                inverses(dve, v, S, 2)
                with dve.Fori(0, B) as b:
                    row_stats(dve, v, S, b, lambda t: v.XX[:, b, t, :], S["normed_x"], b + 1, b + 2 * B)
                inverses(dve, v, S, 3)
                dve.wait_ge(S["shift"], 3)

            def body(b, i, par):
                if stage == 2:
                    dve.wait_ge(S["turned"], b * 2 + 2)
                    for t in range(NT):
                        last = dve.tensor_scalar(v.Hb[par][:, t, :], v.XX[:, b, t, :],
                                                 v.mv_all[:, bass.ds(b * NT + t, 1), 0],
                                                 v.rstd_all[:, bass.ds(b * NT + t, 1)], ALU.subtract, ALU.mult)
                    last.then_inc(S["copied"], 1)
                dve.wait_ge(S["q_ps"], b + 1)
                dve.wait_ge(S["q1"], b + 1)
                dve.wait_ge(S["qr"], b + 1)
                if stage == 1:
                    dve.scalar_tensor_tensor(v.QF.rearrange("p (g s) -> p g s", s=GS),
                                             bank(6).rearrange("p (g s) -> p g s", s=GS), v.bcol[:, 0:1],
                                             over(v.qtab[:, :], T // GS), ALU.add, ALU.mult).then_inc(S["qf"], 1)
                else:
                    dve.tensor_scalar(v.QF, bank(6), v.bcol[:, 2:3], None, ALU.add).then_inc(S["qf"], 1)
                dve.wait_ge(S["k_ps"], b + 1)
                dve.wait_ge(S["k1"], b + 1)
                dve.wait_ge(S["kr"], b + 1)
                if stage == 1:
                    dve.scalar_tensor_tensor(KF, bank(0), v.bcol[:, 1:2], v.ktab[:, :],
                                             ALU.add, ALU.mult).then_inc(S["kf"], 1)
                else:
                    dve.tensor_scalar(KF, bank(0), v.bcol[:, 3:4], None, ALU.add).then_inc(S["kf"], 1)
                if stage == 2:
                    dve.wait_ge(S["v_ps"], b + 1)
                    dve.tensor_tensor(heads_last(v.VT, b), bank(2).rearrange("p (t g n) -> p t g n", t=NT, g=HG),
                                      over(v.brow[:, v.BV2, :].rearrange("p (g n) -> p g n", g=HG), NT),
                                      ALU.add).then_inc(S["vt"], 1)
                    return
                dve.wait_ge(S["ck"], b + 1)
                for t in range(NT):
                    at = NCL - 8 - 8 * t
                    last = dve.tensor_scalar(v.Aw[:, t, :].rearrange("p (a c) -> p a c", a=2),
                                             over(v.ind[:, at:at + NCL], 2), v.wt[:, bass.ds(b * NT + t, 1)], None,
                                             ALU.mult)
                last.then_inc(S["aw"], 1)
                dve.wait_ge(S["v_ps"], b + 1)
                kv = bank(2, 4).rearrange("p (t n) -> p t n", t=NT)
                dve.tensor_tensor(v.KT, kv[:, :, 0:C], over(v.brow[:, v.BK1, :], NT), ALU.add)
                dve.tensor_tensor(heads_last(v.VT, b), kv[:, :, C:2 * C].rearrange("p t (g n) -> p t g n", g=HG),
                                  over(v.brow[:, v.BV1, :].rearrange("p (g n) -> p g n", g=HG), NT),
                                  ALU.add).then_inc(S["vt"], 1)
                dve.wait_ge(S["ck"], b + 2)
                dve.tensor_tensor(v.KF[:, T:TK], v.ps[:, 7, 0:NCL], v.ctab[:, :], ALU.mult).then_inc(S["kc"], 1)
                dve.tensor_copy(v.CV[:, bass.ts(b, HG), :], v.ps[:, 7, P:2 * P].rearrange("p (g n) -> p g n", g=HG))\
                   .then_inc(S["kfc"], 1)
                dve.wait_ge(stored[par], i * (16 * DMAS) + 16 * DMAS)
                dve.wait_ge(S["kc"], b * 4 + 1)
                kf, kr, parts = v.KF[:, T:TK], v.KR[:, T:TK], clusters[par]
                dve.tensor_copy(parts[:, 0, :], kf).then_inc(S["kc"], 1)
                dve.wait_ge(S["kc"], b * 4 + 2)
                dve.tensor_tensor(kr, kf, parts[:, 0, :], ALU.subtract).then_inc(S["kc"], 1)
                dve.wait_ge(S["kc"], b * 4 + 3)
                dve.tensor_copy(parts[:, 1, :], kr).then_inc(S["kc"], 1)
                dve.wait_ge(S["kc"], b * 4 + 4)
                dve.tensor_tensor(parts[:, 2, :], kr, parts[:, 1, :], ALU.subtract).then_inc(S["k3"], 1)
            pairs(dve, body)

        @block.scalar
        def _(act):
            for n in ("q1", "k1"):
                act.sem_inc(S[n], 1)
            if stage == 1:
                roots(act, v, S, B)
                act.wait_ge(S["shift"], 1)
                with act.Fori(0, B) as b:
                    apply_norm(act, v, lambda t: v.X[:, b, t, :], lambda t: v.XX[:, b, t, :], b)\
                        .then_inc(S["norm"], 1)
                act.wait_ge(S["shifted"], 1)
                act.activation(v.wT[0:ALL, :], v.sm[0:ALL, :], ACT.Exp).then_inc(S["ex"], 1)
            else:
                with act.Fori(0, B) as b:
                    for n in range(2):
                        act.wait_ge(S["aturned"], b * 2 + (5 + n))
                        act.activation(v.aT[:, n * HALF:(n + 1) * HALF], v.ps[:, n, :], ACT.Copy)\
                            .then_inc(S["aT"], 1)
                roots(act, v, S, B)
                act.wait_ge(S["shift"], 1)
                with act.Fori(0, B) as b:
                    apply_norm(act, v, lambda t: v.XX[:, b, t, :], lambda t: v.XX[:, b, t, :], b)\
                        .then_inc(S["normed_y"], 1)
                roots(act, v, S, 2 * B)
                act.wait_ge(S["shift"], 2)
                with act.Fori(0, B) as b:
                    apply_norm(act, v, lambda t: v.X[:, b, t, :], lambda t: v.XX[:, b, t, :], b)\
                        .then_inc(S["normed_x"], 1)
                roots(act, v, S, 3 * B)

            def body(b, i, par):
                for n in range(2):
                    act.wait_ge(S["turned"], b * 2 + (5 + n))
                    if stage == 1:
                        act.activation(v.hT[par][:, n * HALF:(n + 1) * HALF], v.ps[:, 4 + n, :], ACT.Copy)\
                            .then_inc(S["hT"], 1)
                    else:
                        act.activation(v.hT[par][:, n * HALF:(n + 1) * HALF], v.ps[:, 4 + n, :], ACT.Identity,
                                       bias=v.gbcol[:, 1:2], scale=v.gbcol[:, 0:1]).then_inc(S["hT"], 1)
                act.wait_ge(S["qf"], b + 2)
                act.wait_ge(stored[par], i * (16 * DMAS) + 16 * DMAS)
                act.activation(v.Qp[par][:, 0, :], v.QF, ACT.Copy).then_inc(S["q1"], 1)
                act.wait_ge(S["kf"], b + 2)
                act.activation(v.Kp[par][:, 0, 0:T], KF, ACT.Copy).then_inc(S["k1"], 1)
                act.wait_ge(S["qr"], b + 2)
                act.activation(v.Qp[par][:, 1, :], v.QR, ACT.Copy).then_inc(S["q2"], 1)
                act.wait_ge(S["kr"], b + 2)
                act.activation(v.Kp[par][:, 1, 0:T], KR, ACT.Copy).then_inc(S["k2"], 1)
            pairs(act, body)

        @block.gpsimd
        def _(pool):
            for n in ("qr", "q3", "kr", "k3"):
                pool.sem_inc(S[n], 1)
            if stage == 2:
                def gather(b, i, par):
                    pool.wait_ge(S["aturned"], b * 2 + 2)
                    for g in range(HG):
                        last = pool.tensor_copy(v.Ab[par][:, :, g * J * D:(g + 1) * J * D], v.AO[:, b * HG + g, :, :])
                    last.then_inc(S["gather"], 1)
                pairs(pool, gather)
            K3 = 2 if stage == 1 else 1

            def body(b, i, par):
                if stage == 1:
                    pool.wait_ge(S["norm"], b + 1)
                    pool.wait_ge(S["turned"], b * 2 + 2)
                    pool.tensor_copy(v.Hb[par], v.XX[:, b, :, :]).then_inc(S["copied"], 1)
                pool.wait_ge(S["q1"], b + 2)
                pool.wait_ge(S["q3"], b + 1)
                pool.tensor_tensor(v.QR, v.QF, v.Qp[par][:, 0, :], ALU.subtract).then_inc(S["qr"], 1)
                pool.wait_ge(S["k1"], b + 2)
                pool.wait_ge(S["k3"], b * K3 + 1)
                pool.tensor_tensor(KR, KF, v.Kp[par][:, 0, 0:T], ALU.subtract).then_inc(S["kr"], 1)
                pool.wait_ge(S["q2"], b + 1)
                pool.tensor_tensor(v.Qp[par][:, 2, :], v.QR, v.Qp[par][:, 1, :], ALU.subtract).then_inc(S["q3"], 1)
                pool.wait_ge(S["k2"], b + 1)
                pool.tensor_tensor(v.Kp[par][:, 2, 0:T], KR, v.Kp[par][:, 1, 0:T], ALU.subtract).then_inc(S["k3"], 1)
            pairs(pool, body)

        @block.sync
        def _(sp):
            for s in stored:
                sp.sem_inc(s, 16 * DMAS)

            def body(b, i, par):
                sp.wait_ge(S["q3"], b + 2)
                qrow = qd[b].rearrange("h (a d) n -> a h d n", a=PARTS)
                for a in range(PARTS):
                    sp.dma_start(qrow[a], v.Qp[par][:, a, :]).then_inc(stored[par], 16)
                sp.wait_ge(S["k3"], b * 2 + 3 if stage == 1 else b + 2)
                krow = kd[b].rearrange("h (a d) n -> a h d n", a=2 * PARTS - 1)
                for a in range(2 * PARTS - 1):
                    sp.dma_start(krow[a][:, :, 0:NK], v.Kp[par][:, a % PARTS, 0:NK]).then_inc(stored[par], 16)
            pairs(sp, body)
            for s in stored:
                sp.wait_ge(s, 16 * DMAS * (B // 2 + 1))

        @block.tensor
        def _(pe):
            pe.sem_inc(S["turned"], 4)
            if stage == 2:
                pe.sem_inc(S["aturned"], 4)

                def output(b, i, par):
                    pe.wait_ge(S["gather"], b + 1)
                    for n in range(2):
                        for t in range(n * NT // 2, (n + 1) * NT // 2):
                            last = pe.transpose(v.ps[:, n, t % 4 * C:t % 4 * C + C], v.Ab[par][:, t, :], v.ident[:, :])
                        last.then_inc(S["aturned"], 1)
                    pe.wait_ge(S["y"], b + 1)
                    for n in range(2):
                        pe.wait_ge(S["aT"], b * 2 + (n + 1))
                        for t in range(n * NT // 2, (n + 1) * NT // 2):
                            last = pe.matmul(v.ps[:, 2 + n, t % 4 * C:t % 4 * C + C],
                                             v.aT[:, t * P:t * P + P], v.wprojT[:, :], start=True, stop=True)
                    last.then_inc(S["y_ps"], 1)
                pairs(pe, output)
                pe.wait_ge(S["y"], B + 1)
            else:
                pe.wait_ge(S["lg"], B + 1)
                pe.transpose(v.ps[0:ALL, 6, 0:P], v.lg[:, :], v.ident[:, :]).then_inc(S["lgT"], 1)
                pe.wait_ge(S["wT"], 1)
                pe.transpose(v.ps[:, 6, P:P + ALL], v.sm[0:ALL, :], v.ident[0:ALL, 0:ALL]).then_inc(S["wback"], 1)
                pe.wait_ge(S["wt"], 1)

            def body(b, i, par):
                pe.wait_ge(S["copied"], b + 1)
                if stage == 1:
                    pe.wait_ge(S["vt"], b + 1)
                for n in range(2):
                    for t in range(n * NT // 2, (n + 1) * NT // 2):
                        last = pe.transpose(v.ps[:, 4 + n, t % 4 * C:t % 4 * C + C], v.Hb[par][:, t, :], v.ident[:, :])
                    last.then_inc(S["turned"], 1)
                pe.wait_ge(S["qf"], b + 1)
                if stage == 1:
                    pe.wait_ge(S["kfc"], b + 1)
                for n in range(2):
                    pe.wait_ge(S["hT"], b * 2 + (n + 1))
                    last = pe.matmul(v.ps[:, 6 + n, :], w[:, 0:C], v.hT[par][:, n * 512:n * 512 + 512],
                                     start=True, stop=True)
                last.then_inc(S["q_ps"], 1)
                pe.wait_ge(S["kf"], b + 1)
                for n in range(2):
                    last = pe.matmul(v.ps[:, n, :], w[:, C:2 * C], v.hT[par][:, n * 512:n * 512 + 512],
                                     start=True, stop=True)
                last.then_inc(S["k_ps"], 1)
                if stage == 2:
                    pe.wait_ge(S["vt"], b + 1)
                    for t in range(NT):
                        last = pe.matmul(v.ps[:, 2 + t // 4, t % 4 * C:t % 4 * C + C],
                                         v.hT[par][:, t * P:t * P + P], w[:, 2 * C:3 * C], start=True, stop=True)
                    last.then_inc(S["v_ps"], 1)
                    return
                for t in range(NT):
                    last = pe.matmul(v.ps[:, 2 + t // 2, t % 2 * 2 * C:t % 2 * 2 * C + 2 * C],
                                     v.hT[par][:, t * P:t * P + P], w[:, C:3 * C], start=True, stop=True)
                last.then_inc(S["v_ps"], 1)
                pe.wait_ge(S["aw"], b + 1)
                pe.wait_ge(S["vt"], b + 2)
                pe.wait_ge(S["qf"], b + 2)
                for t in range(NT):
                    pe.matmul(v.ps[:, 7, 0:NCL], v.KT[:, t, :], v.Aw[:, t, 0:NCL], start=t == 0, stop=t == NT - 1)
                for t in range(NT):
                    last = pe.matmul(v.ps[:, 7, P:2 * P], v.Aw[:, t, :], v.VT[:, bass.ts(b, HG), t, :],
                                     start=t == 0, stop=t == NT - 1)
                last.then_inc(S["ck"], 1)
            pairs(pe, body)


def attend(nc, stage, v):
    S = {n: v.sem(f"a{stage}_{n}") for n in (
        "s1_full", "s1_free", "split0", "split1", "split2", "split3", "s2_full", "exp_done", "av_done",
        "o_out", "inv", "vu", "stacked0", "stacked1", "stacked2", "rows0", "rows1", "first_ones", "ones")}
    if stage == 2:
        S["biased"] = v.sem("a2_biased")
    stacked = [S[f"stacked{i}"] for i in range(SLOTS)]
    rows = [S["rows0"], S["rows1"]]
    full = stage == 2
    PIECES = 16 if full else 4
    GROUPS = 8 if full else 4
    STEPS = 4 if full else 1
    NK = T if full else TK
    TH = NT // 2
    qd = v.q_dram[stage - 1].rearrange("b (g j) r n -> (b g) r j n", j=J)
    kd = v.k_dram[stage - 1].rearrange("b (g j) r n -> (b g) r j n", j=J)
    steps_unit = 2 * GROUPS * STEPS
    LOADS = 6

    def uses(first, last):
        out = []
        for h in range(2):
            for k in range(PIECES):
                if not last:
                    out.append(("piece", h, k))
                if h == 0 and k == (1 if full else 0):
                    out.append(("parts", 1, 0))
                if h == (0 if full else 1) and k == (PIECES // 2 + 1 if full else 1) and not first:
                    out += [("outs", 0, 0), ("outs", 1, 0)]
                if h == 1 and k == (1 if full else 0) and not last:
                    out.append(("parts", 0, 1))
        return out

    def schedule(first, last):
        us = uses(first, last)
        n = 2 * GROUPS
        if last:
            return [us[0:1], [], [], us[1:]] + [[] for _ in range(n - 4)]
        return [us[len(us) * g // n:len(us) * (g + 1) // n] for g in range(n)]

    def prologue_uses():
        rest = [("piece", 1, k) for k in range(PIECES)]
        return [("piece", 0, k) for k in range(PIECES)] + rest[:2] + [("parts", 0, 0)] + rest[2:]

    def bodies(eng, tallies, per, body):
        body(0, 0, True, False)
        with eng.Fori(0, LOOPS) as i:
            for t, n in zip(tallies, per):
                t.enter(i, n)
            for r in range(SLOTS):
                body(i * SLOTS + (r + 1), (r + 1) % SLOTS, False, False)
        for t in tallies:
            t.leave(LOOPS)
        for u in range(SLOTS * LOOPS + 1, UNITS):
            body(u, u % SLOTS, False, u == UNITS - 1)

    USES = len(uses(False, False))

    def segments(stack, j, r, a, b):
        one = stack[0:r, j, a:a + 64]
        return bass.AP(tensor=one.tensor, offset=one.offset, ap=[list(one.ap[0]), [b - a, 2], [1, 64]])

    with nc.Block() as block:
        @block.sync
        def _(sp):
            def load(u, slot):
                for c in range(PARTS):
                    sp.dma_start(v.Qst[slot][c * 24:c * 24 + 24, :, :], qd[u]).then_inc(stacked[slot], 16)
                    sp.dma_start(v.Kst[slot][c * 24:c * 24 + 24, :, 0:NK],
                                 kd[u][c * D:c * D + 24, :, 0:NK]).then_inc(stacked[slot], 16)

            def shift_rows(slot, h):
                n = PARTS * TH
                for j in range(J):
                    sp.dma_start(v.Qst[slot][ROWS:KROWS, j, h * HALF:(h + 1) * HALF].rearrange("p (t q) -> p t q", t=TH),
                                 v.MT[h][j * n:j * n + n, :]).then_inc(rows[h], 16)

            s1, s2 = Tally(), Tally()

            def follow(us, now, nxt):
                for kind, h, k in us:
                    s1.up()
                    if kind == "parts":
                        sp.wait_ge(S["s1_free"], s1.at())
                        shift_rows(now if h == 1 else nxt, h)

            sp.wait_ge(S["first_ones"], 1)
            load(0, 0)
            sp.wait_ge(S["ones"], 1)
            load(1, 1)
            sp.wait_ge(S["ones"], SLOTS - 1)
            follow(prologue_uses(), None, 0)

            def body(u, slot, first, last):
                if not (isinstance(u, int) and u + 2 >= UNITS):
                    if not first:
                        sp.wait_ge(S["s2_full"], s2.at())
                    load(u + 2, (slot + 2) % SLOTS)
                s2.up(steps_unit)
                follow(uses(first, last), slot, (slot + 1) % SLOTS)
            bodies(sp, [s1, s2], [USES * SLOTS, SLOTS * steps_unit], body)
            sp.wait_ge(rows[0], 16 * J * UNITS)
            sp.wait_ge(rows[1], 16 * J * UNITS)

        @block.gpsimd
        def _(pool):
            for i in range(1, SLOTS):
                pool.memset(v.Kst[i][64:96, :, :], 1.0).then_inc(S["ones"], 1)
            pool.wait_ge(S["ones"], SLOTS - 1)
            if full:
                with pool.Fori(0, B) as b:
                    pool.tensor_tensor(v.XX[:, b, :, :], v.XX[:, b, :, :], over(v.brow[:, v.BO2, :], NT), ALU.add)\
                        .then_inc(S["biased"], 1)
                pool.wait_ge(S["biased"], B)
            av = Tally()

            def body(u, slot, first, last):
                out = v.Vu[slot]
                if not (isinstance(u, int) and u < SLOTS):
                    pool.wait_ge(S["av_done"], av.at(-(SLOTS - 1) * 2 * GROUPS))
                av.up(2 * GROUPS)
                if full:
                    pool.tensor_copy(out[:, :, 0, :, 0:D], v.VT[:, u, :, :].rearrange("p t (j d) -> p t j d", j=J))\
                        .then_inc(S["vu"], 1)
                    return
                for s, lo, cl in ((0, 0, 64), (1, 64, 0)):
                    pool.tensor_copy(out[lo:lo + 64, :, s, :, 0:D],
                                     v.VT[lo:lo + 64, u, :, :].rearrange("p t (j d) -> p t j d", j=J))
                    last_one = pool.tensor_copy(out[cl:cl + 64, :, s, :, 0:D],
                                                over(v.CV[cl:cl + 64, u, :].rearrange("p (j d) -> p j d", j=J), NT))
                last_one.then_inc(S["vu"], 1)
            for u in range(SLOTS):
                body(u, u, u == 0, False)
            with pool.Fori(0, LOOPS) as i:
                av.enter(i, 2 * GROUPS * SLOTS)
                for r in range(SLOTS):
                    body(i * SLOTS + (r + SLOTS), r, False, False)
            av.leave(LOOPS)
            body(UNITS - 1, (UNITS - 1) % SLOTS, False, True)

        @block.vector
        def _(dve):
            s1, spl, inv = Tally(), Tally(), Tally()
            taken = [Tally(), Tally()]
            dve.memset(v.Kst[0][64:96, :, :], 1.0).then_inc(S["first_ones"], 1)
            dve.sem_inc(S["inv"], 1)
            inv.up()

            def use(kind, h, k, u):
                at = s1.index() % 2
                s1.up()
                dve.wait_ge(S["s1_full"], s1.at())
                banks = v.ps[:, 2 * at:2 * at + 2, :].rearrange("p a n -> p (a n)")
                if kind == "piece":
                    if k == 0:
                        if spl.base is not None or spl.n:
                            dve.wait_ge(S["split3"], spl.at())
                    if full:
                        j, t = k % J, k // J
                        ins = dve.tensor_reduce(v.Mneg[h][:, j, t:t + 1], banks, AX.X, ALU.max, negate=True)
                    else:
                        ins = dve.tensor_reduce(v.Mneg[h][:, :, k], banks[:, 0:512].rearrange("p (j n) -> p j n", j=J),
                                                AX.X, ALU.max, negate=True)
                    ins.then_inc(S["s1_free"], 1)
                    if k == PIECES - 1:
                        dve.wait_ge(S["s1_free"], s1.at())
                        m, r, p = v.Mneg[h][:, :, :], v.Mres[h][:, :, :], v.Mpart[h][:, 0:J, :, :]
                        dve.tensor_copy(p[:, :, 0, :], m).then_inc(S["split0"], 1)
                        dve.wait_ge(S["split0"], spl.at(1))
                        dve.tensor_tensor(r, m, p[:, :, 0, :], ALU.subtract).then_inc(S["split1"], 1)
                        dve.wait_ge(S["split1"], spl.at(1))
                        dve.tensor_copy(p[:, :, 1, :], r).then_inc(S["split2"], 1)
                        dve.wait_ge(S["split2"], spl.at(1))
                        dve.tensor_tensor(p[:, :, 2, :], r, p[:, :, 1, :], ALU.subtract).then_inc(S["split3"], 1)
                        spl.up()
                elif kind == "parts":
                    if taken[h].base is not None or taken[h].n:
                        dve.wait_ge(rows[h], taken[h].at())
                    taken[h].up(16 * J)
                    dve.tensor_copy(v.MT[h][:, :], banks[0:2 * J * PARTS * TH, 0:P // 2].bitcast(bf16))\
                       .then_inc(S["s1_free"], 1)
                else:
                    o = banks[:, 0:512].rearrange("p (t j n) -> p t j n", t=TH, j=J)
                    dve.wait_ge(S["s1_free"], s1.at(-1))
                    dve.reciprocal(v.rden[:, :, :], o[:, :, :, D]).then_inc(S["inv"], 1)
                    inv.up()
                    dve.wait_ge(S["inv"], inv.at())
                    dst = v.AO[:, u - 1, h * TH:(h + 1) * TH, :].rearrange("p t (j d) -> p t j d", j=J)
                    dve.tensor_tensor(dst, o[:, :, :, 0:D], over(v.rden[:, :, :], D, 3), ALU.mult)\
                       .then_inc(S["s1_free"], 1)

            for kind, h, k in prologue_uses():
                use(kind, h, k, 0)

            def body(u, slot, first, last):
                for kind, h, k in uses(first, last):
                    use(kind, h, k, u)
            bodies(dve, [s1, spl, inv] + taken,
                   [USES * SLOTS, 2 * SLOTS, 2 * SLOTS, 16 * J * SLOTS, 16 * J * SLOTS], body)
            for h in range(2):
                use("outs", h, 0, UNITS)

        @block.scalar
        def _(act):
            s2, done, outs = Tally(), Tally(), Tally()
            lag = RING // STEPS

            def body(u, slot, first, last):
                for g in range(2 * GROUPS):
                    for s in range(STEPS):
                        n = s2.index()
                        s2.up()
                        act.wait_ge(S["s2_full"], s2.at())
                        if s == 0 and not (first and g < lag):
                            act.wait_ge(S["av_done"], done.at(1 - lag))
                        act.activation(v.ring[n % RING], v.ps[:, 4 + n % 2, :], ACT.Exp, scale=SCALE)\
                           .then_inc(S["exp_done"], 1)
                    done.up()
                    if g == 1 and not first:
                        act.wait_ge(S["av_done"], done.at(-2))
                        act.wait_ge(S["inv"], outs.at(1))
                        act.activation(v.Osb[:, HALF:T], v.ps[:, 7, :], ACT.Copy).then_inc(S["o_out"], 1)
                    if g == GROUPS + 1:
                        act.wait_ge(S["av_done"], done.at(-2))
                        if not first:
                            act.wait_ge(S["inv"], outs.at(2))
                            outs.up(2)
                        act.activation(v.Osb[:, 0:HALF], v.ps[:, 6, :], ACT.Copy).then_inc(S["o_out"], 1)
            bodies(act, [s2, done, outs], [SLOTS * steps_unit, SLOTS * 2 * GROUPS, 2 * SLOTS], body)
            act.wait_ge(S["av_done"], done.at())
            act.wait_ge(S["inv"], outs.at(1))
            act.activation(v.Osb[:, HALF:T], v.ps[:, 7, :], ACT.Copy).then_inc(S["o_out"], 1)

        @block.tensor
        def _(pe):
            s1, s2, spl, outs, rws, vu, oc = (Tally() for _ in range(7))
            stk = [Tally() for _ in range(SLOTS)]

            def use(kind, h, k, slot):
                at = s1.index() % 2
                if s1.base is not None or s1.n >= 2:
                    pe.wait_ge(S["s1_free"], s1.at(-1))
                s1.up()
                banks = v.ps[:, 2 * at:2 * at + 2, :]
                if kind == "piece" and full:
                    j, t = k % J, k // J
                    for n in range(2):
                        last = pe.matmul(banks[:, n, :], v.Qst[slot][0:ROWS, j, h * HALF + t * P:h * HALF + t * P + P],
                                         v.Kst[slot][0:ROWS, j, n * 512:n * 512 + 512], start=True, stop=True)
                elif kind == "piece":
                    t = h * TH + k
                    pe.matmul(banks[:, 0, :], v.identb[:, :], over(v.mask_q[:, t, :], J), start=True, stop=False,
                              skip_group_check=True)
                    for j in range(J):
                        for s in range(2):
                            q0 = t * P + 64 * s
                            last = pe.matmul(banks[64 * s:64 * s + 64, 0, j * P:j * P + P],
                                             v.Qst[slot][0:ROWS, j, q0:q0 + 64],
                                             segments(v.Kst[slot], j, ROWS, q0, T), start=False, stop=True,
                                             skip_group_check=True)
                elif kind == "parts":
                    spl.up()
                    pe.wait_ge(S["split3"], spl.at())
                    last = pe.transpose(banks[0:2 * J * PARTS * TH, 0, 0:P // 2].bitcast(bf16),
                                        v.Mpart[h][:, :, :, :].rearrange("p j a t -> p (j a t)"), v.identb[:, :])
                else:
                    outs.up()
                    pe.wait_ge(S["o_out"], outs.at())
                    for t in range(TH):
                        q0 = h * HALF + t * P
                        last = pe.transpose(banks[:, 0, t * P:t * P + P], v.Osb[:, q0:q0 + P], v.ident[:, :])
                last.then_inc(S["s1_full"], 1)

            def scores(g, s, slot):
                n = s2.index()
                if s2.base is not None or s2.n >= 2:
                    pe.wait_ge(S["exp_done"], s2.at(-1))
                s2.up()
                o = v.ps[:, 4 + n % 2, :]
                if full:
                    h, kt = g // GROUPS, g % GROUPS
                    last = pe.matmul(o, v.Kst[slot][0:KROWS, s, kt * P:kt * P + P],
                                     v.Qst[slot][0:KROWS, s, h * HALF:(h + 1) * HALF], start=True, stop=True)
                else:
                    pe.matmul(o, v.identb[:, :], over(v.mask_k[:, g, :].rearrange("p (s q) -> p s q", s=2), J, 2),
                              start=True, stop=False, skip_group_check=True)
                    for hs in range(2):
                        q0 = g * P + 64 * hs
                        for j in range(J):
                            c = (hs * J + j) * 64
                            for p0, k0 in ((64 * hs, q0), (64 - 64 * hs, T)):
                                last = pe.matmul(o[p0:p0 + 64, c:c + 64], v.Kst[slot][0:KROWS, j, k0:k0 + 64],
                                                 v.Qst[slot][0:KROWS, j, q0:q0 + 64], start=False, stop=True,
                                                 skip_group_check=True)
                last.then_inc(S["s2_full"], 1)

            def times_v(g, slot, n):
                h = g // GROUPS
                pe.wait_ge(S["exp_done"], n)
                if full:
                    kt = g % GROUPS
                    for j in range(J):
                        last = pe.matmul(v.ps[32 * j:32 * j + VW, 6 + h, :], v.Vu[slot][:, kt, 0, j, :],
                                         v.ring[(STEPS * g + j) % RING], start=kt == 0, stop=kt == GROUPS - 1)
                else:
                    for hs in range(2):
                        for j in range(J):
                            c = (hs * J + j) * 64
                            q0 = g % TH * P + 64 * hs
                            last = pe.matmul(v.ps[32 * j:32 * j + VW, 6 + h, q0:q0 + 64], v.Vu[slot][:, g, hs, j, :],
                                             v.ring[g % RING][:, c:c + 64], start=True, stop=True)
                last.then_inc(S["av_done"], 1)

            stk[0].up(16 * LOADS)
            pe.wait_ge(stacked[0], stk[0].at())
            for kind, h, k in prologue_uses():
                use(kind, h, k, 0)

            def body(u, slot, first, last):
                nxt = (slot + 1) % SLOTS
                if not last:
                    stk[nxt].up(16 * LOADS)
                    pe.wait_ge(stacked[nxt], stk[nxt].at())
                sched = schedule(first, last)
                rws.up(16 * J)
                vu.up()
                for g in range(2 * GROUPS):
                    if g % GROUPS == 0:
                        pe.wait_ge(rows[g // GROUPS], rws.at())
                    work = list(sched[g])
                    for s in range((STEPS + 1) // 2):
                        scores(g, s, slot)
                        if not full and work:
                            use(*work.pop(0), slot=nxt)
                        if full and s == 0 and len(work) > 2:
                            use(*work.pop(0), slot=nxt)
                    if g == 0 and not first:
                        times_v(2 * GROUPS - 1, (slot + 2) % SLOTS, s2.at(-((STEPS + 1) // 2)))
                    if g > 0:
                        if g == 1:
                            pe.wait_ge(S["vu"], vu.at())
                        if (g - 1) % GROUPS == 0 and not first:
                            pe.wait_ge(S["o_out"], oc.at(1 if g == 1 else 2))
                        times_v(g - 1, slot, s2.at(-((STEPS + 1) // 2)))
                    for s in range((STEPS + 1) // 2, STEPS):
                        scores(g, s, slot)
                    while work:
                        use(*work.pop(0), slot=nxt)
                if not first:
                    oc.up(2)
            bodies(pe, [s1, s2, spl, outs, rws, vu, oc] + stk,
                   [USES * SLOTS, SLOTS * steps_unit, 2 * SLOTS, 2 * SLOTS, 16 * J * SLOTS, SLOTS, 2 * SLOTS]
                   + [16 * LOADS] * SLOTS, body)
            times_v(2 * GROUPS - 1, (UNITS - 1) % SLOTS, s2.at())
            for h in range(2):
                use("outs", h, 0, 0)


def gate(nc, v):
    S = {n: v.sem(f"g_{n}") for n in (
        "gather", "aturned", "aT", "y_ps", "x2", "stats", "mv", "aggr", "root", "inv", "normed", "turned", "hT", "h3",
        "lg_ps", "chain", "delta", "ex", "ew", "ewturned", "ewT", "b2_ps", "x3")}
    bank = lambda i, n=2: v.ps[:, i:i + n, :].rearrange("p a n -> p (a n)")
    rowsof = lambda a: a.rearrange("p (t c) -> p t c", t=NT)
    ALL = B * NT
    turned_at = (4, 2)

    with nc.Block() as block:
        @block.gpsimd
        def _(pool):
            with pool.Fori(0, B // 2) as i:
                for par in range(2):
                    b = i * 2 + par
                    pool.wait_ge(S["aturned"], b * 2 + 2)
                    for g in range(HG):
                        last = pool.tensor_copy(v.Ab2[par][:, :, g * J * D:(g + 1) * J * D], v.AO[:, b * HG + g, :, :])
                    last.then_inc(S["gather"], 1)

        @block.tensor
        def _(pe):
            pe.sem_inc(S["aturned"], 4)
            pe.sem_inc(S["turned"], 4)
            pe.sem_inc(S["lg_ps"], 2)
            with pe.Fori(0, B // 2) as i:
                for par in range(2):
                    b = i * 2 + par
                    pe.wait_ge(S["gather"], b + 1)
                    for n in range(2):
                        for t in range(n * NT // 2, (n + 1) * NT // 2):
                            last = pe.transpose(v.ps[:, n, t % 4 * C:t % 4 * C + C], v.Ab2[par][:, t, :], v.ident[:, :])
                        last.then_inc(S["aturned"], 1)
                    pe.wait_ge(S["x2"], b + 1)
                    for n in range(2):
                        pe.wait_ge(S["aT"], b * 2 + (n + 1))
                        for t in range(n * NT // 2, (n + 1) * NT // 2):
                            last = pe.matmul(v.ps[:, 2 + n, t % 4 * C:t % 4 * C + C], v.aT2[:, t * P:t * P + P],
                                             v.wo2[:, :], start=True, stop=True)
                    last.then_inc(S["y_ps"], 1)
            pe.wait_ge(S["x2"], B + 1)
            with pe.Fori(0, B // 2) as i:
                for par in range(2):
                    b = i * 2 + par
                    pe.wait_ge(S["normed"], b + 3)
                    pe.wait_ge(S["h3"], b + 1)
                    for n in range(2):
                        for t in range(n * NT // 2, (n + 1) * NT // 2):
                            last = pe.transpose(v.ps[:, turned_at[par] + n, t % 4 * C:t % 4 * C + C],
                                                v.Hb2[par][:, t, :], v.ident[:, :])
                        last.then_inc(S["turned"], 1)
                    for t in range(NT):
                        if t % (NT // 2) == 0:
                            pe.wait_ge(S["hT"], b * 2 + (t // (NT // 2) + 1))
                        last = pe.matmul(v.ps[:, 6, bass.ds(b * (NT * E) + t * E, E)], v.hT2[par][:, t * P:t * P + P],
                                         v.gw[:, :], start=True, stop=True)
                    last.then_inc(S["lg_ps"], 1)
            for b in range(B + 1):
                if b < B:
                    if b == 0:
                        pe.wait_ge(S["ew"], 1)
                    if b >= 2:
                        pe.wait_ge(S["ewT"], b - 1)
                    for t in range(NT):
                        last = pe.transpose(v.ps[0:E, b % 2 * 2 + t // 4, t % 4 * P:t % 4 * P + P],
                                            v.EW[:, b * NT + t, :], v.ident[:, :])
                    last.then_inc(S["ewturned"], 1)
                if b > 0:
                    pe.wait_ge(S["ewT"], b)
                    if b >= 3:
                        pe.wait_ge(S["x3"], b - 2)
                    for t in range(NT):
                        last = pe.matmul(v.ps[:, 4 + (b - 1) % 2 * 2 + t // 4, t % 4 * C:t % 4 * C + C],
                                         v.ewT[(b - 1) % 2][0:E, t, :], v.b2r[:, :], start=True, stop=True)
                    last.then_inc(S["b2_ps"], 1)

        @block.scalar
        def _(act):
            act.sem_inc(S["h3"], 2)
            with act.Fori(0, B) as b:
                for n in range(2):
                    act.wait_ge(S["aturned"], b * 2 + (5 + n))
                    act.activation(v.aT2[:, n * HALF:(n + 1) * HALF], v.ps[:, n, :], ACT.Copy).then_inc(S["aT"], 1)
            act.wait_ge(S["aggr"], B)
            act.activation(v.std_all[:, :], v.mv_all[:, :, 1], ACT.Sqrt, bias=v.eps[:, 0:1]).then_inc(S["root"], 1)
            with act.Fori(0, B // 2) as i:
                for par in range(2):
                    b = i * 2 + par
                    act.wait_ge(S["lg_ps"], b + 1)
                    for n in range(2):
                        act.wait_ge(S["turned"], b * 2 + (5 + n))
                        act.activation(v.hT2[par][:, n * HALF:(n + 1) * HALF], v.ps[:, turned_at[par] + n, :],
                                       ACT.Identity, bias=v.gbcol[:, 3:4], scale=v.gbcol[:, 2:3]).then_inc(S["hT"], 1)
                    act.activation(v.H3T[:, bass.ts(b, T)], bank(turned_at[par]), ACT.Identity,
                                   bias=v.gbcol[:, 3:4], scale=v.gbcol[:, 2:3]).then_inc(S["h3"], 1)
            act.wait_ge(S["delta"], 1)
            act.activation(v.red[:, 4, :], v.red[:, 3, :], ACT.Exp).then_inc(S["ex"], 1)
            for b in range(B):
                act.wait_ge(S["ewturned"], b + 1)
                if b >= 2:
                    act.wait_ge(S["b2_ps"], b - 1)
                act.activation(v.ewT[b % 2][0:E, :, :],
                               v.ps[0:E, b % 2 * 2:b % 2 * 2 + 2, :].rearrange("p a (t c) -> p (a t) c", c=P),
                               ACT.Copy).then_inc(S["ewT"], 1)

        @block.vector
        def _(dve):
            dve.sem_inc(S["x2"], 1)
            dve.sem_inc(S["normed"], 2)
            with dve.Fori(0, B) as b:
                dve.wait_ge(S["y_ps"], b + 1)
                dve.tensor_tensor(v.XX[:, b, :, :], v.XX[:, b, :, :], rowsof(bank(2)), ALU.add).then_inc(S["x2"], 1)
                row_stats(dve, v, S, b, lambda t: v.XX[:, b, t, :], S["x2"], b + 2, b)
            dve.wait_ge(S["root"], 1)
            dve.reciprocal(v.rstd_all[:, :], v.std_all[:, :]).then_inc(S["inv"], 1)
            dve.wait_ge(S["inv"], 1)
            with dve.Fori(0, B // 2) as i:
                for par in range(2):
                    b = i * 2 + par
                    dve.wait_ge(S["turned"], b * 2 + 2)
                    for t in range(NT):
                        last = dve.tensor_scalar(v.Hb2[par][:, t, :], v.XX[:, b, t, :],
                                                 v.mv_all[:, bass.ds(b * NT + t, 1), 0],
                                                 v.rstd_all[:, bass.ds(b * NT + t, 1)],
                                                 ALU.subtract, ALU.mult)
                    last.then_inc(S["normed"], 1)

            links = [0]

            def link(ins):
                links[0] += 1
                ins.then_inc(S["chain"], 1)
                dve.wait_ge(S["chain"], links[0])

            L, hit1, first1, L2, hit2, first2 = (v.GL[:, k, :, :] for k in range(6))
            m1, m2, i1, delta, ex, den, i2 = (v.red[:, k, :] for k in range(7))
            dve.wait_ge(S["lg_ps"], B + 2)
            link(dve.tensor_tensor(L, v.ps[:, 6, 0:ALL * E].rearrange("p (t e) -> p t e", t=ALL),
                                   over(v.gbrow[:, :], ALL), ALU.add))
            link(dve.tensor_reduce(m1, L, AX.X, ALU.max))
            link(dve.tensor_tensor(hit1, L, over(m1, E, 2), ALU.is_equal))
            link(dve.scalar_tensor_tensor(first1, hit1, -float(E), over(v.iota[:, :], ALL), ALU.mult, ALU.add))
            link(dve.tensor_reduce(i1, first1, AX.X, ALU.min))
            link(dve.tensor_tensor(hit1, first1, over(i1, E, 2), ALU.is_equal))
            link(dve.scalar_tensor_tensor(L2, hit1, -3.0e38, L, ALU.mult, ALU.add))
            link(dve.tensor_reduce(m2, L2, AX.X, ALU.max))
            dve.tensor_tensor(delta, m2, m1, ALU.subtract).then_inc(S["delta"], 1)
            link(dve.tensor_tensor(hit2, L2, over(m2, E, 2), ALU.is_equal))
            link(dve.scalar_tensor_tensor(first2, hit2, -float(E), over(v.iota[:, :], ALL), ALU.mult, ALU.add))
            link(dve.tensor_reduce(i2, first2, AX.X, ALU.min))
            link(dve.tensor_tensor(hit2, first2, over(i2, E, 2), ALU.is_equal))
            dve.wait_ge(S["ex"], 1)
            link(dve.tensor_scalar(den, ex, 1.0, None, ALU.add))
            link(dve.reciprocal(m1, den))
            link(dve.tensor_tensor(first2, hit2, over(ex, E, 2), ALU.mult))
            link(dve.tensor_tensor(first1, first2, hit1, ALU.add))
            dve.tensor_tensor(v.EW[:, :, :], first1, over(m1, E, 2), ALU.mult).then_inc(S["ew"], 1)
            for b in range(B):
                dve.wait_ge(S["b2_ps"], b + 1)
                dve.tensor_tensor(v.XX[:, b, :, :], v.XX[:, b, :, :], rowsof(bank(4 + b % 2 * 2)), ALU.add)\
                   .then_inc(S["x3"], 1)


def experts(nc, v, out):
    CT = 4
    CHUNKS = B * NT // CT
    S = {n: v.sem(f"e_{n}") for n in ("hid_full", "relu_done", "out_full", "added", "stats", "mv", "aggr", "root",
                                      "inv", "norm", "fin", "stored")}
    XXt = v.XX[:, :, :, :].rearrange("p b t c -> p (b t) c")
    Xt = v.X[:, :, :, :].rearrange("p b t c -> p (b t) c")
    outt = out.rearrange("b (t p) c -> p (b t) c", p=P)

    with nc.Block() as block:
        @block.tensor
        def _(pe):
            pe.sem_inc(S["out_full"], 1)
            pe.wait_ge(v.experts_loaded, 32)
            with pe.Fori(0, CHUNKS) as c:
                def hidden(e):
                    for f in range(FC):
                        pe.wait_ge(S["relu_done"], c * (E * FC) + (e * FC + f - FC + 1 if e else 0) + 1)
                        pe.matmul(v.ps[:, f, :], v.W1[:, e, f * P:f * P + P], v.H3T[:, bass.ts(c, CT * P)],
                                  start=True, stop=True).then_inc(S["hid_full"], 1)

                hidden(0)
                for e in range(E):
                    if e + 1 < E:
                        hidden(e + 1)
                    pe.wait_ge(S["relu_done"], c * (E * FC) + (e + 1) * FC + 1)
                    pe.wait_ge(S["added"], c * E + max(e - 1, 0) + 1)
                    for t in range(CT):
                        for f in range(FC):
                            last = pe.matmul(v.ps[:, 4 + e % 2, t * C:t * C + C],
                                             v.hid[e % 2 * FC + f][:, t * P:t * P + P], v.W2[:, e, f, :],
                                             start=f == 0, stop=f == FC - 1)
                    last.then_inc(S["out_full"], 1)

        @block.scalar
        def _(act):
            act.sem_inc(S["relu_done"], 1)
            with act.Fori(0, CHUNKS) as c:
                for e in range(E):
                    act.wait_ge(S["out_full"], c * E + max(e - 1, 0) + 1)
                    for f in range(FC):
                        act.wait_ge(S["hid_full"], c * E * FC + (e * FC + f + 1))
                        act.activation(v.hid[e % 2 * FC + f], v.ps[:, f, :], ACT.Relu, bias=v.b1T[:, e, f:f + 1])\
                           .then_inc(S["relu_done"], 1)
            act.wait_ge(S["aggr"], CHUNKS)
            act.activation(v.std_all[:, :], v.mv_all[:, :, 1], ACT.Sqrt, bias=v.eps[:, 0:1]).then_inc(S["root"], 1)

        @block.vector
        def _(dve):
            dve.sem_inc(S["added"], 1)
            with dve.Fori(0, CHUNKS) as c:
                for e in range(E):
                    dve.wait_ge(S["out_full"], c * E + (e + 2))
                    dve.wait_ge(S["added"], c * E + (e + 1))
                    for t in range(CT):
                        x = XXt[:, c * CT + t, :]
                        last = dve.scalar_tensor_tensor(x, v.ps[:, 4 + e % 2, t * C:t * C + C],
                                                        v.EW[:, c * CT + t, e:e + 1], x, ALU.mult, ALU.add)
                    last.then_inc(S["added"], 1)
                settled(dve, v, S["added"], c * E + (E + 1))
                for t in range(CT):
                    last = dve.bn_stats(v.stat[:, t, :], XXt[:, c * CT + t, :])
                last.then_inc(S["stats"], 1)
                settled(dve, v, S["stats"], c + 1)
                for t in range(CT):
                    last = dve.bn_aggr(v.mv_chunk[:, t, :], v.stat[:, t, :])
                last.then_inc(S["mv"], 1)
                dve.wait_ge(S["mv"], c + 1)
                dve.tensor_copy(v.mv_all[:, bass.ts(c, CT), :], v.mv_chunk[:, :, :]).then_inc(S["aggr"], 1)
                settled(dve, v, S["aggr"], c + 1)
            dve.wait_ge(S["root"], 1)
            dve.reciprocal(v.rstd_all[:, :], v.std_all[:, :]).then_inc(S["inv"], 1)
            dve.wait_ge(S["inv"], 1)
            for c in range(CHUNKS):
                for t in range(c * CT, c * CT + CT):
                    last = dve.tensor_scalar(XXt[:, t, :], XXt[:, t, :], v.mv_all[:, t, 0:1], v.rstd_all[:, t:t + 1],
                                             ALU.subtract, ALU.mult)
                last.then_inc(S["norm"], 1)
                dve.wait_ge(S["norm"], c + 1)
                dve.tensor_tensor(XXt[:, c * CT:c * CT + CT, :], XXt[:, c * CT:c * CT + CT, :],
                                  Xt[:, c * CT:c * CT + CT, :], ALU.add).then_inc(S["fin"], 1)

        @block.sync
        def _(sp):
            for c in range(CHUNKS):
                sp.wait_ge(S["fin"], c + 1)
                sp.dma_start(outt[:, c * CT:c * CT + CT, :], XXt[:, c * CT:c * CT + CT, :]).then_inc(S["stored"], 16)
            sp.wait_ge(S["stored"], 16 * CHUNKS)


_INS = ["L0_attn_x", "L0_attn_w_attn", "L0_attn_b_attn", "L0_attn_w_proj", "L0_attn_b_proj", "L0_attn_w_assign",
        "L0_ffn_ln1_g", "L0_ffn_ln1_b", "L0_ffn_w_qkv", "L0_ffn_b_qkv", "L0_ffn_w_o", "L0_ffn_b_o", "L0_ffn_ln2_g",
        "L0_ffn_ln2_b", "L0_ffn_gate_w", "L0_ffn_gate_b", "L0_ffn_W1", "L0_ffn_b1", "L0_ffn_W2", "L0_ffn_b2"]


def constants():
    import numpy as np

    f = np.float32
    div = np.exp(np.arange(0, D, 2, dtype=f) * f(-np.log(10000.0) / D)).astype(f)

    def table(pos):
        ang = np.asarray(pos, f)[:, None] * div
        s = np.stack([np.sin(ang), np.cos(ang)], axis=-1).reshape(len(pos), D).astype(f)
        a = np.stack([s[:, :D // 2], s[:, D // 2:]], axis=-1).reshape(len(pos), D)
        return np.tile(a, (1, H))

    t = np.arange(T)
    p = np.arange(P)
    neg = f(-1e30)
    mask_q = np.zeros((P, NT, P), f)
    mask_k = np.zeros((P, NT, P), f)
    for tile in range(NT):
        for q in range(P):
            s, r = q // 64, q % 64
            k = np.arange(64)
            local = (k // GS == r // GS) & (k <= r)
            group = (tile * P + q) // GS
            clus = k < group * NCPG
            row = np.where(np.concatenate([local, clus]), f(0), neg)
            mask_q[q, tile] = row
            mask_k[:, tile, q] = row if s == 0 else np.concatenate([row[64:], row[:64]])
    return {
        "c_ident": np.eye(P, dtype=f),
        "c_qtab": np.ascontiguousarray(table(np.arange(GS)).T),
        "c_ktab": np.ascontiguousarray(table(t // GS * NCPG + t % GS).T),
        "c_ctab": np.ascontiguousarray(table(np.arange(NCL)).T),
        "c_ind": (np.arange(2 * NCL)[None, :] == (NCL - 8) + p[:, None] // NTPC).astype(f),
        "c_iota": np.tile(np.arange(E, dtype=f), (P, 1)),
        "c_mask_q": mask_q.reshape(P, NT * P),
        "c_mask_k": mask_k.reshape(P, NT * P),
    }


def kernel(**inputs):
    import numpy as np
    import concourse.bacc as bacc
    from concourse.bass_utils import run_bass_kernel_spmd as run

    nc = bacc.Bacc("TRN2", target_bir_lowering=False, num_devices=1)
    arrays = {n: np.ascontiguousarray(inputs[n]) for n in _INS}
    arrays.update(constants())
    A = {n: nc.dram_tensor(f"in_{n}", a.shape, mybir.dt.from_np(a.dtype), kind="ExternalInput").ap()
         for n, a in arrays.items()}
    out = nc.dram_tensor("out_dram", (B, T, C), fp32, kind="ExternalOutput").ap()
    program(nc, A, out)
    r = run(nc, [{f"in_{n}": a for n, a in arrays.items()}], core_ids=[0])
    return r.results[0]["out_dram"]
```

```python
import concourse.bass as bass
from concourse import mybir
from contextlib import ExitStack

P = 128
B, T, C = 4, 1024, 128
H, D = 16, 8
HG, J = 4, 4
UNITS = B * HG
NT = T // P
HALF = T // 2
NCL, GS, NTPC = 64, 32, 16
NCPG = GS // NTPC
E, DFF = 8, 512
FC = DFF // P
TK = T + NCL
PARTS = 3
ROWS = PARTS * PARTS * D
KROWS = ROWS + PARTS
VW = D + 1
ONES = TK // 2
RING = 8
SLOTS = 3
LOOPS = 4
SCALE = float(D) ** -0.5
EPS = 1e-5

fp32 = mybir.dt.float32
bf16 = mybir.dt.bfloat16
ALU = mybir.AluOpType
ACT = mybir.ActivationFunctionType
AX = mybir.AxisListType


def settled(dve, v, sem, value):
    dve.wait_ge(sem, value)
    dve.memset(v.rstd[:, :], 0.0)


class Tally:

    def __init__(self):
        self.n = 0
        self.base = None

    def enter(self, i, per):
        self.base, self.per, self.start = self.n + i * per, per, self.n
        self.n = 0

    def leave(self, trips):
        assert self.n == self.per, (self.n, self.per)
        self.n = self.start + self.per * trips
        self.base = None

    def at(self, k=0):
        return self.n + k if self.base is None else self.base + (self.n + k)

    def index(self):
        return self.n if self.base is None else self.start + self.n

    def up(self, k=1):
        self.n += k


class Buffers:
    pass


def program(nc, A, out):
    ctx = ExitStack()
    v = Buffers()
    with ctx:
        def sb(name, shape, dt=fp32):
            return ctx.enter_context(nc.sbuf_tensor(name, shape, dt))

        def sem(name):
            return ctx.enter_context(nc.semaphore(name))

        def dram(name, shape, dt):
            return nc.dram_tensor(name, shape, dt, kind="Internal").ap()

        v.sem = sem
        v.q_dram = [dram(f"q_parts{s}", [B, H, PARTS * D, T], bf16) for s in (1, 2)]
        v.k_dram = [dram(f"k_parts{s}", [B, H, (2 * PARTS - 1) * D, TK], bf16) for s in (1, 2)]

        v.ps = ctx.enter_context(nc.psum_tensor("ps", [P, 8, 512], fp32))
        v.ident = sb("ident", [P, P])
        v.identb = sb("identb", [P, P], bf16)
        v.X = sb("X", [P, B, NT, C])
        v.XX = sb("XX", [P, B, NT, C])
        v.AO = sb("AO", [P, UNITS, NT, J * D])
        v.VT = sb("VT", [P, UNITS, NT, J * D])
        v.CV = sb("CV", [P, UNITS, J * D])
        v.Vu = [sb(f"Vu{i}", [P, NT, 2, J, VW]) for i in range(SLOTS)]
        v.wqkvT = sb("wqkvT", [P, 3 * C])
        v.wprojT = sb("wprojT", [P, C])
        v.wqkv2 = sb("wqkv2", [P, 3 * C])
        v.wo2 = sb("wo2", [P, C])
        v.W1 = sb("W1", [P, E, DFF])
        v.W2 = sb("W2", [P, E, FC, C])
        v.b1T = sb("b1T", [P, E, FC])
        v.gw = sb("gw", [P, E])
        v.bcol = sb("bcol", [P, 4])
        v.gbcol = sb("gbcol", [P, 4])
        v.brow = sb("brow", [P, 4, C])
        (v.BV1, v.BP1, v.BV2, v.BO2) = range(4)
        v.gbrow = sb("gbrow", [P, E])
        v.iota = sb("iota", [P, E])
        v.qtab = sb("qtab", [P, GS])
        v.ktab = sb("ktab", [P, T])
        v.ctab = sb("ctab", [P, NCL])
        v.ind = sb("ind", [P, 2 * NCL])
        v.mask_q = sb("mask_q", [P, NT, P], bf16)
        v.mask_k = sb("mask_k", [P, NT, P], bf16)
        v.eps = sb("eps", [P, 1])
        v.ones = sb("ones", [PARTS, ONES], bf16)
        v.stat = sb("stat", [P, NT, 6])
        v.mv = sb("mv", [P, NT, 2])
        v.rstd = sb("rstd", [P, NT])
        v.mv_all = sb("mv_all", [P, B * NT, 2])
        v.mv_chunk = sb("mv_chunk", [P, NT // 2, 2])
        v.std_all = sb("std_all", [P, B * NT])
        v.rstd_all = sb("rstd_all", [P, B * NT])
        v.shift_all = sb("shift_all", [P, B * NT])
        v.Mneg = [sb(f"Mneg{h}", [P, J, NT // 2]) for h in range(2)]
        v.Mres = [sb(f"Mres{h}", [P, J, NT // 2]) for h in range(2)]
        v.Mpart = [sb(f"Mpart{h}", [P, 2 * J, PARTS, NT // 2], bf16) for h in range(2)]
        v.MT = [sb(f"MT{h}", [2 * J * PARTS * NT // 2, P], bf16) for h in range(2)]
        v.rden = sb("rden", [P, NT // 2, J])
        v.EW = sb("EW", [P, B * NT, E])
        SCR = 35600
        scr = sb("scr", [P, SCR], bf16)
        place = [0]

        def carve(shape, dt, reset=False):
            if reset:
                place[0] = 0
            n = 1
            for s in shape:
                n *= s
            n *= 2 if dt == fp32 else 1
            part = scr[:, place[0]:place[0] + n]
            place[0] += n
            assert place[0] <= SCR, place
            if dt == fp32:
                part = part.bitcast(fp32)
            if len(shape) == 2:
                part = part.rearrange("p (a b) -> p a b", a=shape[0])
            return part

        v.Qst = [carve([J, T], bf16, reset=i == 0) for i in range(SLOTS)]
        v.Kst = [carve([J, TK], bf16) for _ in range(SLOTS)]
        v.ring = [carve([512], fp32) for _ in range(RING)]
        v.Osb = carve([T], fp32)
        v.Hb = [carve([NT, C], fp32, reset=i == 0) for i in range(2)]
        v.hT = [carve([T], fp32) for _ in range(2)]
        v.QF = carve([T], fp32)
        v.KF = carve([TK], fp32)
        v.QR = carve([T], fp32)
        v.KR = carve([TK], fp32)
        v.Qp = [carve([PARTS, T], bf16) for _ in range(2)]
        v.Kp = [carve([PARTS, TK], bf16) for _ in range(2)]
        shared_at = place[0]
        v.Ab = [carve([NT, C], fp32) for _ in range(2)]
        v.aT = carve([T], fp32)
        place[0] = shared_at
        v.cxT = carve([P], fp32)
        v.wx = carve([NT, C], fp32)
        v.Aw = carve([NT, P], fp32)
        v.wt = carve([B * NT], fp32)
        v.products = v.QR.rearrange("p (t c) -> p t c", t=NT)
        v.sm, v.wT, v.sm2, v.lg = (v.QF[:, a:a + n] for a, n in (
            (0, P), (P, P), (2 * P, 16), (3 * P, B * NT)))
        v.wload = v.Hb[0][:, 0:3, :]
        v.wpload = v.Hb[0][:, 3, :]
        v.b1rows = v.Hb[0][:, 4, :]
        v.H3T = carve([B * T], fp32, reset=True)
        v.GL = carve([6, B * NT * E], fp32).rearrange("p k (t e) -> p k t e", e=E)
        v.red = carve([7, B * NT], fp32)
        v.b2b = carve([E * C], fp32)
        gate_at = place[0]
        v.hT2 = [carve([T], fp32) for _ in range(2)]
        v.aT2 = carve([T], fp32)
        v.Hb2 = [carve([NT, C], fp32) for _ in range(2)]
        v.Ab2 = [carve([NT, C], fp32) for _ in range(2)]
        place[0] = gate_at
        v.hid = [carve([512], fp32) for _ in range(2 * FC)]

        v.b2_dram = A["L0_ffn_b2"].rearrange("e c -> (e c)")
        v.b2_loaded = sem("b2_loaded")
        v.late_loaded = sem("late_loaded")
        v.experts_loaded = sem("experts_loaded")
        v.x_loaded = [sem(f"x_loaded{b}") for b in range(B)]
        v.first = {n: sem(f"x_{n}") for n in ("stats", "mv", "aggr", "root", "inv", "shift", "norm")}
        load_all(nc, A, v)
        project(nc, 1, v)
        attend(nc, 1, v)
        project(nc, 2, v)
        attend(nc, 2, v)
        gate(nc, v)
        experts(nc, v, out)


def load_all(nc, A, v):
    loaded, const_set, turned = v.sem("loaded"), v.sem("const_set"), v.sem("turned")
    def column(vector):
        return vector.rearrange("(p o) -> p o", o=1)

    def row(k, vector):
        return v.brow[:, k, :], vector.partition_broadcast(P)

    jobs = [
        (v.ident[:, :], A["c_ident"]),
        (v.wload, A["L0_attn_w_attn"].rearrange("(a p) c -> p a c", p=P)),
        (v.wpload, A["L0_attn_w_proj"]),
        (v.b1rows[0:E * FC, :], A["L0_ffn_b1"].rearrange("e (f p) -> (e f) p", p=P)),
        (v.AO[:, 0:4, :, :].rearrange("p u t n -> p (u t n)"), A["c_mask_q"]),
        (v.AO[:, 4:8, :, :].rearrange("p u t n -> p (u t n)"), A["c_mask_k"]),
    ]
    jobs += [(v.wx[16 * k:16 * k + 16, :, :],
              A["L0_attn_w_assign"].rearrange("(t k) c -> k t c", k=NCL // NT)[k].partition_broadcast(NTPC))
             for k in range(NCL // NT)]
    jobs += [
        *[(v.bcol[:, k:k + 1], column(A["L0_attn_b_attn"][k * C:(k + 1) * C])) for k in range(2)],
        (v.qtab[:, :], A["c_qtab"]), (v.ktab[:, :], A["c_ktab"]), (v.ctab[:, :], A["c_ctab"]),
        (v.ind[:, :], A["c_ind"]),
        row(v.BV1, A["L0_attn_b_attn"][2 * C:3 * C]),
    ]
    late = [
        *[(v.bcol[:, 2 + k:3 + k], column(A["L0_ffn_b_qkv"][k * C:(k + 1) * C])) for k in range(2)],
        row(v.BP1, A["L0_attn_b_proj"]), row(v.BV2, A["L0_ffn_b_qkv"][2 * C:3 * C]), row(v.BO2, A["L0_ffn_b_o"]),
        *[(v.gbcol[:, k:k + 1], column(A[n]))
          for k, n in enumerate(("L0_ffn_ln1_g", "L0_ffn_ln1_b", "L0_ffn_ln2_g", "L0_ffn_ln2_b"))],
        (v.wqkv2[:, :], A["L0_ffn_w_qkv"]), (v.wo2[:, :], A["L0_ffn_w_o"]),
        (v.gw[:, :], A["L0_ffn_gate_w"]), (v.iota[:, :], A["c_iota"]),
        (v.gbrow[:, :], A["L0_ffn_gate_b"].partition_broadcast(P)),
    ]
    v.late_count = 16 * len(late)
    experts_in = [(v.W1[:, :, :], A["L0_ffn_W1"].rearrange("e p f -> p e f")),
             (v.W2[:, :, :, :].rearrange("p e f c -> p (e f) c"),
              A["L0_ffn_W2"].rearrange("e (f p) c -> p (e f) c", p=P))]

    with nc.Block() as block:
        @block.sync
        def _(sp):
            for b in range(B):
                sp.dma_start(v.X[:, b, :, :], A["L0_attn_x"][b].rearrange("(t p) c -> p t c", p=P))\
                  .then_inc(v.x_loaded[b], 16)
            for dst, src in jobs[0::2]:
                sp.dma_start(dst, src).then_inc(loaded, 16)
            for dst, src in late:
                sp.dma_start(dst, src).then_inc(v.late_loaded, 16)
            for dst, src in experts_in:
                sp.dma_start(dst, src).then_inc(v.experts_loaded, 16)
            sp.wait_ge(loaded, 16 * len(jobs))

        @block.scalar
        def _(act):
            for dst, src in jobs[1::2]:
                act.dma_start(dst, src).then_inc(loaded, 16)
            roots(act, v, v.first, B)
            act.wait_ge(v.first["shift"], 1)
            with act.Fori(0, B) as b:
                apply_norm(act, v, lambda t: v.X[:, b, t, :], lambda t: v.XX[:, b, t, :], b)\
                    .then_inc(v.first["norm"], 1)

        @block.vector
        def _(dve):
            dve.memset(v.eps[:, :], EPS)
            dve.memset(v.ones[:, :], 1.0)
            for b in range(B):
                dve.wait_ge(v.x_loaded[b], 16)
                row_stats(dve, v, v.first, b, lambda t: v.X[:, b, t, :], None, None, b)
            inverses(dve, v, v.first, 1)
            for m in v.Mpart:
                dve.memset(m[:, :, :, :], 0.0)
            dve.wait_ge(loaded, 16 * len(jobs))
            dve.tensor_copy(v.identb[:, :], v.ident[:, :])
            for m, u in ((v.mask_q, 0), (v.mask_k, 4)):
                dve.tensor_copy(m[:, :, :].rearrange("p t n -> p (t n)"),
                                v.AO[:, u:u + 4, :, :].rearrange("p u t n -> p (u t n)"))
            dve.memset(v.ps[:, :, :], 0.0).then_inc(const_set, 1)
            dve.wait_ge(turned, 1)
            dve.tensor_copy(v.wqkvT[:, :], v.ps[:, 0, 0:3 * C])
            dve.tensor_copy(v.b1T[:, :, :].rearrange("p e f -> p (e f)"), v.ps[:, 1, 0:E * FC])
            dve.tensor_copy(v.wprojT[:, :], v.ps[:, 0, 3 * C:4 * C])

        @block.gpsimd
        def _(pool):
            for i in range(SLOTS):
                pool.memset(v.Vu[i][:, :, :, :, :], 1.0)
            pool.memset(v.rden[:, :, :], 1.0).then_inc(const_set, 1)

        @block.tensor
        def _(pe):
            pe.wait_ge(loaded, 16 * len(jobs))
            pe.wait_ge(const_set, 2)
            for a in range(3):
                pe.transpose(v.ps[:, 0, a * C:a * C + C], v.wload[:, a, :], v.ident[:, :])
            pe.transpose(v.ps[:, 1, 0:E * FC], v.b1rows[0:E * FC, :], v.ident[0:E * FC, 0:E * FC])
            pe.transpose(v.ps[:, 0, 3 * C:4 * C], v.wpload, v.ident[:, :]).then_inc(turned, 1)


def row_stats(dve, v, S, b, src, written, value, count):
    if written is not None:
        settled(dve, v, written, value)
    for t in range(NT):
        last = dve.bn_stats(v.stat[:, t, :], src(t))
    last.then_inc(S["stats"], 1)
    settled(dve, v, S["stats"], count + 1)
    for t in range(NT):
        last = dve.bn_aggr(v.mv[:, t, :], v.stat[:, t, :])
    last.then_inc(S["mv"], 1)
    dve.wait_ge(S["mv"], count + 1)
    dve.tensor_copy(v.mv_all[:, bass.ts(b, NT), :], v.mv[:, :, :]).then_inc(S["aggr"], 1)


def over(ap, n, axis=1):
    a = ap.unsqueeze(axis)
    s = list(a.shape)
    s[axis] = n
    return a.broadcast_to(s)


def heads_last(VT, b):
    return VT[:, bass.ts(b, HG), :, :].rearrange("p g t n -> p t g n")


def apply_norm(act, v, src, dst, b):
    for t in range(NT):
        last = act.activation(dst(t), src(t), ACT.Identity, bias=v.shift_all[:, bass.ds(b * NT + t, 1)],
                              scale=v.rstd_all[:, bass.ds(b * NT + t, 1)])
    return last


def roots(act, v, S, rows):
    act.wait_ge(S["aggr"], rows)
    act.activation(v.std_all[:, :], v.mv_all[:, :, 1], ACT.Sqrt, bias=v.eps[:, 0:1]).then_inc(S["root"], 1)


def inverses(dve, v, S, n):
    dve.wait_ge(S["root"], n)
    dve.reciprocal(v.rstd_all[:, :], v.std_all[:, :]).then_inc(S["inv"], 1)
    dve.wait_ge(S["inv"], n)
    dve.scalar_tensor_tensor(v.shift_all[:, :], v.mv_all[:, :, 0], -1.0, v.rstd_all[:, :], ALU.mult, ALU.mult)\
       .then_inc(S["shift"], 1)


def project(nc, stage, v):
    S = {}

    def new(*ns):
        for n in ns:
            S[n] = v.sem(f"p{stage}_{n}")

    new("copied", "turned", "hT", "q_ps", "k_ps", "v_ps", "qf", "kf",
        "vt", "q1", "q2", "k1", "k2", "qr", "kr", "q3", "k3", "stored0", "stored1")
    if stage == 1:
        S.update(v.first)
        new("xw", "lg", "lgT", "softmax", "shifted", "ex", "wT", "wback", "wt", "aw", "cx_ps", "cx", "ck", "kfc", "kc")
    else:
        new("stats", "mv", "aggr", "root", "inv", "shift", "gather", "aturned", "aT", "y_ps", "y", "normed_y",
            "x1", "normed_x")
    stored = [S["stored0"], S["stored1"]]
    w = v.wqkvT if stage == 1 else v.wqkv2
    NK = TK if stage == 1 else T
    ALL = B * NT
    qd, kd = v.q_dram[stage - 1], v.k_dram[stage - 1]
    bank = lambda i, n=2: v.ps[:, i:i + n, :].rearrange("p a n -> p (a n)")
    KF, KR = v.KF[:, 0:T], v.KR[:, 0:T]
    clusters = [p[:, :, T:TK] for p in v.Kp]
    K3 = 2 if stage == 1 else 1
    DMAS = 3 * PARTS - 1

    def pairs(eng, body):
        with eng.Fori(0, B // 2) as i:
            for par in range(2):
                body(i * 2 + par, i, par)

    with nc.Block() as block:
        @block.vector
        def _(dve):
            for n in ("qf", "kf", "qr", "kr", "vt") + (("kfc", "ck", "lg") if stage == 1 else ()):
                dve.sem_inc(S[n], 1)
            if stage == 2:
                dve.sem_inc(S["y"], 1)
            if stage == 1:
                with dve.Fori(0, B) as b:
                    dve.wait_ge(S["norm"], b + 1)
                    dve.wait_ge(S["lg"], b + 1)
                    dve.tensor_tensor(v.products, v.XX[:, b, :, :], v.wx, ALU.mult).then_inc(S["xw"], 1)
                    dve.wait_ge(S["xw"], b + 1)
                    dve.tensor_reduce(v.lg[:, bass.ts(b, NT)], v.products, AX.X, ALU.add).then_inc(S["lg"], 1)
                dve.wait_ge(S["lgT"], 1)
                lgT = v.ps[0:ALL, 6, 0:P].rearrange("p (k s) -> p k s", s=NTPC)
                dve.tensor_reduce(v.sm2[0:ALL, 0:8], lgT, AX.X, ALU.max).then_inc(S["softmax"], 1)
                dve.wait_ge(S["softmax"], 1)
                smv = v.sm[0:ALL, :].rearrange("p (k s) -> p k s", s=NTPC)
                dve.tensor_tensor(smv, lgT, over(v.sm2[0:ALL, 0:8], NTPC, 2), ALU.subtract).then_inc(S["shifted"], 1)
                dve.wait_ge(S["ex"], 1)
                wTv = v.wT[0:ALL, :].rearrange("p (k s) -> p k s", s=NTPC)
                dve.tensor_reduce(v.sm2[0:ALL, 8:16], wTv, AX.X, ALU.add).then_inc(S["softmax"], 1)
                dve.wait_ge(S["softmax"], 2)
                dve.reciprocal(v.sm2[0:ALL, 0:8], v.sm2[0:ALL, 8:16]).then_inc(S["softmax"], 1)
                dve.wait_ge(S["softmax"], 3)
                dve.tensor_tensor(smv, wTv, over(v.sm2[0:ALL, 0:8], NTPC, 2), ALU.mult).then_inc(S["wT"], 1)
                dve.wait_ge(S["wback"], 1)
                dve.tensor_copy(v.wt[:, :], v.ps[:, 6, P:P + ALL]).then_inc(S["wt"], 1)
                dve.wait_ge(S["wt"], 1)
            else:
                with dve.Fori(0, B) as b:
                    dve.wait_ge(S["y_ps"], b + 1)
                    dve.tensor_tensor(v.XX[:, b, :, :], bank(2).rearrange("p (t c) -> p t c", t=NT),
                                      over(v.brow[:, v.BP1, :], NT), ALU.add).then_inc(S["y"], 1)
                    row_stats(dve, v, S, b, lambda t: v.XX[:, b, t, :], S["y"], b + 2, b)
                inverses(dve, v, S, 1)
                with dve.Fori(0, B) as b:
                    row_stats(dve, v, S, b, lambda t: v.X[:, b, t, :], S["x1"], b + 1, b + B)
                inverses(dve, v, S, 2)
                with dve.Fori(0, B) as b:
                    row_stats(dve, v, S, b, lambda t: v.XX[:, b, t, :], S["normed_x"], b + 1, b + 2 * B)
                inverses(dve, v, S, 3)
                dve.wait_ge(S["shift"], 3)

            def own_norm(b, buffer):
                dve.wait_ge(S["turned"], b * 2 + 2)
                for t in range(NT):
                    last = dve.tensor_scalar(v.Hb[buffer][:, t, :], v.XX[:, b, t, :],
                                             v.mv_all[:, bass.ds(b * NT + t, 1), 0],
                                             v.rstd_all[:, bass.ds(b * NT + t, 1)], ALU.subtract, ALU.mult)
                last.then_inc(S["copied"], 1)

            def body(b, i, par):
                if stage == 2 and par == 0:
                    own_norm(b, 0)
                if stage == 1:
                    dve.wait_ge(S["ck"], b + 1)
                    for t in range(NT):
                        at = NCL - 8 - 8 * t
                        last = dve.tensor_scalar(v.Aw[:, t, :].rearrange("p (a c) -> p a c", a=2),
                                                 over(v.ind[:, at:at + NCL], 2), v.wt[:, bass.ds(b * NT + t, 1)], None,
                                                 ALU.mult)
                    last.then_inc(S["aw"], 1)
                dve.wait_ge(S["q_ps"], b + 1)
                dve.wait_ge(S["q1"], b + 1)
                dve.wait_ge(S["qr"], b + 1)
                if stage == 1:
                    dve.scalar_tensor_tensor(v.QF.rearrange("p (g s) -> p g s", s=GS),
                                             bank(6).rearrange("p (g s) -> p g s", s=GS), v.bcol[:, 0:1],
                                             over(v.qtab[:, :], T // GS), ALU.add, ALU.mult).then_inc(S["qf"], 1)
                else:
                    dve.tensor_scalar(v.QF, bank(6), v.bcol[:, 2:3], None, ALU.add).then_inc(S["qf"], 1)
                dve.wait_ge(S["k_ps"], b + 1)
                dve.wait_ge(S["k1"], b + 1)
                dve.wait_ge(S["kr"], b + 1)
                if stage == 1:
                    dve.scalar_tensor_tensor(KF, bank(0), v.bcol[:, 1:2], v.ktab[:, :],
                                             ALU.add, ALU.mult).then_inc(S["kf"], 1)
                else:
                    dve.tensor_scalar(KF, bank(0), v.bcol[:, 3:4], None, ALU.add).then_inc(S["kf"], 1)
                if stage == 2 and par == 0:
                    own_norm(b + 1, 1)
                dve.wait_ge(S["q1"], b + 2)
                dve.wait_ge(S["q3"], b + 1)
                dve.tensor_tensor(v.QR, v.QF, v.Qp[par][:, 0, :], ALU.subtract).then_inc(S["qr"], 1)
                dve.wait_ge(S["k1"], b + 2)
                dve.wait_ge(S["k3"], b * K3 + 1)
                dve.tensor_tensor(KR, KF, v.Kp[par][:, 0, 0:T], ALU.subtract).then_inc(S["kr"], 1)
                if stage == 2:
                    dve.wait_ge(S["v_ps"], b + 1)
                    dve.tensor_tensor(heads_last(v.VT, b), bank(2).rearrange("p (t g n) -> p t g n", t=NT, g=HG),
                                      over(v.brow[:, v.BV2, :].rearrange("p (g n) -> p g n", g=HG), NT),
                                      ALU.add).then_inc(S["vt"], 1)
                    return
                dve.wait_ge(S["cx_ps"], b + 3)
                dve.tensor_copy(v.cxT, v.ps[:, 1, 0:P]).then_inc(S["cx"], 1)
                dve.wait_ge(S["v_ps"], b + 1)
                dve.tensor_tensor(heads_last(v.VT, b), bank(2).rearrange("p (t g n) -> p t g n", t=NT, g=HG),
                                  over(v.brow[:, v.BV1, :].rearrange("p (g n) -> p g n", g=HG), NT),
                                  ALU.add).then_inc(S["vt"], 1)
                dve.wait_ge(S["ck"], b + 2)
                dve.scalar_tensor_tensor(v.KF[:, T:TK], v.ps[:, 0, 0:NCL], v.bcol[:, 1:2], v.ctab[:, :],
                                         ALU.add, ALU.mult).then_inc(S["kc"], 1)
                dve.tensor_tensor(v.CV[:, bass.ts(b, HG), :], v.ps[:, 0, P:2 * P].rearrange("p (g n) -> p g n", g=HG),
                                  v.brow[:, v.BV1, :].rearrange("p (g n) -> p g n", g=HG), ALU.add)\
                   .then_inc(S["kfc"], 1)
                dve.wait_ge(stored[par], i * (16 * DMAS) + 16 * DMAS)
                dve.wait_ge(S["kc"], b * 4 + 1)
                kf, kr, parts = v.KF[:, T:TK], v.KR[:, T:TK], clusters[par]
                dve.tensor_copy(parts[:, 0, :], kf).then_inc(S["kc"], 1)
                dve.wait_ge(S["kc"], b * 4 + 2)
                dve.tensor_tensor(kr, kf, parts[:, 0, :], ALU.subtract).then_inc(S["kc"], 1)
                dve.wait_ge(S["kc"], b * 4 + 3)
                dve.tensor_copy(parts[:, 1, :], kr).then_inc(S["kc"], 1)
                dve.wait_ge(S["kc"], b * 4 + 4)
                dve.tensor_tensor(parts[:, 2, :], kr, parts[:, 1, :], ALU.subtract).then_inc(S["k3"], 1)
            pairs(dve, body)

        @block.scalar
        def _(act):
            for n in ("q1", "k1"):
                act.sem_inc(S[n], 1)
            if stage == 1:
                act.wait_ge(S["shifted"], 1)
                act.activation(v.wT[0:ALL, :], v.sm[0:ALL, :], ACT.Exp).then_inc(S["ex"], 1)
            else:
                with act.Fori(0, B) as b:
                    for n in range(2):
                        act.wait_ge(S["aturned"], b * 2 + (5 + n))
                        act.activation(v.aT[:, n * HALF:(n + 1) * HALF], v.ps[:, n, :], ACT.Copy)\
                            .then_inc(S["aT"], 1)
                roots(act, v, S, B)
                act.wait_ge(S["shift"], 1)
                with act.Fori(0, B) as b:
                    apply_norm(act, v, lambda t: v.XX[:, b, t, :], lambda t: v.XX[:, b, t, :], b)\
                        .then_inc(S["normed_y"], 1)
                roots(act, v, S, 2 * B)
                act.wait_ge(S["shift"], 2)
                with act.Fori(0, B) as b:
                    apply_norm(act, v, lambda t: v.X[:, b, t, :], lambda t: v.XX[:, b, t, :], b)\
                        .then_inc(S["normed_x"], 1)
                roots(act, v, S, 3 * B)

            def body(b, i, par):
                for n in range(2):
                    act.wait_ge(S["turned"], b * 2 + (5 + n))
                    if stage == 1:
                        act.activation(v.hT[par][:, n * HALF:(n + 1) * HALF], v.ps[:, 4 + n, :], ACT.Copy)\
                            .then_inc(S["hT"], 1)
                    else:
                        act.activation(v.hT[par][:, n * HALF:(n + 1) * HALF], v.ps[:, 4 + n, :], ACT.Identity,
                                       bias=v.gbcol[:, 1:2], scale=v.gbcol[:, 0:1]).then_inc(S["hT"], 1)
                act.wait_ge(S["qf"], b + 2)
                act.wait_ge(stored[par], i * (16 * DMAS) + 16 * DMAS)
                act.activation(v.Qp[par][:, 0, :], v.QF, ACT.Copy).then_inc(S["q1"], 1)
                act.wait_ge(S["kf"], b + 2)
                act.activation(v.Kp[par][:, 0, 0:T], KF, ACT.Copy).then_inc(S["k1"], 1)
                act.wait_ge(S["qr"], b + 2)
                act.activation(v.Qp[par][:, 1, :], v.QR, ACT.Copy).then_inc(S["q2"], 1)
                act.wait_ge(S["kr"], b + 2)
                act.activation(v.Kp[par][:, 1, 0:T], KR, ACT.Copy).then_inc(S["k2"], 1)
            pairs(act, body)

        @block.gpsimd
        def _(pool):
            for n in ("q3", "k3"):
                pool.sem_inc(S[n], 1)
            if stage == 2:
                def gather(b, i, par):
                    pool.wait_ge(S["aturned"], b * 2 + 2)
                    for g in range(HG):
                        last = pool.tensor_copy(v.Ab[par][:, :, g * J * D:(g + 1) * J * D], v.AO[:, b * HG + g, :, :])
                    last.then_inc(S["gather"], 1)
                pairs(pool, gather)
                with pool.Fori(0, B) as b:
                    pool.wait_ge(S["normed_y"], b + 1)
                    pool.tensor_tensor(v.X[:, b, :, :], v.X[:, b, :, :], v.XX[:, b, :, :], ALU.add)\
                        .then_inc(S["x1"], 1)

            def body(b, i, par):
                if stage == 1 and par == 0:
                    for k in range(2):
                        pool.wait_ge(S["cx_ps"], b + (k + 1))
                        pool.tensor_copy(v.Hb[k], v.XX[:, b + k, :, :]).then_inc(S["copied"], 1)
                pool.wait_ge(S["q2"], b + 1)
                pool.tensor_tensor(v.Qp[par][:, 2, :], v.QR, v.Qp[par][:, 1, :], ALU.subtract).then_inc(S["q3"], 1)
                pool.wait_ge(S["k2"], b + 1)
                pool.tensor_tensor(v.Kp[par][:, 2, 0:T], KR, v.Kp[par][:, 1, 0:T], ALU.subtract).then_inc(S["k3"], 1)
            pairs(pool, body)

        @block.sync
        def _(sp):
            for s in stored:
                sp.sem_inc(s, 16 * DMAS)

            def body(b, i, par):
                sp.wait_ge(S["q3"], b + 2)
                qrow = qd[b].rearrange("h (a d) n -> a h d n", a=PARTS)
                for a in range(PARTS):
                    sp.dma_start(qrow[a], v.Qp[par][:, a, :]).then_inc(stored[par], 16)
                sp.wait_ge(S["k3"], b * 2 + 3 if stage == 1 else b + 2)
                krow = kd[b].rearrange("h (a d) n -> a h d n", a=2 * PARTS - 1)
                for a in range(2 * PARTS - 1):
                    sp.dma_start(krow[a][:, :, 0:NK], v.Kp[par][:, a % PARTS, 0:NK]).then_inc(stored[par], 16)
            pairs(sp, body)
            if stage == 1:
                sp.wait_ge(v.late_loaded, v.late_count)
            for s in stored:
                sp.wait_ge(s, 16 * DMAS * (B // 2 + 1))

        @block.tensor
        def _(pe):
            pe.sem_inc(S["turned"], 4)
            if stage == 1:
                pe.sem_inc(S["cx_ps"], 2)
            if stage == 2:
                pe.sem_inc(S["aturned"], 4)

                def output(b, i, par):
                    pe.wait_ge(S["gather"], b + 1)
                    for n in range(2):
                        for t in range(n * NT // 2, (n + 1) * NT // 2):
                            last = pe.transpose(v.ps[:, n, t % 4 * C:t % 4 * C + C], v.Ab[par][:, t, :], v.ident[:, :])
                        last.then_inc(S["aturned"], 1)
                    pe.wait_ge(S["y"], b + 1)
                    for n in range(2):
                        pe.wait_ge(S["aT"], b * 2 + (n + 1))
                        for t in range(n * NT // 2, (n + 1) * NT // 2):
                            last = pe.matmul(v.ps[:, 2 + n, t % 4 * C:t % 4 * C + C],
                                             v.aT[:, t * P:t * P + P], v.wprojT[:, :], start=True, stop=True)
                    last.then_inc(S["y_ps"], 1)
                pairs(pe, output)
                pe.wait_ge(S["y"], B + 1)
            else:
                pe.wait_ge(S["lg"], B + 1)
                pe.transpose(v.ps[0:ALL, 6, 0:P], v.lg[:, :], v.ident[:, :]).then_inc(S["lgT"], 1)
                pe.wait_ge(S["wT"], 1)
                pe.transpose(v.ps[:, 6, P:P + ALL], v.sm[0:ALL, :], v.ident[0:ALL, 0:ALL]).then_inc(S["wback"], 1)
                pe.wait_ge(S["wt"], 1)

            def body(b, i, par):
                pe.wait_ge(S["copied"], b + 1)
                for n in range(2):
                    for t in range(n * NT // 2, (n + 1) * NT // 2):
                        last = pe.transpose(v.ps[:, 4 + n, t % 4 * C:t % 4 * C + C], v.Hb[par][:, t, :], v.ident[:, :])
                    last.then_inc(S["turned"], 1)
                pe.wait_ge(S["qf"], b + 1)
                for n in range(2):
                    pe.wait_ge(S["hT"], b * 2 + (n + 1))
                    last = pe.matmul(v.ps[:, 6 + n, :], w[:, 0:C], v.hT[par][:, n * 512:n * 512 + 512],
                                     start=True, stop=True)
                last.then_inc(S["q_ps"], 1)
                pe.wait_ge(S["kf"], b + 1)
                if stage == 1:
                    pe.wait_ge(S["kfc"], b + 1)
                for n in range(2):
                    last = pe.matmul(v.ps[:, n, :], w[:, C:2 * C], v.hT[par][:, n * 512:n * 512 + 512],
                                     start=True, stop=True)
                last.then_inc(S["k_ps"], 1)
                pe.wait_ge(S["vt"], b + 1)
                for t in range(NT):
                    last = pe.matmul(v.ps[:, 2 + t // 4, t % 4 * C:t % 4 * C + C],
                                     v.hT[par][:, t * P:t * P + P], w[:, 2 * C:3 * C], start=True, stop=True)
                last.then_inc(S["v_ps"], 1)
                if stage == 2:
                    return
                pe.wait_ge(S["aw"], b + 1)
                pe.wait_ge(S["kf"], b + 2)
                for t in range(NT):
                    last = pe.matmul(v.ps[:, 1, 0:P], v.Hb[par][:, t, :], v.Aw[:, t, :], start=t == 0, stop=t == NT - 1)
                last.then_inc(S["cx_ps"], 1)
                pe.wait_ge(S["cx"], b + 1)
                pe.matmul(v.ps[:, 0, 0:NCL], w[:, C:2 * C], v.cxT[:, 0:NCL], start=True, stop=True)
                pe.matmul(v.ps[:, 0, P:2 * P], v.cxT, w[:, 2 * C:3 * C], start=True, stop=True).then_inc(S["ck"], 1)
            pairs(pe, body)


def attend(nc, stage, v):
    S = {n: v.sem(f"a{stage}_{n}") for n in (
        "s1_full", "s1_free", "split0", "split1", "split2", "split3", "s2_full", "exp_done", "av_done",
        "o_out", "inv", "vu", "stacked0", "stacked1", "stacked2", "rows0", "rows1", "ones")}
    if stage == 2:
        S["biased"] = v.sem("a2_biased")
    stacked = [S[f"stacked{i}"] for i in range(SLOTS)]
    rows = [S["rows0"], S["rows1"]]
    full = stage == 2
    PIECES = 16 if full else 4
    GROUPS = 8 if full else 4
    STEPS = 4 if full else 1
    NK = T if full else TK
    TH = NT // 2
    qd = v.q_dram[stage - 1].rearrange("b (g j) r n -> (b g) r j n", j=J)
    kd = v.k_dram[stage - 1].rearrange("b (g j) r n -> (b g) r j n", j=J)
    steps_unit = 2 * GROUPS * STEPS
    LOADS = 6

    def uses(first, last):
        out = []
        for h in range(2):
            for k in range(PIECES):
                if not last:
                    out.append(("piece", h, k))
                if h == 0 and k == (1 if full else 0):
                    out.append(("parts", 1, 0))
                if h == (0 if full else 1) and k == (PIECES // 2 + 1 if full else 1) and not first:
                    out += [("outs", 0, 0), ("outs", 1, 0)]
                if h == 1 and k == (1 if full else 0) and not last:
                    out.append(("parts", 0, 1))
        return out

    def schedule(first, last):
        us = uses(first, last)
        n = 2 * GROUPS
        if last:
            return [us[0:1], [], [], us[1:]] + [[] for _ in range(n - 4)]
        return [us[(len(us) * g + n - 1) // n:(len(us) * (g + 1) + n - 1) // n] for g in range(n)]

    def prologue_uses():
        rest = [("piece", 1, k) for k in range(PIECES)]
        return [("piece", 0, k) for k in range(PIECES)] + rest[:2] + [("parts", 0, 0)] + rest[2:]

    def bodies(eng, tallies, per, body):
        body(0, 0, True, False)
        with eng.Fori(0, LOOPS) as i:
            for t, n in zip(tallies, per):
                t.enter(i, n)
            for r in range(SLOTS):
                body(i * SLOTS + (r + 1), (r + 1) % SLOTS, False, False)
        for t in tallies:
            t.leave(LOOPS)
        for u in range(SLOTS * LOOPS + 1, UNITS):
            body(u, u % SLOTS, False, u == UNITS - 1)

    USES = len(uses(False, False))

    def segments(stack, j, r, a, b):
        one = stack[0:r, j, a:a + 64]
        return bass.AP(tensor=one.tensor, offset=one.offset, ap=[list(one.ap[0]), [b - a, 2], [1, 64]])

    with nc.Block() as block:
        @block.sync
        def _(sp):
            def load(u, slot):
                for c in range(PARTS):
                    sp.dma_start(v.Qst[slot][c * 24:c * 24 + 24, :, :], qd[u]).then_inc(stacked[slot], 16)
                    sp.dma_start(v.Kst[slot][c * 24:c * 24 + 24, :, 0:NK],
                                 kd[u][c * D:c * D + 24, :, 0:NK]).then_inc(stacked[slot], 16)

            def shift_rows(slot, h):
                n = PARTS * TH
                for j in range(J):
                    sp.dma_start(v.Qst[slot][ROWS:KROWS, j, h * HALF:(h + 1) * HALF].rearrange("p (t q) -> p t q", t=TH),
                                 v.MT[h][j * n:j * n + n, :]).then_inc(rows[h], 16)

            s1, s2 = Tally(), Tally()

            def follow(us, now, nxt):
                for kind, h, k in us:
                    s1.up()
                    if kind == "parts":
                        sp.wait_ge(S["s1_free"], s1.at())
                        shift_rows(now if h == 1 else nxt, h)

            load(0, 0)
            for k in v.Kst:
                sp.dma_start(k[ROWS:KROWS, :, :].rearrange("p j n -> p (j n)").rearrange("p (a n) -> p a n", n=ONES),
                             over(v.ones[:, :], J * TK // ONES)).then_inc(S["ones"], 16)
            load(1, 1)
            follow(prologue_uses(), None, 0)

            def body(u, slot, first, last):
                if not (isinstance(u, int) and u + 2 >= UNITS):
                    if not first:
                        sp.wait_ge(S["s2_full"], s2.at())
                    load(u + 2, (slot + 2) % SLOTS)
                s2.up(steps_unit)
                follow(uses(first, last), slot, (slot + 1) % SLOTS)
            bodies(sp, [s1, s2], [USES * SLOTS, SLOTS * steps_unit], body)
            sp.wait_ge(rows[0], 16 * J * UNITS)
            sp.wait_ge(rows[1], 16 * J * UNITS)

        @block.gpsimd
        def _(pool):
            if full:
                with pool.Fori(0, B) as b:
                    pool.tensor_tensor(v.XX[:, b, :, :], v.XX[:, b, :, :], over(v.brow[:, v.BO2, :], NT), ALU.add)\
                        .then_inc(S["biased"], 1)
                pool.wait_ge(S["biased"], B)
            av = Tally()

            def body(u, slot, first, last):
                out = v.Vu[slot]
                if not (isinstance(u, int) and u < SLOTS):
                    pool.wait_ge(S["av_done"], av.at(-(SLOTS - 1) * 2 * GROUPS))
                av.up(2 * GROUPS)
                if full:
                    pool.tensor_copy(out[:, :, 0, :, 0:D], v.VT[:, u, :, :].rearrange("p t (j d) -> p t j d", j=J))\
                        .then_inc(S["vu"], 1)
                    return
                for s, lo, cl in ((0, 0, 64), (1, 64, 0)):
                    pool.tensor_copy(out[lo:lo + 64, :, s, :, 0:D],
                                     v.VT[lo:lo + 64, u, :, :].rearrange("p t (j d) -> p t j d", j=J))
                    last_one = pool.tensor_copy(out[cl:cl + 64, :, s, :, 0:D],
                                                over(v.CV[cl:cl + 64, u, :].rearrange("p (j d) -> p j d", j=J), NT))
                last_one.then_inc(S["vu"], 1)
            for u in range(SLOTS):
                body(u, u, u == 0, False)
            with pool.Fori(0, LOOPS) as i:
                av.enter(i, 2 * GROUPS * SLOTS)
                for r in range(SLOTS):
                    body(i * SLOTS + (r + SLOTS), r, False, False)
            av.leave(LOOPS)
            body(UNITS - 1, (UNITS - 1) % SLOTS, False, True)

        @block.vector
        def _(dve):
            s1, spl, inv = Tally(), Tally(), Tally()
            taken = [Tally(), Tally()]
            dve.sem_inc(S["inv"], 1)
            inv.up()

            def use(kind, h, k, u):
                at = s1.index() % 2
                s1.up()
                dve.wait_ge(S["s1_full"], s1.at())
                banks = v.ps[:, 2 * at:2 * at + 2, :].rearrange("p a n -> p (a n)")
                if kind == "piece":
                    if k == 0:
                        if spl.base is not None or spl.n:
                            dve.wait_ge(S["split3"], spl.at())
                    if full:
                        j, t = k % J, k // J
                        ins = dve.tensor_reduce(v.Mneg[h][:, j, t:t + 1], banks, AX.X, ALU.max, negate=True)
                    else:
                        ins = dve.tensor_reduce(v.Mneg[h][:, :, k], banks[:, 0:512].rearrange("p (j n) -> p j n", j=J),
                                                AX.X, ALU.max, negate=True)
                    ins.then_inc(S["s1_free"], 1)
                    if k == PIECES - 1:
                        dve.wait_ge(S["s1_free"], s1.at())
                        m, r, p = v.Mneg[h][:, :, :], v.Mres[h][:, :, :], v.Mpart[h][:, 0:J, :, :]
                        dve.tensor_copy(p[:, :, 0, :], m).then_inc(S["split0"], 1)
                        dve.wait_ge(S["split0"], spl.at(1))
                        dve.tensor_tensor(r, m, p[:, :, 0, :], ALU.subtract).then_inc(S["split1"], 1)
                        dve.wait_ge(S["split1"], spl.at(1))
                        dve.tensor_copy(p[:, :, 1, :], r).then_inc(S["split2"], 1)
                        dve.wait_ge(S["split2"], spl.at(1))
                        dve.tensor_tensor(p[:, :, 2, :], r, p[:, :, 1, :], ALU.subtract).then_inc(S["split3"], 1)
                        spl.up()
                elif kind == "parts":
                    if taken[h].base is not None or taken[h].n:
                        dve.wait_ge(rows[h], taken[h].at())
                    taken[h].up(16 * J)
                    dve.tensor_copy(v.MT[h][:, :], banks[0:2 * J * PARTS * TH, 0:P // 2].bitcast(bf16))\
                       .then_inc(S["s1_free"], 1)
                else:
                    o = banks[:, 0:512].rearrange("p (t j n) -> p t j n", t=TH, j=J)
                    dve.wait_ge(S["s1_free"], s1.at(-1))
                    dve.reciprocal(v.rden[:, :, :], o[:, :, :, D]).then_inc(S["inv"], 1)
                    inv.up()
                    dve.wait_ge(S["inv"], inv.at())
                    dst = v.AO[:, u - 1, h * TH:(h + 1) * TH, :].rearrange("p t (j d) -> p t j d", j=J)
                    dve.tensor_tensor(dst, o[:, :, :, 0:D], over(v.rden[:, :, :], D, 3), ALU.mult)\
                       .then_inc(S["s1_free"], 1)

            for kind, h, k in prologue_uses():
                use(kind, h, k, 0)

            def body(u, slot, first, last):
                for kind, h, k in uses(first, last):
                    use(kind, h, k, u)
            bodies(dve, [s1, spl, inv] + taken,
                   [USES * SLOTS, 2 * SLOTS, 2 * SLOTS, 16 * J * SLOTS, 16 * J * SLOTS], body)
            for h in range(2):
                use("outs", h, 0, UNITS)

        @block.scalar
        def _(act):
            s2, done, outs = Tally(), Tally(), Tally()
            lag = RING // STEPS

            def body(u, slot, first, last):
                for g in range(2 * GROUPS):
                    for s in range(STEPS):
                        n = s2.index()
                        s2.up()
                        act.wait_ge(S["s2_full"], s2.at())
                        if s == 0 and not (first and g < lag):
                            act.wait_ge(S["av_done"], done.at(1 - lag))
                        act.activation(v.ring[n % RING], v.ps[:, 4 + n % 2, :], ACT.Exp, scale=SCALE)\
                           .then_inc(S["exp_done"], 1)
                    done.up()
                    if g == 1 and not first:
                        act.wait_ge(S["av_done"], done.at(-2))
                        act.wait_ge(S["inv"], outs.at(1))
                        act.activation(v.Osb[:, HALF:T], v.ps[:, 7, :], ACT.Copy).then_inc(S["o_out"], 1)
                    if g == GROUPS + 1:
                        act.wait_ge(S["av_done"], done.at(-2))
                        if not first:
                            act.wait_ge(S["inv"], outs.at(2))
                            outs.up(2)
                        act.activation(v.Osb[:, 0:HALF], v.ps[:, 6, :], ACT.Copy).then_inc(S["o_out"], 1)
            bodies(act, [s2, done, outs], [SLOTS * steps_unit, SLOTS * 2 * GROUPS, 2 * SLOTS], body)
            act.wait_ge(S["av_done"], done.at())
            act.wait_ge(S["inv"], outs.at(1))
            act.activation(v.Osb[:, HALF:T], v.ps[:, 7, :], ACT.Copy).then_inc(S["o_out"], 1)

        @block.tensor
        def _(pe):
            s1, s2, spl, outs, rws, vu, oc = (Tally() for _ in range(7))
            stk = [Tally() for _ in range(SLOTS)]

            def use(kind, h, k, slot):
                at = s1.index() % 2
                if s1.base is not None or s1.n >= 2:
                    pe.wait_ge(S["s1_free"], s1.at(-1))
                s1.up()
                banks = v.ps[:, 2 * at:2 * at + 2, :]
                if kind == "piece" and full:
                    j, t = k % J, k // J
                    for n in range(2):
                        last = pe.matmul(banks[:, n, :], v.Qst[slot][0:ROWS, j, h * HALF + t * P:h * HALF + t * P + P],
                                         v.Kst[slot][0:ROWS, j, n * 512:n * 512 + 512], start=True, stop=True)
                elif kind == "piece":
                    t = h * TH + k
                    pe.matmul(banks[:, 0, :], v.identb[:, :], over(v.mask_q[:, t, :], J), start=True, stop=False,
                              skip_group_check=True)
                    for j in range(J):
                        for s in range(2):
                            q0 = t * P + 64 * s
                            last = pe.matmul(banks[64 * s:64 * s + 64, 0, j * P:j * P + P],
                                             v.Qst[slot][0:ROWS, j, q0:q0 + 64],
                                             segments(v.Kst[slot], j, ROWS, q0, T), start=False, stop=True,
                                             skip_group_check=True)
                elif kind == "parts":
                    spl.up()
                    pe.wait_ge(S["split3"], spl.at())
                    last = pe.transpose(banks[0:2 * J * PARTS * TH, 0, 0:P // 2].bitcast(bf16),
                                        v.Mpart[h][:, :, :, :].rearrange("p j a t -> p (j a t)"), v.identb[:, :])
                else:
                    outs.up()
                    pe.wait_ge(S["o_out"], outs.at())
                    for t in range(TH):
                        q0 = h * HALF + t * P
                        last = pe.transpose(banks[:, 0, t * P:t * P + P], v.Osb[:, q0:q0 + P], v.ident[:, :])
                last.then_inc(S["s1_full"], 1)

            def scores(g, s, slot):
                n = s2.index()
                if s2.base is not None or s2.n >= 2:
                    pe.wait_ge(S["exp_done"], s2.at(-1))
                s2.up()
                o = v.ps[:, 4 + n % 2, :]
                if full:
                    h, kt = g // GROUPS, g % GROUPS
                    last = pe.matmul(o, v.Kst[slot][0:KROWS, s, kt * P:kt * P + P],
                                     v.Qst[slot][0:KROWS, s, h * HALF:(h + 1) * HALF], start=True, stop=True)
                else:
                    pe.matmul(o, v.identb[:, :], over(v.mask_k[:, g, :].rearrange("p (s q) -> p s q", s=2), J, 2),
                              start=True, stop=False, skip_group_check=True)
                    for hs in range(2):
                        q0 = g * P + 64 * hs
                        for j in range(J):
                            c = (hs * J + j) * 64
                            for p0, k0 in ((64 * hs, q0), (64 - 64 * hs, T)):
                                last = pe.matmul(o[p0:p0 + 64, c:c + 64], v.Kst[slot][0:KROWS, j, k0:k0 + 64],
                                                 v.Qst[slot][0:KROWS, j, q0:q0 + 64], start=False, stop=True,
                                                 skip_group_check=True)
                last.then_inc(S["s2_full"], 1)

            def times_v(g, slot, n):
                h = g // GROUPS
                pe.wait_ge(S["exp_done"], n)
                if full:
                    kt = g % GROUPS
                    for j in range(J):
                        last = pe.matmul(v.ps[32 * j:32 * j + VW, 6 + h, :], v.Vu[slot][:, kt, 0, j, :],
                                         v.ring[(STEPS * g + j) % RING], start=kt == 0, stop=kt == GROUPS - 1)
                else:
                    for hs in range(2):
                        for j in range(J):
                            c = (hs * J + j) * 64
                            q0 = g % TH * P + 64 * hs
                            last = pe.matmul(v.ps[32 * j:32 * j + VW, 6 + h, q0:q0 + 64], v.Vu[slot][:, g, hs, j, :],
                                             v.ring[g % RING][:, c:c + 64], start=True, stop=True)
                last.then_inc(S["av_done"], 1)

            stk[0].up(16 * LOADS)
            pe.wait_ge(stacked[0], stk[0].at())
            for kind, h, k in prologue_uses():
                use(kind, h, k, 0)
            pe.wait_ge(S["ones"], 16 * SLOTS)

            def body(u, slot, first, last):
                nxt = (slot + 1) % SLOTS
                if not last:
                    stk[nxt].up(16 * LOADS)
                    pe.wait_ge(stacked[nxt], stk[nxt].at())
                sched = schedule(first, last)
                rws.up(16 * J)
                vu.up()
                for g in range(2 * GROUPS):
                    if g % GROUPS == 0:
                        pe.wait_ge(rows[g // GROUPS], rws.at())
                    work = list(sched[g])
                    if not full and work and g % GROUPS == 0:
                        use(*work.pop(0), slot=nxt)
                    for s in range((STEPS + 1) // 2):
                        scores(g, s, slot)
                        if not full and work:
                            use(*work.pop(0), slot=nxt)
                        if full and s == 0 and len(work) > 2:
                            use(*work.pop(0), slot=nxt)
                    if g == 0 and not first:
                        times_v(2 * GROUPS - 1, (slot + 2) % SLOTS, s2.at(-((STEPS + 1) // 2)))
                    if g > 0:
                        if g == 1:
                            pe.wait_ge(S["vu"], vu.at())
                        if (g - 1) % GROUPS == 0 and not first:
                            pe.wait_ge(S["o_out"], oc.at(1 if g == 1 else 2))
                        times_v(g - 1, slot, s2.at(-((STEPS + 1) // 2)))
                    for s in range((STEPS + 1) // 2, STEPS):
                        scores(g, s, slot)
                    while work:
                        use(*work.pop(0), slot=nxt)
                if not first:
                    oc.up(2)
            bodies(pe, [s1, s2, spl, outs, rws, vu, oc] + stk,
                   [USES * SLOTS, SLOTS * steps_unit, 2 * SLOTS, 2 * SLOTS, 16 * J * SLOTS, SLOTS, 2 * SLOTS]
                   + [16 * LOADS] * SLOTS, body)
            times_v(2 * GROUPS - 1, (UNITS - 1) % SLOTS, s2.at())
            for h in range(2):
                use("outs", h, 0, 0)


def gate(nc, v):
    S = {n: v.sem(f"g_{n}") for n in (
        "gather", "aturned", "aT", "y_ps", "x2", "stats", "mv", "aggr", "root", "inv", "normed", "turned", "hT", "h3",
        "lg_ps")}
    bank = lambda i, n=2: v.ps[:, i:i + n, :].rearrange("p a n -> p (a n)")
    rowsof = lambda a: a.rearrange("p (t c) -> p t c", t=NT)
    turned_at = (4, 2)

    with nc.Block() as block:
        @block.gpsimd
        def _(pool):
            with pool.Fori(0, B // 2) as i:
                for par in range(2):
                    b = i * 2 + par
                    pool.wait_ge(S["aturned"], b * 2 + 2)
                    for g in range(HG):
                        last = pool.tensor_copy(v.Ab2[par][:, :, g * J * D:(g + 1) * J * D], v.AO[:, b * HG + g, :, :])
                    last.then_inc(S["gather"], 1)

        @block.tensor
        def _(pe):
            pe.sem_inc(S["aturned"], 4)
            pe.sem_inc(S["turned"], 4)
            pe.sem_inc(S["lg_ps"], 2)
            with pe.Fori(0, B // 2) as i:
                for par in range(2):
                    b = i * 2 + par
                    pe.wait_ge(S["gather"], b + 1)
                    for n in range(2):
                        for t in range(n * NT // 2, (n + 1) * NT // 2):
                            last = pe.transpose(v.ps[:, n, t % 4 * C:t % 4 * C + C], v.Ab2[par][:, t, :], v.ident[:, :])
                        last.then_inc(S["aturned"], 1)
                    pe.wait_ge(S["x2"], b + 1)
                    for n in range(2):
                        pe.wait_ge(S["aT"], b * 2 + (n + 1))
                        for t in range(n * NT // 2, (n + 1) * NT // 2):
                            last = pe.matmul(v.ps[:, 2 + n, t % 4 * C:t % 4 * C + C], v.aT2[:, t * P:t * P + P],
                                             v.wo2[:, :], start=True, stop=True)
                    last.then_inc(S["y_ps"], 1)
            pe.wait_ge(S["x2"], B + 1)
            with pe.Fori(0, B // 2) as i:
                for par in range(2):
                    b = i * 2 + par
                    pe.wait_ge(S["normed"], b + 3)
                    pe.wait_ge(S["h3"], b + 1)
                    for n in range(2):
                        for t in range(n * NT // 2, (n + 1) * NT // 2):
                            last = pe.transpose(v.ps[:, turned_at[par] + n, t % 4 * C:t % 4 * C + C],
                                                v.Hb2[par][:, t, :], v.ident[:, :])
                        last.then_inc(S["turned"], 1)
                    for t in range(NT):
                        if t % (NT // 2) == 0:
                            pe.wait_ge(S["hT"], b * 2 + (t // (NT // 2) + 1))
                        last = pe.matmul(v.ps[:, 6, bass.ds(b * (NT * E) + t * E, E)], v.hT2[par][:, t * P:t * P + P],
                                         v.gw[:, :], start=True, stop=True)
                    last.then_inc(S["lg_ps"], 1)

        @block.scalar
        def _(act):
            act.sem_inc(S["h3"], 2)
            with act.Fori(0, B) as b:
                for n in range(2):
                    act.wait_ge(S["aturned"], b * 2 + (5 + n))
                    act.activation(v.aT2[:, n * HALF:(n + 1) * HALF], v.ps[:, n, :], ACT.Copy).then_inc(S["aT"], 1)
            act.wait_ge(S["aggr"], B)
            act.activation(v.std_all[:, :], v.mv_all[:, :, 1], ACT.Sqrt, bias=v.eps[:, 0:1]).then_inc(S["root"], 1)
            with act.Fori(0, B // 2) as i:
                for par in range(2):
                    b = i * 2 + par
                    act.wait_ge(S["lg_ps"], b + 1)
                    for n in range(2):
                        act.wait_ge(S["turned"], b * 2 + (5 + n))
                        act.activation(v.hT2[par][:, n * HALF:(n + 1) * HALF], v.ps[:, turned_at[par] + n, :],
                                       ACT.Identity, bias=v.gbcol[:, 3:4], scale=v.gbcol[:, 2:3]).then_inc(S["hT"], 1)
                    act.activation(v.H3T[:, bass.ts(b, T)], bank(turned_at[par]), ACT.Identity,
                                   bias=v.gbcol[:, 3:4], scale=v.gbcol[:, 2:3]).then_inc(S["h3"], 1)

        @block.vector
        def _(dve):
            dve.sem_inc(S["x2"], 1)
            dve.sem_inc(S["normed"], 2)
            with dve.Fori(0, B) as b:
                dve.wait_ge(S["y_ps"], b + 1)
                dve.tensor_tensor(v.XX[:, b, :, :], v.XX[:, b, :, :], rowsof(bank(2)), ALU.add).then_inc(S["x2"], 1)
                row_stats(dve, v, S, b, lambda t: v.XX[:, b, t, :], S["x2"], b + 2, b)
            dve.wait_ge(S["root"], 1)
            dve.reciprocal(v.rstd_all[:, :], v.std_all[:, :]).then_inc(S["inv"], 1)
            dve.wait_ge(S["inv"], 1)
            with dve.Fori(0, B // 2) as i:
                for par in range(2):
                    b = i * 2 + par
                    dve.wait_ge(S["turned"], b * 2 + 2)
                    for t in range(NT):
                        last = dve.tensor_scalar(v.Hb2[par][:, t, :], v.XX[:, b, t, :],
                                                 v.mv_all[:, bass.ds(b * NT + t, 1), 0],
                                                 v.rstd_all[:, bass.ds(b * NT + t, 1)],
                                                 ALU.subtract, ALU.mult)
                    last.then_inc(S["normed"], 1)

        @block.sync
        def _(sp):
            sp.dma_start(v.b2b[:, :], v.b2_dram.partition_broadcast(P)).then_inc(v.b2_loaded, 16)


def experts(nc, v, out):
    CT = 4
    CHUNKS = B * NT // CT
    ALL = B * NT
    S = {n: v.sem(f"e_{n}") for n in ("chain", "delta", "ex", "hid_full", "relu_done", "out_full", "added", "stats",
                                      "mv", "aggr", "root", "inv", "norm", "fin", "stored")}
    XXt = v.XX[:, :, :, :].rearrange("p b t c -> p (b t) c")
    Xt = v.X[:, :, :, :].rearrange("p b t c -> p (b t) c")
    outt = out.rearrange("b (t p) c -> p (b t) c", p=P)

    with nc.Block() as block:
        @block.tensor
        def _(pe):
            pe.sem_inc(S["out_full"], 1)
            pe.wait_ge(v.experts_loaded, 32)
            with pe.Fori(0, CHUNKS) as c:
                def hidden(e):
                    for f in range(FC):
                        pe.wait_ge(S["relu_done"], c * (E * FC) + (e * FC + f - FC + 1 if e else 0) + 1)
                        pe.matmul(v.ps[:, f, :], v.W1[:, e, f * P:f * P + P], v.H3T[:, bass.ts(c, CT * P)],
                                  start=True, stop=True).then_inc(S["hid_full"], 1)

                hidden(0)
                for e in range(E):
                    if e + 1 < E:
                        hidden(e + 1)
                    pe.wait_ge(S["relu_done"], c * (E * FC) + (e + 1) * FC + 1)
                    pe.wait_ge(S["added"], c * (2 * E) + (2 * max(e - 1, 0) + 1))
                    for t in range(CT):
                        for f in range(FC):
                            last = pe.matmul(v.ps[:, 4 + e % 2, t * C:t * C + C],
                                             v.hid[e % 2 * FC + f][:, t * P:t * P + P], v.W2[:, e, f, :],
                                             start=f == 0, stop=f == FC - 1)
                    last.then_inc(S["out_full"], 1)

        def last_root(act, a, b, n):
            act.wait_ge(S["aggr"], n)
            act.activation(v.std_all[:, a:b], v.mv_all[:, a:b, 1], ACT.Sqrt, bias=v.eps[:, 0:1]).then_inc(S["root"], 1)

        @block.scalar
        def _(act):
            act.sem_inc(S["relu_done"], 1)
            act.wait_ge(S["delta"], 1)
            act.activation(v.red[:, 4, :], v.red[:, 3, :], ACT.Exp).then_inc(S["ex"], 1)

            def chunk(c, last):
                for e in range(E):
                    act.wait_ge(S["out_full"], c * E + max(e - 1, 0) + 1)
                    for f in range(FC):
                        act.wait_ge(S["hid_full"], c * E * FC + (e * FC + f + 1))
                        act.activation(v.hid[e % 2 * FC + f], v.ps[:, f, :], ACT.Relu, bias=v.b1T[:, e, f:f + 1])\
                           .then_inc(S["relu_done"], 1)
                    if last and e == 1:
                        last_root(act, 0, c * CT, c)
            with act.Fori(0, CHUNKS - 1) as c:
                chunk(c, False)
            chunk(CHUNKS - 1, True)
            last_root(act, (CHUNKS - 1) * CT, CHUNKS * CT, CHUNKS)

        @block.vector
        def _(dve):
            dve.sem_inc(S["added"], 1)
            links = [0]

            def link(ins):
                links[0] += 1
                ins.then_inc(S["chain"], 1)
                dve.wait_ge(S["chain"], links[0])

            L, hit1, first1, L2, hit2, first2 = (v.GL[:, k, :, :] for k in range(6))
            m1, m2, i1, delta, ex, den, i2 = (v.red[:, k, :] for k in range(7))
            link(dve.tensor_tensor(L, v.ps[:, 6, 0:ALL * E].rearrange("p (t e) -> p t e", t=ALL),
                                   over(v.gbrow[:, :], ALL), ALU.add))
            link(dve.tensor_reduce(m1, L, AX.X, ALU.max))
            link(dve.tensor_tensor(hit1, L, over(m1, E, 2), ALU.is_equal))
            link(dve.scalar_tensor_tensor(first1, hit1, -float(E), over(v.iota[:, :], ALL), ALU.mult, ALU.add))
            link(dve.tensor_reduce(i1, first1, AX.X, ALU.min))
            link(dve.tensor_tensor(hit1, first1, over(i1, E, 2), ALU.is_equal))
            link(dve.scalar_tensor_tensor(L2, hit1, -3.0e38, L, ALU.mult, ALU.add))
            link(dve.tensor_reduce(m2, L2, AX.X, ALU.max))
            dve.tensor_tensor(delta, m2, m1, ALU.subtract).then_inc(S["delta"], 1)
            link(dve.tensor_tensor(hit2, L2, over(m2, E, 2), ALU.is_equal))
            link(dve.scalar_tensor_tensor(first2, hit2, -float(E), over(v.iota[:, :], ALL), ALU.mult, ALU.add))
            link(dve.tensor_reduce(i2, first2, AX.X, ALU.min))
            link(dve.tensor_tensor(hit2, first2, over(i2, E, 2), ALU.is_equal))
            dve.wait_ge(S["ex"], 1)
            link(dve.tensor_scalar(den, ex, 1.0, None, ALU.add))
            link(dve.reciprocal(m1, den))
            link(dve.tensor_tensor(first2, hit2, over(ex, E, 2), ALU.mult))
            link(dve.tensor_tensor(first1, first2, hit1, ALU.add))
            link(dve.tensor_tensor(v.EW[:, :, :], first1, over(m1, E, 2), ALU.mult))
            dve.wait_ge(v.b2_loaded, 16)

            def inverse(a, b, n):
                dve.wait_ge(S["root"], n)
                dve.reciprocal(v.rstd_all[:, a:b], v.std_all[:, a:b]).then_inc(S["inv"], 1)
                dve.wait_ge(S["inv"], n)

            def finish(c):
                for t in range(c * CT, c * CT + CT):
                    last = dve.tensor_scalar(XXt[:, t, :], XXt[:, t, :], v.mv_all[:, t, 0:1], v.rstd_all[:, t:t + 1],
                                             ALU.subtract, ALU.mult)
                last.then_inc(S["norm"], 1)
                dve.wait_ge(S["norm"], c + 1)
                dve.tensor_tensor(XXt[:, c * CT:c * CT + CT, :], XXt[:, c * CT:c * CT + CT, :],
                                  Xt[:, c * CT:c * CT + CT, :], ALU.add).then_inc(S["fin"], 1)

            def chunk(c, final):
                for e in range(E):
                    dve.wait_ge(S["added"], c * (2 * E) + (2 * e + 1))
                    for t in range(CT):
                        x = XXt[:, c * CT + t, :]
                        last = dve.scalar_tensor_tensor(x, v.b2b[:, e * C:e * C + C], v.EW[:, c * CT + t, e:e + 1], x,
                                                        ALU.mult, ALU.add)
                    last.then_inc(S["added"], 1)
                    dve.wait_ge(S["out_full"], c * E + (e + 2))
                    dve.wait_ge(S["added"], c * (2 * E) + (2 * e + 2))
                    for t in range(CT):
                        x = XXt[:, c * CT + t, :]
                        last = dve.scalar_tensor_tensor(x, v.ps[:, 4 + e % 2, t * C:t * C + C],
                                                        v.EW[:, c * CT + t, e:e + 1], x, ALU.mult, ALU.add)
                    last.then_inc(S["added"], 1)
                    if final and e == 1:
                        inverse(0, c * CT, 1)
                    if final and e >= 1:
                        finish(e - 1)
                settled(dve, v, S["added"], c * (2 * E) + (2 * E + 1))
                for t in range(CT):
                    last = dve.bn_stats(v.stat[:, t, :], XXt[:, c * CT + t, :])
                last.then_inc(S["stats"], 1)
                settled(dve, v, S["stats"], c + 1)
                for t in range(CT):
                    last = dve.bn_aggr(v.mv_chunk[:, t, :], v.stat[:, t, :])
                last.then_inc(S["mv"], 1)
                dve.wait_ge(S["mv"], c + 1)
                dve.tensor_copy(v.mv_all[:, bass.ts(c, CT), :], v.mv_chunk[:, :, :]).then_inc(S["aggr"], 1)
                settled(dve, v, S["aggr"], c + 1)
            with dve.Fori(0, CHUNKS - 1) as c:
                chunk(c, False)
            chunk(CHUNKS - 1, True)
            inverse((CHUNKS - 1) * CT, CHUNKS * CT, 2)
            finish(CHUNKS - 1)

        @block.sync
        def _(sp):
            for c in range(CHUNKS):
                sp.wait_ge(S["fin"], c + 1)
                sp.dma_start(outt[:, c * CT:c * CT + CT, :], XXt[:, c * CT:c * CT + CT, :]).then_inc(S["stored"], 16)
            sp.wait_ge(S["stored"], 16 * CHUNKS)


_INS = ["L0_attn_x", "L0_attn_w_attn", "L0_attn_b_attn", "L0_attn_w_proj", "L0_attn_b_proj", "L0_attn_w_assign",
        "L0_ffn_ln1_g", "L0_ffn_ln1_b", "L0_ffn_w_qkv", "L0_ffn_b_qkv", "L0_ffn_w_o", "L0_ffn_b_o", "L0_ffn_ln2_g",
        "L0_ffn_ln2_b", "L0_ffn_gate_w", "L0_ffn_gate_b", "L0_ffn_W1", "L0_ffn_b1", "L0_ffn_W2", "L0_ffn_b2"]


def constants():
    import numpy as np

    f = np.float32
    div = np.exp(np.arange(0, D, 2, dtype=f) * f(-np.log(10000.0) / D)).astype(f)

    def table(pos):
        ang = np.asarray(pos, f)[:, None] * div
        s = np.stack([np.sin(ang), np.cos(ang)], axis=-1).reshape(len(pos), D).astype(f)
        a = np.stack([s[:, :D // 2], s[:, D // 2:]], axis=-1).reshape(len(pos), D)
        return np.tile(a, (1, H))

    t = np.arange(T)
    p = np.arange(P)
    neg = f(-1e30)
    mask_q = np.zeros((P, NT, P), f)
    mask_k = np.zeros((P, NT, P), f)
    for tile in range(NT):
        for q in range(P):
            s, r = q // 64, q % 64
            k = np.arange(64)
            local = (k // GS == r // GS) & (k <= r)
            group = (tile * P + q) // GS
            clus = k < group * NCPG
            row = np.where(np.concatenate([local, clus]), f(0), neg)
            mask_q[q, tile] = row
            mask_k[:, tile, q] = row if s == 0 else np.concatenate([row[64:], row[:64]])
    return {
        "c_ident": np.eye(P, dtype=f),
        "c_qtab": np.ascontiguousarray(table(np.arange(GS)).T),
        "c_ktab": np.ascontiguousarray(table(t // GS * NCPG + t % GS).T),
        "c_ctab": np.ascontiguousarray(table(np.arange(NCL)).T),
        "c_ind": (np.arange(2 * NCL)[None, :] == (NCL - 8) + p[:, None] // NTPC).astype(f),
        "c_iota": np.tile(np.arange(E, dtype=f), (P, 1)),
        "c_mask_q": mask_q.reshape(P, NT * P),
        "c_mask_k": mask_k.reshape(P, NT * P),
    }


def kernel(**inputs):
    import numpy as np
    import concourse.bacc as bacc
    from concourse.bass_utils import run_bass_kernel_spmd as run

    nc = bacc.Bacc("TRN2", target_bir_lowering=False, num_devices=1)
    arrays = {n: np.ascontiguousarray(inputs[n]) for n in _INS}
    arrays.update(constants())
    A = {n: nc.dram_tensor(f"in_{n}", a.shape, mybir.dt.from_np(a.dtype), kind="ExternalInput").ap()
         for n, a in arrays.items()}
    out = nc.dram_tensor("out_dram", (B, T, C), fp32, kind="ExternalOutput").ap()
    program(nc, A, out)
    r = run(nc, [{f"in_{n}": a for n, a in arrays.items()}], core_ids=[0])
    return r.results[0]["out_dram"]
```
